# Optimizing a Trainium2 kernel written in Bass

```python
import numpy as np
import jax
import jax.numpy as jnp

def _softmax(x, axis=-1):
    return jax.nn.softmax(x, axis=axis)

def _gelu(x):
    return jax.nn.gelu(x, approximate=True)

def _silu(x):
    return jax.nn.silu(x)

def _sigmoid(x):
    return jax.nn.sigmoid(x)

def _layernorm(x, axis=-1, eps=1e-05):
    m = jnp.mean(x, axis=axis, keepdims=True)
    v = jnp.var(x, axis=axis, keepdims=True)
    return (x - m) / jnp.sqrt(v + eps)

def _scatter_add(tgt, idx, src, axis=0):
    return tgt.at[idx].add(src)

def _segment_sum(src, seg, n):
    return jax.ops.segment_sum(src, seg, n)
kernel_name = 'mk_audio_tower_d2_tok_aud1d768_r4_79a2a0'

def setup_inputs(seed: int=0):
    np.random.seed(seed)
    _w = jnp.asarray

    def _rec_inputs():
        import jax
        import jax.numpy as jnp
        _rk = jax.random.key(seed)
        x = -6.41493e-05 + 1.00002 * jax.random.normal(jax.random.fold_in(_rk, 1), (32, 40000), jnp.float32)
        return x
    x = _rec_inputs()

    def _L0_tok_setup():
        import jax, jax.numpy as jnp
        import numpy as np
        import math
        SR = 4000
        FRAME_LEN = 100
        FRAME_STEP = 160
        N_FILTERS = 40
        N_MFCC = 13
        EMBED = 192
        BATCH = 64
        AUDIO_LEN = 40000
        N_FFT_BINS = FRAME_LEN // 2 + 1

        def _mel_filterbank():
            low_mel = 2595.0 * math.log10(1.0 + 0.0 / 700.0)
            high_mel = 2595.0 * math.log10(1.0 + SR // 2 / 700.0)
            mel_points = np.linspace(low_mel, high_mel, N_FILTERS + 2)
            hz_points = 700.0 * (10.0 ** (mel_points / 2595.0) - 1.0)
            bin_points = np.floor((FRAME_LEN + 1) * hz_points / SR)
            filt = np.zeros((N_FILTERS, N_FFT_BINS), dtype=np.float32)
            for i in range(1, N_FILTERS + 1):
                l, c, r = (bin_points[i - 1], bin_points[i], bin_points[i + 1])
                for j in range(int(l), int(c)):
                    filt[i - 1, j] = (j - l) / (c - l)
                for j in range(int(c), int(r)):
                    filt[i - 1, j] = (r - j) / (r - c)
            return jnp.asarray(filt)

        def _dct_matrix():
            k = np.arange(N_MFCC)[:, None]
            j = np.arange(N_FILTERS)[None, :]
            m = np.cos(np.pi * k * (2 * j + 1) / (2 * N_FILTERS)) * math.sqrt(2.0 / N_FILTERS)
            return jnp.asarray(m.astype(np.float32))
        key = jax.random.key(seed)
        kx, kw = jax.random.split(key)
        x = jax.random.normal(kx, (BATCH, AUDIO_LEN), dtype=jnp.float32)
        bound = 1.0 / math.sqrt(N_MFCC)
        w_proj = jax.random.uniform(kw, (N_MFCC, EMBED), minval=-bound, maxval=bound, dtype=jnp.float32)
        b_proj = jnp.zeros((EMBED,), dtype=jnp.float32)
        return {'x': x, 'mel_filters': _mel_filterbank(), 'dct': _dct_matrix(), 'w_proj': w_proj, 'b_proj': b_proj}
    _L0_tok_all = _L0_tok_setup()
    _L0_tok_in = {k: v for k, v in _L0_tok_all.items() if k in ('mel_filters', 'dct', 'w_proj', 'b_proj')}
    del _L0_tok_all

    def _L0_attn_setup():
        import jax, jax.numpy as jnp
        import numpy as np
        NUM_HEADS = 12
        ACT_BITS = 8
        W_BITS = 8
        EXP_COEF = (0.35815147, 0.96963238, 1.0)
        LN2 = 0.6931471805599453
        N_EXP = 30

        def ste_round(x):
            return x + jax.lax.stop_gradient(jnp.round(x) - x)

        def fq_act(x, bits=ACT_BITS):
            mn = jax.lax.stop_gradient(jnp.min(x))
            mx = jax.lax.stop_gradient(jnp.max(x))
            qmax = 2.0 ** bits - 1.0
            scale = jnp.maximum((mx - mn) / qmax, 1e-08)
            zero = jnp.round(-mn / scale)
            q = jnp.clip(ste_round(x / scale) + zero, 0.0, qmax)
            return ((q - zero) * scale, scale)

        def fq_weight(w, bits=W_BITS):
            amax = jax.lax.stop_gradient(jnp.max(jnp.abs(w), axis=1, keepdims=True))
            qmax = 2.0 ** (bits - 1) - 1.0
            scale = jnp.maximum(amax / qmax, 1e-08)
            q = jnp.clip(ste_round(w / scale), -qmax - 1.0, qmax)
            return q * scale

        def int_softmax(x, scale):
            a, b, c = EXP_COEF
            x_int = ste_round(x / scale)
            x_int = x_int - jnp.max(x_int, axis=-1, keepdims=True)
            x0_int = jnp.floor(-LN2 / scale)
            x_int = jnp.maximum(x_int, N_EXP * x0_int)
            qexp = jnp.floor(x_int / x0_int)
            r = x_int - x0_int * qexp
            b_int = jnp.floor(b / a / scale)
            c_int = jnp.floor(c / a / (scale * scale))
            p_int = r * (r + b_int) + c_int
            e = p_int * jnp.exp2(-qexp) * (a * scale * scale)
            return e / jnp.sum(e, axis=-1, keepdims=True)
        key = jax.random.key(seed)
        ks = jax.random.split(key, 5)
        B, N, C = (64, 197, 192)
        x = jax.random.normal(ks[0], (B, N, C), dtype=jnp.float32)
        w_qkv = jax.random.normal(ks[1], (3 * C, C), dtype=jnp.float32) * 0.02
        b_qkv = jax.random.normal(ks[2], (3 * C,), dtype=jnp.float32) * 0.02
        w_proj = jax.random.normal(ks[3], (C, C), dtype=jnp.float32) * 0.02
        b_proj = jax.random.normal(ks[4], (C,), dtype=jnp.float32) * 0.02
        return {'x': x, 'w_qkv': w_qkv, 'b_qkv': b_qkv, 'w_proj': w_proj, 'b_proj': b_proj}
    _L0_attn_all = _L0_attn_setup()
    _L0_attn_in = {k: v for k, v in _L0_attn_all.items() if k in ('w_qkv', 'b_qkv', 'w_proj', 'b_proj')}
    del _L0_attn_all

    def _L0_ffn_setup():
        import jax, jax.numpy as jnp
        import numpy as np
        DIM = 192
        HEADS = 12
        HIDDEN = 768
        E = 8
        TOPK = 2
        EPS = 1e-05

        def _ln(x, g, b):
            m = x.mean(-1, keepdims=True)
            v = jnp.mean((x - m) ** 2, axis=-1, keepdims=True)
            return (x - m) * jax.lax.rsqrt(v + EPS) * g + b
        key = jax.random.key(seed)
        ks = jax.random.split(key, 10)
        s = 0.02
        return {'x': jax.random.normal(ks[0], (8, 256, DIM), jnp.float32), 'ln1_g': jnp.ones((DIM,), jnp.float32), 'ln1_b': jnp.zeros((DIM,), jnp.float32), 'qkv_w': jax.random.normal(ks[1], (DIM, 3 * DIM), jnp.float32) * s, 'proj_w': jax.random.normal(ks[2], (DIM, DIM), jnp.float32) * s, 'proj_b': jnp.zeros((DIM,), jnp.float32), 'ln2_g': jnp.ones((DIM,), jnp.float32), 'ln2_b': jnp.zeros((DIM,), jnp.float32), 'gate_w': jax.random.normal(ks[3], (DIM, E), jnp.float32) * s, 'gate_b': jnp.zeros((E,), jnp.float32), 'w1': jax.random.normal(ks[4], (E, DIM, HIDDEN), jnp.float32) * s, 'b1': jnp.zeros((E, HIDDEN), jnp.float32), 'w2': jax.random.normal(ks[5], (E, HIDDEN, DIM), jnp.float32) * s, 'b2': jnp.zeros((E, DIM), jnp.float32)}
    _L0_ffn_all = _L0_ffn_setup()
    _L0_ffn_in = {k: v for k, v in _L0_ffn_all.items() if k in ('ln1_g', 'ln1_b', 'qkv_w', 'proj_w', 'proj_b', 'ln2_g', 'ln2_b', 'gate_w', 'gate_b', 'w1', 'b1', 'w2', 'b2')}
    del _L0_ffn_all

    def _L1_attn_setup():
        import jax, jax.numpy as jnp
        import numpy as np
        NH, DK, DV, D = (8, 64, 64, 192)
        DECAY = 0.95
        WRITE_STRENGTH = 0.1
        key = jax.random.key(seed)
        ks = jax.random.split(key, 6)
        s = 0.02
        return {'x': jax.random.normal(ks[0], (4, 1024, D), dtype=jnp.float32), 'w_key': jax.random.normal(ks[1], (NH * DK, D), dtype=jnp.float32) * s, 'w_value': jax.random.normal(ks[2], (NH * DV, D), dtype=jnp.float32) * s, 'w_query': jax.random.normal(ks[3], (NH * DK, D), dtype=jnp.float32) * s, 'w_gate': jax.random.normal(ks[4], (NH, D), dtype=jnp.float32) * s, 'w_out': jax.random.normal(ks[5], (D, NH * DV), dtype=jnp.float32) * s}
    _L1_attn_all = _L1_attn_setup()
    _L1_attn_in = {k: v for k, v in _L1_attn_all.items() if k in ('w_key', 'w_value', 'w_query', 'w_gate', 'w_out')}
    del _L1_attn_all

    def _L1_ffn_setup():
        import jax, jax.numpy as jnp
        import numpy as np
        CAPACITY_FACTOR = 1.25
        key = jax.random.key(seed)
        ks = jax.random.split(key, 5)
        B, S, D, F, E = (8, 512, 192, 768, 8)
        return {'x': jax.random.normal(ks[0], (B, S, D), jnp.float32), 'switch_w': jax.random.normal(ks[1], (D, E), jnp.float32) * 0.02, 'switch_b': jnp.zeros((E,), jnp.float32), 'w1': jax.random.normal(ks[2], (E, D, F), jnp.float32) * 0.02, 'b1': jnp.zeros((E, F), jnp.float32), 'w2': jax.random.normal(ks[3], (E, F, D), jnp.float32) * 0.02, 'b2': jnp.zeros((E, D), jnp.float32)}
    _L1_ffn_all = _L1_ffn_setup()
    _L1_ffn_in = {k: v for k, v in _L1_ffn_all.items() if k in ('switch_w', 'switch_b', 'w1', 'b1', 'w2', 'b2')}
    del _L1_ffn_all
    return {'x': x, 'L0_tok_mel_filters': _L0_tok_in['mel_filters'], 'L0_tok_dct': _L0_tok_in['dct'], 'L0_tok_w_proj': _L0_tok_in['w_proj'], 'L0_tok_b_proj': _L0_tok_in['b_proj'], 'L0_attn_w_qkv': _L0_attn_in['w_qkv'], 'L0_attn_b_qkv': _L0_attn_in['b_qkv'], 'L0_attn_w_proj': _L0_attn_in['w_proj'], 'L0_attn_b_proj': _L0_attn_in['b_proj'], 'L0_ffn_ln1_g': _L0_ffn_in['ln1_g'], 'L0_ffn_ln1_b': _L0_ffn_in['ln1_b'], 'L0_ffn_qkv_w': _L0_ffn_in['qkv_w'], 'L0_ffn_proj_w': _L0_ffn_in['proj_w'], 'L0_ffn_proj_b': _L0_ffn_in['proj_b'], 'L0_ffn_ln2_g': _L0_ffn_in['ln2_g'], 'L0_ffn_ln2_b': _L0_ffn_in['ln2_b'], 'L0_ffn_gate_w': _L0_ffn_in['gate_w'], 'L0_ffn_gate_b': _L0_ffn_in['gate_b'], 'L0_ffn_w1': _L0_ffn_in['w1'], 'L0_ffn_b1': _L0_ffn_in['b1'], 'L0_ffn_w2': _L0_ffn_in['w2'], 'L0_ffn_b2': _L0_ffn_in['b2'], 'L1_attn_w_key': _L1_attn_in['w_key'], 'L1_attn_w_value': _L1_attn_in['w_value'], 'L1_attn_w_query': _L1_attn_in['w_query'], 'L1_attn_w_gate': _L1_attn_in['w_gate'], 'L1_attn_w_out': _L1_attn_in['w_out'], 'L1_ffn_switch_w': _L1_ffn_in['switch_w'], 'L1_ffn_switch_b': _L1_ffn_in['switch_b'], 'L1_ffn_w1': _L1_ffn_in['w1'], 'L1_ffn_b1': _L1_ffn_in['b1'], 'L1_ffn_w2': _L1_ffn_in['w2'], 'L1_ffn_b2': _L1_ffn_in['b2']}

def reference(x, L0_tok_mel_filters, L0_tok_dct, L0_tok_w_proj, L0_tok_b_proj, L0_attn_w_qkv, L0_attn_b_qkv, L0_attn_w_proj, L0_attn_b_proj, L0_ffn_ln1_g, L0_ffn_ln1_b, L0_ffn_qkv_w, L0_ffn_proj_w, L0_ffn_proj_b, L0_ffn_ln2_g, L0_ffn_ln2_b, L0_ffn_gate_w, L0_ffn_gate_b, L0_ffn_w1, L0_ffn_b1, L0_ffn_w2, L0_ffn_b2, L1_attn_w_key, L1_attn_w_value, L1_attn_w_query, L1_attn_w_gate, L1_attn_w_out, L1_ffn_switch_w, L1_ffn_switch_b, L1_ffn_w1, L1_ffn_b1, L1_ffn_w2, L1_ffn_b2):
    import jax
    import jax.numpy as jnp

    def _L0_tok_ref(x, mel_filters, dct, w_proj, b_proj):
        import jax, jax.numpy as jnp
        import numpy as np
        import math
        SR = 4000
        FRAME_LEN = 100
        FRAME_STEP = 160
        N_FILTERS = 40
        N_MFCC = 13
        EMBED = 192
        BATCH = 64
        AUDIO_LEN = 40000
        N_FFT_BINS = FRAME_LEN // 2 + 1

        def _mel_filterbank():
            low_mel = 2595.0 * math.log10(1.0 + 0.0 / 700.0)
            high_mel = 2595.0 * math.log10(1.0 + SR // 2 / 700.0)
            mel_points = np.linspace(low_mel, high_mel, N_FILTERS + 2)
            hz_points = 700.0 * (10.0 ** (mel_points / 2595.0) - 1.0)
            bin_points = np.floor((FRAME_LEN + 1) * hz_points / SR)
            filt = np.zeros((N_FILTERS, N_FFT_BINS), dtype=np.float32)
            for i in range(1, N_FILTERS + 1):
                l, c, r = (bin_points[i - 1], bin_points[i], bin_points[i + 1])
                for j in range(int(l), int(c)):
                    filt[i - 1, j] = (j - l) / (c - l)
                for j in range(int(c), int(r)):
                    filt[i - 1, j] = (r - j) / (r - c)
            return jnp.asarray(filt)

        def _dct_matrix():
            k = np.arange(N_MFCC)[:, None]
            j = np.arange(N_FILTERS)[None, :]
            m = np.cos(np.pi * k * (2 * j + 1) / (2 * N_FILTERS)) * math.sqrt(2.0 / N_FILTERS)
            return jnp.asarray(m.astype(np.float32))
        B, T = x.shape
        n_frames = 1 + (T - FRAME_LEN) // FRAME_STEP
        idx = jnp.arange(n_frames)[:, None] * FRAME_STEP + jnp.arange(FRAME_LEN)[None, :]
        frames = x[:, idx]
        window = 0.54 - 0.46 * jnp.cos(2.0 * jnp.pi * jnp.arange(FRAME_LEN, dtype=jnp.float32) / (FRAME_LEN - 1))
        windowed = frames * window
        fft = jnp.fft.rfft(windowed, axis=-1)
        power = fft.real ** 2 + fft.imag ** 2
        mel_energies = jnp.einsum('bnf,mf->bnm', power, mel_filters)
        log_energies = jnp.log(mel_energies + 1e-06)
        mfcc = jnp.einsum('bnm,km->bnk', log_energies, dct)
        out = mfcc @ w_proj + b_proj
        return out

    def _L0_attn_ref(x, w_qkv, b_qkv, w_proj, b_proj):
        import jax, jax.numpy as jnp
        import numpy as np
        NUM_HEADS = 12
        ACT_BITS = 8
        W_BITS = 8
        EXP_COEF = (0.35815147, 0.96963238, 1.0)
        LN2 = 0.6931471805599453
        N_EXP = 30

        def ste_round(x):
            return x + jax.lax.stop_gradient(jnp.round(x) - x)

        def fq_act(x, bits=ACT_BITS):
            mn = jax.lax.stop_gradient(jnp.min(x))
            mx = jax.lax.stop_gradient(jnp.max(x))
            qmax = 2.0 ** bits - 1.0
            scale = jnp.maximum((mx - mn) / qmax, 1e-08)
            zero = jnp.round(-mn / scale)
            q = jnp.clip(ste_round(x / scale) + zero, 0.0, qmax)
            return ((q - zero) * scale, scale)

        def fq_weight(w, bits=W_BITS):
            amax = jax.lax.stop_gradient(jnp.max(jnp.abs(w), axis=1, keepdims=True))
            qmax = 2.0 ** (bits - 1) - 1.0
            scale = jnp.maximum(amax / qmax, 1e-08)
            q = jnp.clip(ste_round(w / scale), -qmax - 1.0, qmax)
            return q * scale

        def int_softmax(x, scale):
            a, b, c = EXP_COEF
            x_int = ste_round(x / scale)
            x_int = x_int - jnp.max(x_int, axis=-1, keepdims=True)
            x0_int = jnp.floor(-LN2 / scale)
            x_int = jnp.maximum(x_int, N_EXP * x0_int)
            qexp = jnp.floor(x_int / x0_int)
            r = x_int - x0_int * qexp
            b_int = jnp.floor(b / a / scale)
            c_int = jnp.floor(c / a / (scale * scale))
            p_int = r * (r + b_int) + c_int
            e = p_int * jnp.exp2(-qexp) * (a * scale * scale)
            return e / jnp.sum(e, axis=-1, keepdims=True)
        B, N, C = x.shape
        H = NUM_HEADS
        D = C // H
        attn_scale = D ** (-0.5)
        qkv = jnp.einsum('bnc,oc->bno', x, fq_weight(w_qkv)) + b_qkv
        qkv, _ = fq_act(qkv)
        q, _ = fq_act(qkv[:, :, :C])
        k, _ = fq_act(qkv[:, :, C:2 * C])
        v, _ = fq_act(qkv[:, :, 2 * C:])
        q = q.reshape(B, N, H, D).transpose(0, 2, 1, 3)
        k = k.reshape(B, N, H, D).transpose(0, 2, 1, 3)
        v = v.reshape(B, N, H, D).transpose(0, 2, 1, 3)
        attn = jnp.einsum('bhnd,bhmd->bhnm', q, k) * attn_scale
        attn, kv_scale = fq_act(attn)
        attn = int_softmax(attn, kv_scale)
        out = jnp.einsum('bhnm,bhmd->bhnd', attn, v)
        out = out.transpose(0, 2, 1, 3).reshape(B, N, C)
        out, _ = fq_act(out)
        out = jnp.einsum('bnc,oc->bno', out, fq_weight(w_proj)) + b_proj
        out, _ = fq_act(out)
        return out

    def _L0_ffn_ref(x, ln1_g, ln1_b, qkv_w, proj_w, proj_b, ln2_g, ln2_b, gate_w, gate_b, w1, b1, w2, b2):
        import jax, jax.numpy as jnp
        import numpy as np
        DIM = 192
        HEADS = 12
        HIDDEN = 768
        E = 8
        TOPK = 2
        EPS = 1e-05

        def _ln(x, g, b):
            m = x.mean(-1, keepdims=True)
            v = jnp.mean((x - m) ** 2, axis=-1, keepdims=True)
            return (x - m) * jax.lax.rsqrt(v + EPS) * g + b
        B, S, D = x.shape
        hd = D // HEADS
        h = _ln(x, ln1_g, ln1_b)
        qkv = (h @ qkv_w).reshape(B, S, 3, HEADS, hd).transpose(2, 0, 3, 1, 4)
        q, k, v = (qkv[0], qkv[1], qkv[2])
        att = jax.nn.softmax(jnp.einsum('bhqd,bhkd->bhqk', q, k) * hd ** (-0.5), axis=-1)
        o = jnp.einsum('bhqk,bhkd->bhqd', att, v).transpose(0, 2, 1, 3).reshape(B, S, D)
        x = x + o @ proj_w + proj_b
        h2 = _ln(x, ln2_g, ln2_b).reshape(B * S, D)
        logits = h2 @ gate_w + gate_b
        wts, sel = jax.lax.top_k(logits, TOPK)
        wts = jax.nn.softmax(wts.astype(jnp.float32), axis=-1).astype(x.dtype)
        cw = (jax.nn.one_hot(sel, E, dtype=x.dtype) * wts[..., None]).sum(axis=1)
        res = jnp.zeros_like(h2)
        for e in range(E):
            he = jax.nn.gelu(h2 @ w1[e] + b1[e], approximate=False)
            res = res + cw[:, e:e + 1] * (he @ w2[e] + b2[e])
        return x + res.reshape(B, S, D)

    def _L1_attn_ref(x, w_key, w_value, w_query, w_gate, w_out):
        import jax, jax.numpy as jnp
        import numpy as np
        NH, DK, DV, D = (8, 64, 64, 192)
        DECAY = 0.95
        WRITE_STRENGTH = 0.1
        B, S, _ = x.shape
        k = (x @ w_key.T).reshape(B, S, NH, DK)
        v = (x @ w_value.T).reshape(B, S, NH, DV)
        q = (x @ w_query.T).reshape(B, S, NH, DK)
        gate = jax.nn.sigmoid(x @ w_gate.T)
        k0 = k[0]
        v0 = v[0]
        g0 = gate[0]

        def step(fw, inp):
            q_t, k0_t, v0_t, g0_t = inp
            retrieved = jnp.einsum('bhk,hkv->bhv', q_t, fw)
            write = (WRITE_STRENGTH * g0_t)[:, None, None] * (k0_t[:, :, None] * v0_t[:, None, :])
            fw_new = DECAY * fw + jax.lax.stop_gradient(write)
            return (fw_new, retrieved)
        fw0 = jnp.zeros((NH, DK, DV), dtype=x.dtype)
        inputs = (q.transpose(1, 0, 2, 3), k0, v0, g0)
        _, retrieved = jax.lax.scan(step, fw0, inputs)
        retrieved = retrieved.transpose(1, 0, 2, 3).reshape(B, S, NH * DV)
        return x + retrieved @ w_out.T

    def _L1_ffn_ref(x, switch_w, switch_b, w1, b1, w2, b2):
        import jax, jax.numpy as jnp
        import numpy as np
        CAPACITY_FACTOR = 1.25
        B, S, D = x.shape
        E = w1.shape[0]
        xf = x.reshape(-1, D)
        N = xf.shape[0]
        capacity = int(CAPACITY_FACTOR * N / E)
        probs = jax.nn.softmax(xf @ switch_w + switch_b, axis=-1)
        prob_max = jnp.max(probs, axis=-1)
        routes = jnp.argmax(probs, axis=-1)
        sort_idx = jnp.lexsort((-prob_max, routes))
        counts = jnp.bincount(routes, length=E)
        starts = jnp.concatenate([jnp.zeros((1,), counts.dtype), jnp.cumsum(counts)[:-1]])
        rank_sorted = jnp.arange(N) - starts[routes[sort_idx]]
        rank = jnp.zeros((N,), jnp.int32).at[sort_idx].set(rank_sorted.astype(jnp.int32))
        keep = rank < capacity
        dest_e = jnp.where(keep, routes, E)
        dest_c = jnp.where(keep, rank, 0)
        buf = jnp.zeros((E + 1, capacity, D), xf.dtype).at[dest_e, dest_c].set(xf)
        h = jax.nn.gelu(jnp.einsum('ecd,edf->ecf', buf[:E], w1) + b1[:, None, :], approximate=False)
        o = jnp.einsum('ecf,efd->ecd', h, w2) + b2[:, None, :]
        y_exp = o[routes, dest_c]
        y = jnp.where(keep[:, None], y_exp, xf)
        out = y * prob_max[:, None]
        return out.reshape(B, S, D)
    h = _L0_tok_ref(x, L0_tok_mel_filters, L0_tok_dct, L0_tok_w_proj, L0_tok_b_proj)
    h = h + _L0_attn_ref(_layernorm(h, axis=-1), L0_attn_w_qkv, L0_attn_b_qkv, L0_attn_w_proj, L0_attn_b_proj)
    h = h + _L0_ffn_ref(_layernorm(h, axis=-1), L0_ffn_ln1_g, L0_ffn_ln1_b, L0_ffn_qkv_w, L0_ffn_proj_w, L0_ffn_proj_b, L0_ffn_ln2_g, L0_ffn_ln2_b, L0_ffn_gate_w, L0_ffn_gate_b, L0_ffn_w1, L0_ffn_b1, L0_ffn_w2, L0_ffn_b2)
    h = h + _L1_attn_ref(_layernorm(h, axis=-1), L1_attn_w_key, L1_attn_w_value, L1_attn_w_query, L1_attn_w_gate, L1_attn_w_out)
    h = h + _L1_ffn_ref(_layernorm(h, axis=-1), L1_ffn_switch_w, L1_ffn_switch_b, L1_ffn_w1, L1_ffn_b1, L1_ffn_w2, L1_ffn_b2)
    return h

_drawn_inputs = setup_inputs


def setup_inputs(seed=0):
    import zlib

    import numpy as np

    out = dict(_drawn_inputs(seed))
    spreads = {'L0_tok_b_proj': (0.0, 0.321),
     'L0_ffn_ln1_g': (1.0, 0.6),
     'L0_ffn_ln1_b': (0.0, 0.8),
     'L0_ffn_proj_b': (0.0, 0.361),
     'L0_ffn_ln2_g': (1.0, 0.6),
     'L0_ffn_ln2_b': (0.0, 0.8),
     'L0_ffn_gate_b': (0.0, 0.474),
     'L0_ffn_b1': (0.0, 0.8),
     'L0_ffn_b2': (0.0, 0.562),
     'L1_ffn_switch_b': (0.0, 0.8),
     'L1_ffn_b1': (0.0, 0.8),
     'L1_ffn_b2': (0.0, 0.8)}
    factors = {'L0_attn_w_qkv': 3.13,
     'L0_attn_b_qkv': 8.0,
     'L0_attn_w_proj': 3.406,
     'L0_attn_b_proj': 8.0,
     'L0_ffn_qkv_w': 2.728,
     'L0_ffn_proj_w': 3.219,
     'L0_ffn_gate_w': 2.967,
     'L0_ffn_w1': 4.871,
     'L0_ffn_w2': 4.122,
     'L1_attn_w_key': 4.316,
     'L1_attn_w_value': 5.11,
     'L1_attn_w_query': 4.172,
     'L1_attn_w_gate': 8.0,
     'L1_attn_w_out': 5.783,
     'L1_ffn_switch_w': 4.603,
     'L1_ffn_w1': 8.0,
     'L1_ffn_w2': 8.0}
    for name, (base, spread) in spreads.items():
        noise = np.random.default_rng([zlib.crc32(name.encode()), seed]).standard_normal(out[name].shape)
        drawn = base * np.exp(spread * noise) if base else spread * noise
        out[name] = jnp.asarray(drawn.astype(out[name].dtype))
    for name, factor in factors.items():
        out[name] = (out[name] * factor).astype(out[name].dtype)
    return out
```

```python
from contextlib import ExitStack

import numpy as np

import concourse.bass as bass
from concourse import mybir

F32 = mybir.dt.float32
BF16 = mybir.dt.bfloat16
I32 = mybir.dt.int32
I16 = mybir.dt.int16
ALU = mybir.AluOpType
ACT = mybir.ActivationFunctionType
AX = mybir.AxisListType
RMAX = bass.bass_isa.ReduceOp.max

B, AUDIO, HOP, FRAME = 32, 40000, 160, 100
S = 1 + (AUDIO - FRAME) // HOP
TR = S // 2
N = B * S
NT = N // TR
BINS = FRAME // 2 + 1
FILTERS, MFCC = 40, 13
D = 192
DH = D // 2
HEADS, HD = 12, 16
GROUPS = HEADS // 4
HPB = 32
PAIRS = HEADS // 2
QK = 2 * GROUPS * 128
QKV = QK + D
EXPERTS = 8
HIDDEN = 768
HC = HIDDEN // 128
SLOTS = 128
TILES2 = (2 * N + EXPERTS * (SLOTS - 1)) // SLOTS
TILES1 = (N + EXPERTS * (SLOTS - 1)) // SLOTS
FILLS = 12
CAPACITY = int(1.25 * N / EXPERTS)
EPS = 1e-5
MAGIC = 1.5 * 2.0**23
BIG = 3.0e38
BITS = 28
MEM_HEADS, MEM = 8, 512
DECAY = 0.95
COEF_A, COEF_B, COEF_C = 0.35815147, 0.96963238, 1.0
LN2 = 0.6931471805599453
N_EXP = 30


class Ctx:

    def __init__(self, nc, ctx, prefix):
        self.nc, self.ctx, self.prefix = nc, ctx, prefix
        self.sems = []
        ctx.callback(self.clear)

    def clear(self):
        with self.nc.Block() as block:
            @block.sync
            def _(sp):
                for sem in self.sems:
                    sp.sem_clear(sem)

    def sb(self, name, shape, dt=F32):
        return self.ctx.enter_context(self.nc.sbuf_tensor(self.prefix + name, shape, dt))

    def ps(self, name, shape, dt=F32):
        return self.ctx.enter_context(self.nc.psum_tensor(self.prefix + name, shape, dt))

    def sem(self, name):
        self.sems.append(self.ctx.enter_context(self.nc.semaphore(self.prefix + name)))
        return self.sems[-1]


class Chain:

    def __init__(self, eng, sem):
        self.eng, self.sem, self.n, self.base = eng, sem, 0, 0

    def start(self, base):
        self.base, self.n = base, 0

    def of(self, ins):
        self.n += 1
        ins.then_inc(self.sem, 1)
        return ins

    def sync(self):
        self.eng.wait_ge(self.sem, self.base + self.n)

    def link(self, ins):
        self.of(ins)
        self.sync()


class Row:

    def __init__(self, b, u, k, first=False):
        self.b, self.u, self.k, self.first = b, u, k, first


def rows(eng, body):
    with eng.Fori(0, B // 2) as i:
        for u in range(2):
            body(Row(i * 2 + u, u, i))


def rows_skewed(eng, first, step, last):
    first(Row(0, 0, 0))
    with eng.Fori(0, B // 2 - 1) as i:
        step(Row(i * 2 + 1, 1, i), Row(i * 2, 0, i))
        step(Row(i * 2 + 2, 0, i + 1), Row(i * 2 + 1, 1, i))
    end = Row(B - 1, 1, B // 2 - 1)
    step(end, Row(B - 2, 0, B // 2 - 1))
    last(end)


def load_store_rows(sp, load, store):
    load(Row(0, 0, 0, first=True))
    load(Row(1, 1, 0, first=True))
    with sp.Fori(0, B // 2 - 1) as i:
        for u in range(2):
            load(Row(i * 2 + (u + 2), u, i + 1))
            store(Row(i * 2 + u, u, i))
    store(Row(B - 2, 0, B // 2 - 1))
    store(Row(B - 1, 1, B // 2 - 1))


def rows_deep(eng, step, depth, n=B):
    start = depth // 2 * 2

    def at(a):
        return Row(a, a % 2, a // 2) if 0 <= a < n else None

    for a in range(start):
        step(*[at(a - j) for j in range(depth)])
    with eng.Fori(0, (n - start) // 2) as i:
        for u in range(2):
            step(*[Row(i * 2 + (start + u - j), (u - j) % 2, i + (start + u - j) // 2) for j in range(depth)])
    for a in range(n, n + depth - 1):
        step(*[at(a - j) for j in range(depth)])


class NormTiles:

    def __init__(self, c, name=""):
        self.st = c.sb(name + "st", [128, 2, 6])
        self.mv = c.sb(name + "mv", [128, 2, 2])
        self.ve = c.sb(name + "ve", [128, 2])
        self.half = c.sb(name + "half", [128, 2])
        self.rstd = c.sb(name + "rstd", [128, 2])
        self.half_ready = c.sem(name + "half_ready")
        self.ve_ready = c.sem(name + "ve_ready")
        self.passed = c.sem(name + "ln_passed")
        self.rstd_ready = c.sem(name + "rstd_ready")


def inverse_root(nc, pool, ln, n):
    pool.wait_ge(ln.ve_ready, n + 1)
    nc.gpsimd.tensor_tensor(ln.rstd[0:TR, :], ln.ve[0:TR, :], ln.half[0:TR, :], ALU.pow).then_inc(ln.rstd_ready, 1)


def norm_stats(nc, dve, ch, src, ln):
    for t in range(2):
        ch.of(nc.vector.bn_stats(ln.st[0:TR, t, :], src[0:TR, t, :]))
    ch.sync()
    dve.sem_inc(ln.passed, 1)
    for t in range(2):
        ch.of(nc.vector.bn_aggr(ln.mv[0:TR, t, :], ln.st[0:TR, t, :]))
    ch.sync()
    nc.vector.tensor_scalar(ln.ve[0:TR, :], ln.mv[0:TR, :, 1], EPS, None, ALU.add).then_inc(ln.ve_ready, 1)


def norm_apply(nc, dve, src, dst, ln, n):
    dve.wait_ge(ln.rstd_ready, n + 1)
    for t in range(2):
        last = nc.vector.tensor_scalar(dst[0:TR, t, :], src[0:TR, t, :], ln.mv[0:TR, t, 0:1], ln.rstd[0:TR, t:t + 1],
                                       ALU.subtract, ALU.mult)
    return last


PAR = {n: i for i, n in enumerate(
    "inv1 top1 ratio_q ratio_k ratio_v top_q top_k top_v s_q s_k s_v "
    "c_a a_top n_inv n_bias n_step n_least b_half c_rest "
    "o_inv o_top o_scale y_inv y_top y_scale".split())}


def par(keep, name, p=128):
    i = PAR[name]
    return keep["par"][0:p, i:i + 1]


class Scalars:

    def __init__(self, nc, ch, tile, first):
        self.nc, self.ch, self.tile, self.at = nc, ch, tile, first

    def new(self, w=1):
        self.at += w
        assert self.at <= self.tile.shape[1]
        return self.tile[:, self.at - w:self.at]

    def ts(self, x, s1, op0, s2=None, op1=None, out=None):
        out = self.new(x.shape[1]) if out is None else out
        self.ch.link(self.nc.vector.tensor_scalar(out, x, s1, s2, op0, *([op1] if op1 is not None else [])))
        return out

    def tt(self, x, y, op, out=None):
        out = self.new(x.shape[1]) if out is None else out
        self.ch.link(self.nc.vector.tensor_tensor(out, x, y, op))
        return out

    def inverse(self, x, out=None):
        out = self.new(x.shape[1]) if out is None else out
        self.ch.link(self.nc.vector.reciprocal(out, x))
        return out

    def round(self, x):
        return self.ts(x, MAGIC, ALU.add, MAGIC, ALU.subtract)

    def floor(self, x):
        near = self.ts(x, 2.0**23, ALU.add, 2.0**23, ALU.subtract)
        return self.tt(near, self.tt(near, x, ALU.is_gt), ALU.subtract)

    def scale(self, top, minus_least):
        return self.ts(self.tt(top, minus_least, ALU.add), 1.0 / 255.0, ALU.mult, 1e-8, ALU.max)


def quantisers_qkv(nc, dve, ch, tile, extrema):
    s = Scalars(nc, ch, tile, len(PAR))
    col = lambda n: tile[:, PAR[n]:PAR[n] + 1]
    cols = lambda n: tile[:, PAR[n]:PAR[n] + 3]
    top, low = extrema[:, 0:3], extrema[:, 3:6]
    both = [s.tt(s.tt(e[:, 0:1], e[:, 1:2], ALU.max), e[:, 2:3], ALU.max) for e in (top, low)]
    s1 = s.scale(*both)
    inv1 = s.inverse(s1, out=col("inv1"))
    zero1 = s.round(s.tt(both[1], inv1, ALU.mult))
    most1 = s.ts(zero1, -1.0, ALU.mult, 255.0, ALU.add)
    s.ts(most1, MAGIC, ALU.add, out=col("top1"))
    q_top = s.ts(s.round(s.ts(top, inv1, ALU.mult)), most1, ALU.min, s1, ALU.mult)
    q_low = s.ts(s.round(s.ts(low, inv1, ALU.mult)), s1, ALU.mult)
    s2 = s.ts(s.scale(q_top, q_low), 1.0, ALU.mult, out=cols("s_q"))
    inv2 = s.inverse(s2)
    s.ts(inv2, s1, ALU.mult, out=cols("ratio_q"))
    zero2 = s.round(s.tt(q_low, inv2, ALU.mult))
    s.ts(s.ts(zero2, -1.0, ALU.mult, 255.0, ALU.add), MAGIC, ALU.add, out=cols("top_q"))


def quantiser_scores(nc, dve, ch, tile, extrema):
    s = Scalars(nc, ch, tile, len(PAR))
    col = lambda n: tile[:, PAR[n]:PAR[n] + 1]
    unit = s.ts(s.tt(col("s_q"), col("s_k"), ALU.mult), HD**-0.5, ALU.mult)
    top, low = (s.tt(extrema[:, i:i + 1], unit, ALU.mult) for i in range(2))
    inv = s.inverse(s.scale(top, low))
    s.tt(unit, inv, ALU.mult, out=col("c_a"))
    zero = s.round(s.tt(low, inv, ALU.mult))
    s.ts(s.ts(zero, -1.0, ALU.mult, 255.0, ALU.add), MAGIC, ALU.add, out=col("a_top"))
    steps = s.ts(inv, LN2, ALU.mult)
    near = s.ts(steps, 2.0**23, ALU.add, 2.0**23, ALU.subtract)
    up = s.tt(near, s.tt(near, steps, ALU.is_lt), ALU.add)
    n = s.ts(up, 512.0, ALU.min, out=col("n_step"))
    s.ts(n, -float(N_EXP), ALU.mult, out=col("n_least"))
    n_inv = s.inverse(n)
    s.ts(n_inv, -1.0, ALU.mult, out=col("n_inv"))
    s.ts(n_inv, 0.5, ALU.mult, -0.5, ALU.add, out=col("n_bias"))
    b_int = s.floor(s.ts(inv, COEF_B / COEF_A, ALU.mult))
    c_int = s.floor(s.ts(s.tt(inv, inv, ALU.mult), COEF_C / COEF_A, ALU.mult))
    b_half = s.ts(b_int, 0.5, ALU.mult, out=col("b_half"))
    s.tt(c_int, s.tt(b_half, b_half, ALU.mult), ALU.subtract, out=col("c_rest"))


def quantiser_out(nc, dve, ch, tile, extrema, name):
    s = Scalars(nc, ch, tile, len(PAR))
    col = lambda n: tile[:, PAR[n]:PAR[n] + 1]
    scale = s.ts(s.scale(extrema[:, 0:1], extrema[:, 1:2]), 1.0, ALU.mult, out=col(name + "_scale"))
    inv = s.inverse(scale, out=col(name + "_inv"))
    zero = s.round(s.tt(extrema[:, 1:2], inv, ALU.mult))
    s.ts(s.ts(zero, -1.0, ALU.mult, 255.0, ALU.add), MAGIC, ALU.add, out=col(name + "_top"))


def turn_tokens(nc, ps, x, ident):
    for half in range(2):
        for t in range(2):
            last = nc.tensor.transpose(ps[0:DH, half, t * TR:t * TR + TR], x[0:TR, t, half * DH:half * DH + DH], ident)
    return last


def project_tokens(nc, ps, w, xT, width):
    for t in range(2):
        nc.tensor.matmul(ps[0:TR, t, 0:width], xT[0:DH, 0, t * TR:t * TR + TR], w[0:DH, 0, 0:width],
                         start=True, stop=False)
        last = nc.tensor.matmul(ps[0:TR, t, 0:width], xT[:, 1, t * TR:t * TR + TR], w[:, 1, 0:width],
                                start=False, stop=True)
    return last


def project_heads(nc, ps, w, xT, slot, m):
    nc.tensor.matmul(ps[:, slot, 0:S], w[0:DH, 0, m * 128:m * 128 + 128], xT[0:DH, 0, :], start=True, stop=False)
    return nc.tensor.matmul(ps[:, slot, 0:S], w[0:DH + 1, 1, m * 128:m * 128 + 128], xT[:, 1, :], start=False, stop=True)


def project_values(nc, ps, w, xT):
    for t in range(2):
        nc.tensor.matmul(ps[0:TR, t, 0:D], xT[0:DH, 0, t * TR:t * TR + TR], w[0:DH, 0, QK:QKV], start=True, stop=False)
        last = nc.tensor.matmul(ps[0:TR, t, 0:D], xT[:, 1, t * TR:t * TR + TR], w[0:DH + 1, 1, QK:QKV],
                                start=False, stop=True)
    return last


def setup_pass(nc, io, keep):
    with ExitStack() as stack:
        c = Ctx(nc, stack, "setup_")
        amax = c.sb("amax", [128, 2, QKV])
        scale = c.sb("scale", [128, QKV])
        inv = c.sb("inv", [128, QKV])
        q = c.sb("q", [128, 2, QKV])
        wp = c.sb("wp", [128, 2, D])
        loaded = c.sem("loaded")
        cleared = c.sem("cleared")
        reduced = c.sem("reduced")
        steps = c.sem("steps")
        block = stack.enter_context(nc.Block())
        names = ["ident", "padmask", "falling", "tile_start"]
        zeros = c.sb("zeros", [128, TILES2 // FILLS * D])
        tri = c.sb("tri", [128, 128])
        zeroed = c.sem("zeroed")
        filled = c.sem("filled")

        @block.sync
        def _(sp):
            for n in names:
                sp.dma_start(keep[n][:], io[n]).then_inc(loaded, 16)
            sp.dma_start(keep["wqkv"][:], io["wqkv"]).then_inc(loaded, 16)
            sp.dma_start(tri[:], io["tri"]).then_inc(loaded, 16)
            sp.wait_ge(zeroed, 1)
            for n in range(FILLS):
                sp.dma_start(io["slotted"].rearrange("(n p s) d -> n p (s d)", n=FILLS, p=128)[n], zeros[:]).then_inc(filled, 16)
            sp.wait_ge(cleared, 1)
            sp.dma_start(wp[0:DH], io["wproj_q"]).then_inc(loaded, 16)
            sp.wait_ge(filled, 16 * FILLS)

        @block.gpsimd
        def _(pool):
            nc.gpsimd.memset(zeros[:], 0.0).then_inc(zeroed, 1)
            pool.wait_ge(loaded, 16 * (len(names) + 3))
            nc.gpsimd.partition_all_reduce(amax[0:DH].rearrange("p a n -> p (a n)"),
                                           keep["wqkv"][0:DH].rearrange("p a n -> p (a n)"), DH,
                                           bass.bass_isa.ReduceOp.absmax).then_inc(reduced, 1)
            pool.wait_ge(steps, 6)
            nc.gpsimd.partition_all_reduce(amax[:, :, 0:D], wp[:, :, :], 128,
                                           bass.bass_isa.ReduceOp.absmax).then_inc(reduced, 1)

        @block.vector
        def _(dve):
            nc.vector.memset(wp[:], 0.0).then_inc(cleared, 1)
            nc.vector.memset(keep["magic"][:], MAGIC)
            nc.vector.memset(keep["onesb"][:], 1.0)
            ch = Chain(dve, steps)

            def quantise(w, a, sc, iv, qq):
                ch.link(nc.vector.tensor_tensor(sc, a[:, 0, :], a[:, 1, :], ALU.max))
                ch.link(nc.vector.tensor_scalar(sc, sc, 1.0 / 127.0, 1e-8, ALU.mult, ALU.max))
                ch.link(nc.vector.reciprocal(iv, sc))
                for h in range(2):
                    ch.link(nc.vector.tensor_tensor(qq[:, h, :], w[:, h, :], iv, ALU.mult))
                ch.link(nc.vector.tensor_scalar(qq, qq, MAGIC, MAGIC, ALU.add, ALU.subtract))

            dve.wait_ge(reduced, 1)
            quantise(keep["wqkv"][0:DH], amax[0:DH], scale[0:DH, :], inv[0:DH, :], q[0:DH])
            ch.link(nc.vector.tensor_scalar(q[0:DH], q[0:DH], 127.0, -128.0, ALU.min, ALU.max))
            for h in range(2):
                ch.link(nc.vector.tensor_tensor(keep["wqkv"][0:DH, h, :], q[0:DH, h, :], scale[0:DH, :], ALU.mult))
            dve.wait_ge(reduced, 2)
            quantise(wp, amax[:, :, 0:D], keep["wp_scale"][:], inv[:, 0:D], q[:, :, 0:D])
            ch.link(nc.vector.tensor_scalar(keep["wp"][:], q[0:DH, :, 0:D], 127.0, -128.0, ALU.min, ALU.max))
            ch.link(nc.vector.tensor_copy(keep["identb"][:], keep["ident"][:]))
            ch.link(nc.vector.tensor_copy(keep["tri"][:], tri[:]))


def token_pass(nc, io, keep):
    with ExitStack() as stack:
        c = Ctx(nc, stack, "tok_")
        frames = c.sb("frames", [128, 2, 2, FRAME])
        frT = c.sb("frT", [FRAME, S])
        power = c.sb("power", [2 * BINS, S])
        logmel = c.sb("logmel", [FILTERS, S])
        mfcc = c.sb("mfcc", [MFCC + 1, S])
        dft = c.sb("dft", [FRAME, 2 * BINS])
        mel = c.sb("mel", [2 * BINS, FILTERS])
        dct = c.sb("dct", [FILTERS, MFCC])
        wtok = c.sb("wtok", [MFCC + 1, D])
        tiny = c.sb("tiny", [128, 1])
        h1 = c.sb("h1", [128, 2, 2, D])
        ln = NormTiles(c)
        xn = c.sb("xn", [128, 2, D])
        xnT = c.sb("xnT", [DH + 1, 2, 2, S])
        ext = c.sb("ext", [128, 6])
        acc = c.sb("acc", [128, 6])
        extrema = c.sb("extrema", [128, 6])

        ps_fr = c.ps("ps_fr", [128, 2, 256])
        ps_mel = c.ps("ps_mel", [128, 2, 256])
        ps_h = c.ps("ps_h", [128, 2, 256])
        ps_xT = c.ps("ps_xT", [128, 2, 256])
        ps_qk = c.ps("ps_qk", [128, 6, 256])
        ps_v = c.ps("ps_v", [128, 2, 256])

        loaded = c.sem("loaded")
        inited = c.sem("inited")
        frames_in = [c.sem(f"frames_in{u}") for u in range(2)]
        frT_ps = c.sem("frT_ps")
        frT_ready = c.sem("frT_ready")
        dft_ps = c.sem("dft_ps")
        power_ready = c.sem("power_ready")
        mel_ps = c.sem("mel_ps")
        log_ready = c.sem("log_ready")
        mfcc_ps = c.sem("mfcc_ps")
        mfcc_ready = c.sem("mfcc_ready")
        h_ps = c.sem("h_ps")
        passed = c.sem("passed")
        h1_done = c.sem("h1_done")
        h1_stored = [c.sem(f"h1_stored{u}") for u in range(2)]
        xn_ready = c.sem("xn_ready")
        xT_ps = c.sem("xT_ps")
        xnT_ready = c.sem("xnT_ready")
        xnT_stored = [c.sem(f"xnT_stored{u}") for u in range(2)]
        qkv_ps = c.sem("qkv_ps")
        qkv_free = c.sem("qkv_free")
        chain = c.sem("chain")
        pads_out = c.sem("pads_out")
        acc_ready = c.sem("acc_ready")
        all_ready = c.sem("all_ready")
        scalars = c.sem("scalars")
        n_wload = 4

        block = stack.enter_context(nc.Block())

        @block.sync
        def _(sp):
            sp.dma_start(dft[:], io["dft"]).then_inc(loaded, 16)
            sp.dma_start(mel[:], io["mel"]).then_inc(loaded, 16)
            sp.dma_start(dct[:], io["dct"]).then_inc(loaded, 16)
            sp.dma_start(wtok[:], io["wtok"]).then_inc(loaded, 16)

            def load(r):
                b, u = r.b, r.u
                if not r.first:
                    sp.wait_ge(frT_ps, b - 1)
                    sp.sem_inc(passed, 1)
                src = io["x"][b].rearrange("(t p s) -> p t s", t=2, p=TR)[:, :, 0:FRAME]
                sp.dma_start(frames[0:TR, u, :, :], src).then_inc(frames_in[u], 16)

            def store(r):
                b, u = r.b, r.u
                sp.wait_ge(h1_done, b + 2)
                sp.dma_start(io["h1"][b], h1[0:TR, u, :, :]).then_inc(h1_stored[u], 16)
                sp.wait_ge(xnT_ready, b + 1)
                sp.dma_start(io["xnT"][b], xnT[0:DH, u, :, :]).then_inc(xnT_stored[u], 16)

            load_store_rows(sp, load, store)
            for u in range(2):
                sp.wait_ge(h1_stored[u], 16 + 8 * B)
                sp.wait_ge(xnT_stored[u], 16 + 8 * B)

        @block.tensor
        def _(pe):
            pe.wait_ge(loaded, 16 * n_wload)
            pe.wait_ge(inited, 3)

            def front(r):
                b, u = r.b, r.u
                """The steps from frames to h1, each waiting for the one before on ScalarE."""
                def transposes():
                    pe.wait_ge(frames_in[u], r.k * 16 + 16)
                    for t in range(2):
                        last = nc.tensor.transpose(ps_fr[0:FRAME, 0, t * TR:t * TR + TR], frames[0:TR, u, t, :],
                                                   keep["ident"][0:TR, 0:TR])
                    last.then_inc(frT_ps, 1)

                def spectrum():
                    pe.wait_ge(frT_ready, b + 1)
                    nc.tensor.matmul(ps_fr[0:2 * BINS, 1, 0:S], dft[:], frT[:], start=True, stop=True).then_inc(dft_ps, 1)

                def filters():
                    pe.wait_ge(power_ready, b + 1)
                    nc.tensor.matmul(ps_mel[0:FILTERS, 0, 0:S], mel[:], power[:], start=True, stop=True).then_inc(mel_ps, 1)

                def cepstrum():
                    pe.wait_ge(log_ready, b + 1)
                    pe.sem_inc(passed, 1)
                    nc.tensor.matmul(ps_mel[0:MFCC, 1, 0:S], dct[:], logmel[:], start=True, stop=True).then_inc(mfcc_ps, 1)

                def project():
                    pe.wait_ge(mfcc_ready, b + 1)
                    pe.wait_ge(h1_done, b + 1)
                    for t in range(2):
                        last = nc.tensor.matmul(ps_h[0:TR, t, 0:D], mfcc[:, t * TR:t * TR + TR], wtok[:], start=True, stop=True)
                    last.then_inc(h_ps, 1)

                return [transposes, spectrum, filters, cepstrum, project]

            def back(r):
                b, u = r.b, r.u
                """The normed tokens transposed, then q and k by rows of heads, v by tokens."""
                def transposes():
                    pe.wait_ge(xn_ready, b + 1)
                    for half_ in range(2):
                        for t in range(2):
                            last = nc.tensor.transpose(ps_xT[0:DH, half_, t * TR:t * TR + TR],
                                                       xn[0:TR, t, half_ * DH:half_ * DH + DH], keep["ident"][0:TR, 0:TR])
                    last.then_inc(xT_ps, 1)

                def heads(g):
                    def do():
                        if g == 0:
                            pe.wait_ge(xnT_ready, b + 1)
                            pe.wait_ge(qkv_free, b + 1)
                        for m in (2 * g, 2 * g + 1):
                            project_heads(nc, ps_qk, keep["wqkv"], xnT[:, u], m, m)
                    return do

                def values():
                    project_values(nc, ps_v, keep["wqkv"], xnT[:, u]).then_inc(qkv_ps, 1)

                return [transposes, heads(0), heads(1), heads(2), values]

            def mixed(r, before):
                for f, g in zip(back(before), front(r)):
                    f()
                    g()

            rows_skewed(pe, lambda r: [f() for f in front(r)], mixed, lambda r: [f() for f in back(r)])

        @block.scalar
        def _(act):
            for u in range(2):
                act.sem_inc(xnT_stored[u], 16)
            act.wait_ge(inited, 3)

            def front(r):
                b, u = r.b, r.u
                act.wait_ge(frT_ps, b + 1)
                nc.scalar.activation(frT[:], ps_fr[0:FRAME, 0, 0:S], ACT.Copy).then_inc(frT_ready, 1)
                act.wait_ge(dft_ps, b + 1)
                nc.scalar.activation(power[:], ps_fr[0:2 * BINS, 1, 0:S], ACT.Square).then_inc(power_ready, 1)
                act.wait_ge(mel_ps, b + 1)
                nc.scalar.activation(logmel[:], ps_mel[0:FILTERS, 0, 0:S], ACT.Ln, bias=tiny[0:FILTERS, :]).then_inc(log_ready, 1)
                act.wait_ge(mfcc_ps, b + 1)
                nc.scalar.activation(mfcc[0:MFCC, :], ps_mel[0:MFCC, 1, 0:S], ACT.Copy).then_inc(mfcc_ready, 1)

            def back(r):
                b, u = r.b, r.u
                act.wait_ge(xT_ps, b + 1)
                act.wait_ge(xnT_stored[u], r.k * 16 + 16)
                nc.scalar.activation(xnT[0:DH, u, :, :], ps_xT[0:DH, :, 0:S], ACT.Copy).then_inc(xnT_ready, 1)

            def mixed(r, before):
                back(before)
                front(r)

            rows_skewed(act, front, mixed, back)

        @block.gpsimd
        def _(pool):
            nc.gpsimd.memset(ln.half[:], -0.5).then_inc(ln.half_ready, 1)
            nc.gpsimd.memset(mfcc[:], 1.0).then_inc(inited, 1)
            pool.wait_ge(ln.half_ready, 1)

            def body(r):
                b, u = r.b, r.u
                inverse_root(nc, pool, ln, b)

            rows(pool, body)
            pool.wait_ge(acc_ready, 1)
            nc.gpsimd.partition_all_reduce(extrema[:], acc[:], 128, RMAX).then_inc(all_ready, 1)

        @block.vector
        def _(dve):
            ch = Chain(dve, chain)
            for u in range(2):
                dve.sem_inc(h1_stored[u], 16)
            dve.sem_inc(h1_done, 1)
            dve.sem_inc(qkv_free, 1)
            nc.vector.memset(tiny[:], 1e-6).then_inc(inited, 1)
            ch.of(nc.vector.memset(ext[:, 0:3], -BIG))
            ch.of(nc.vector.memset(ext[:, 3:6], BIG))
            ch.of(nc.vector.memset(acc[:, 0:3], -BIG))
            ch.of(nc.vector.memset(acc[:, 3:6], BIG))
            nc.vector.memset(xnT[DH:DH + 1, :, :, :], 1.0).then_inc(inited, 1)
            ch.sync()
            ahead, in_front, in_back = 4, 4, 5

            def front(r):
                b, u = r.b, r.u
                dve.wait_ge(h_ps, b + 1)
                dve.wait_ge(h1_stored[u], r.k * 16 + 16)
                nc.vector.tensor_copy(h1[0:TR, u, :, :], ps_h[0:TR, :, 0:D]).then_inc(h1_done, 1)
                dve.wait_ge(h1_done, b + 2)
                norm_stats(nc, dve, ch, h1[:, u], ln)
                norm_apply(nc, dve, h1[:, u], xn, ln, b).then_inc(xn_ready, 1)

            def back(r):
                b, u = r.b, r.u
                dve.wait_ge(qkv_ps, b + 1)
                for op, at in ((ALU.max, 0), (ALU.min, 3)):
                    ch.of(nc.vector.tensor_reduce(ext[:, at:at + 2], ps_qk[:, :, 0:S].rearrange("p (a g) s -> p a g s", a=2),
                                                  AX.XY, op))
                    last = nc.vector.tensor_reduce(ext[0:TR, at + 2:at + 3], ps_v[0:TR, :, 0:D], AX.XY, op)
                    if op == ALU.max:
                        ch.of(last)
                    else:
                        last.then_inc(qkv_free, 1)
                ch.sync()
                dve.wait_ge(qkv_free, b + 2)
                ch.of(nc.vector.tensor_tensor(acc[:, 0:3], acc[:, 0:3], ext[:, 0:3], ALU.max))
                ch.of(nc.vector.tensor_tensor(acc[:, 3:6], acc[:, 3:6], ext[:, 3:6], ALU.min))
                ch.sync()

            def mixed(r, before):
                ch.start(r.b * (in_front + in_back) + (ahead - in_back))
                back(before)
                front(r)
                assert ch.n == in_front + in_back

            def first(r):
                front(r)
                assert ch.n == ahead + in_front

            def last(r):
                ch.start(ahead + B * in_front + (B - 1) * in_back)
                back(r)

            rows_skewed(dve, first, mixed, last)
            nc.vector.tensor_scalar(acc[:, 0:2], acc[:, 0:2], keep["padmask"][:, 0:1], None, ALU.subtract).then_inc(pads_out, 1)
            nc.vector.tensor_scalar(acc[:, 3:5], acc[:, 3:5], keep["padmask"][:, 0:1], None, ALU.add).then_inc(pads_out, 1)
            dve.wait_ge(pads_out, 2)
            nc.vector.tensor_scalar(acc[:, 3:6], acc[:, 3:6], -1.0, None, ALU.mult).then_inc(acc_ready, 1)
            dve.wait_ge(all_ready, 1)
            quantisers_qkv(nc, dve, Chain(dve, scalars), keep["par"], extrema)


def quantise_pass(nc, io, keep):
    with ExitStack() as stack:
        c = Ctx(nc, stack, "quant_")
        xnT = c.sb("xnT", [DH + 1, 2, 2, S])
        x1 = c.sb("x1", [128, 6, S])
        v1 = c.sb("v1", [128, 2, D])
        i1 = c.sb("i1", [128, 6, S], BF16)
        j1 = c.sb("j1", [128, 2, D], BF16)
        x2 = c.sb("x2", [128, 6, S])
        v2 = c.sb("v2", [128, 2, D])
        qk = c.sb("qk", [128, 2, 6, S], BF16)
        v = c.sb("v", [128, 2, 2, D], BF16)
        row_max = c.sb("row_max", [128, 2, 2 * HEADS])
        least = c.sb("least", [128, PAIRS])
        ext = c.sb("ext", [128, 2])
        acc = c.sb("acc", [128, 2])
        extrema = c.sb("extrema", [128, 2])
        ps_qk = c.ps("ps_qk", [128, 6, 256])
        ps_v = c.ps("ps_v", [128, 2, 256])
        ps_s = c.ps("ps_s", [128, 2, 2, 2, 256])

        passed = c.sem("passed")
        inited = c.sem("inited")
        xnT_in = [c.sem(f"xnT_in{u}") for u in range(2)]
        stored = [c.sem(f"stored{u}") for u in range(2)]
        qkv_ps = c.sem("qkv_ps")
        x1_done = c.sem("x1_done")
        v1_done = c.sem("v1_done")
        i1_ready = c.sem("i1_ready")
        x2_ready = c.sem("x2_ready")
        qk_ready = c.sem("qk_ready")
        v_ready = c.sem("v_ready")
        scores_ps = c.sem("scores_ps")
        pair_done = c.sem("pair_done")
        row_max_ready = c.sem("row_max_ready")
        chain = c.sem("chain")
        acc_ready = c.sem("acc_ready")
        all_ready = c.sem("all_ready")
        scalars = c.sem("scalars")
        block = stack.enter_context(nc.Block())

        @block.sync
        def _(sp):
            def load(r):
                if not r.first:
                    sp.wait_ge(qkv_ps, r.b - 1)
                    sp.sem_inc(passed, 1)
                sp.dma_start(xnT[0:DH, r.u, :, :], io["xnT"][r.b]).then_inc(xnT_in[r.u], 16)

            def store(r):
                sp.wait_ge(qk_ready, r.b + 1)
                sp.dma_start(io["qk"][r.b], qk[:, r.u, :, :]).then_inc(stored[r.u], 16)
                sp.wait_ge(v_ready, r.b + 1)
                sp.dma_start(io["v"][r.b], v[0:TR, r.u, :, :]).then_inc(stored[r.u], 16)
                sp.wait_ge(row_max_ready, r.b + 1)
                sp.dma_start(io["row_max"][r.b], row_max[0:TR, r.u, :]).then_inc(stored[r.u], 16)

            load_store_rows(sp, load, store)
            for u in range(2):
                sp.wait_ge(stored[u], 48 + 24 * B)

        @block.tensor
        def _(pe):
            pe.wait_ge(inited, 1)

            def project(r):
                pe.wait_ge(xnT_in[r.u], r.k * 16 + 16)
                pe.wait_ge(x1_done, r.b + 1)
                for m in range(6):
                    project_heads(nc, ps_qk, keep["wqkv"], xnT[:, r.u], m, m)
                pe.wait_ge(v1_done, r.b + 1)
                project_values(nc, ps_v, keep["wqkv"], xnT[:, r.u]).then_inc(qkv_ps, 1)

            def scores(r, p):
                if p == 0:
                    pe.wait_ge(qk_ready, r.b + 1)
                pe.wait_ge(pair_done, r.b * PAIRS + (p + 1))
                for e in range(2):
                    g, at = (2 * p + e) // 4, HPB * ((2 * p + e) % 4)
                    for t in range(2):
                        last = nc.tensor.matmul(ps_s[0:TR, p % 2, e, t, 0:S], qk[at:at + HPB, r.u, g, t * TR:t * TR + TR],
                                                qk[at:at + HPB, r.u, GROUPS + g, :], start=True, stop=True)
                last.then_inc(scores_ps, 1)

            def step(r, before):
                scores(before, 0)
                scores(before, 1)
                project(r)
                for p in range(2, PAIRS):
                    scores(before, p)

            rows_skewed(pe, project, step, lambda r: [scores(r, p) for p in range(PAIRS)])

        @block.scalar
        def _(act):
            act.sem_inc(x1_done, 1)
            act.sem_inc(v1_done, 1)
            act.sem_inc(pair_done, 2)
            for u in range(2):
                act.sem_inc(stored[u], 48)

            def body(r):
                magic, inv1 = keep["magic"], par(keep, "inv1")
                act.wait_ge(qkv_ps, r.b + 1)
                nc.scalar.activation(x1[:], ps_qk[:, :, 0:S], ACT.Identity, scale=inv1, bias=magic[:]).then_inc(x1_done, 1)
                nc.scalar.activation(v1[0:TR], ps_v[0:TR, :, 0:D], ACT.Identity, scale=par(keep, "inv1", TR),
                                     bias=magic[0:TR, :]).then_inc(v1_done, 1)
                act.wait_ge(i1_ready, r.b + 1)
                nc.scalar.activation(x2[:, 0:3, :], i1[:, 0:3, :], ACT.Identity, scale=par(keep, "ratio_q"), bias=magic[:])
                nc.scalar.activation(x2[:, 3:6, :], i1[:, 3:6, :], ACT.Identity, scale=par(keep, "ratio_k"), bias=magic[:])
                nc.scalar.activation(v2[0:TR], j1[0:TR], ACT.Identity, scale=par(keep, "ratio_v", TR),
                                     bias=magic[0:TR, :]).then_inc(x2_ready, 1)

            rows(act, body)

        @block.gpsimd
        def _(pool):
            nc.gpsimd.memset(xnT[DH:DH + 1, :, :, :], 1.0).then_inc(inited, 1)
            pool.wait_ge(acc_ready, 1)
            nc.gpsimd.partition_all_reduce(extrema[:], acc[:], 128, RMAX).then_inc(all_ready, 1)

        @block.vector
        def _(dve):
            ch = Chain(dve, chain)
            ch.of(nc.vector.memset(acc[:, 0:1], -BIG))
            ch.of(nc.vector.memset(acc[:, 1:2], BIG))
            ch.sync()

            def first_quantiser(r):
                dve.wait_ge(x1_done, r.b + 2)
                nc.vector.tensor_scalar(i1[:], x1[:], par(keep, "top1"), MAGIC, ALU.min, ALU.subtract)
                dve.wait_ge(v1_done, r.b + 2)
                nc.vector.tensor_scalar(j1[0:TR], v1[0:TR], par(keep, "top1", TR), MAGIC, ALU.min, ALU.subtract)\
                    .then_inc(i1_ready, 1)

            def second_quantiser(r):
                dve.wait_ge(x2_ready, r.b + 1)
                dve.wait_ge(stored[r.u], r.k * 48 + 48)
                nc.vector.tensor_scalar(qk[:, r.u, 0:3, :], x2[:, 0:3, :], par(keep, "top_q"), MAGIC, ALU.min, ALU.subtract)
                nc.vector.tensor_scalar(qk[:, r.u, 3:6, :], x2[:, 3:6, :], par(keep, "top_k"), MAGIC, ALU.min, ALU.subtract)\
                    .then_inc(qk_ready, 1)
                nc.vector.tensor_scalar(v[0:TR, r.u], v2[0:TR], par(keep, "top_v", TR), MAGIC, ALU.min, ALU.subtract)\
                    .then_inc(v_ready, 1)

            def pair(r, p):
                dve.wait_ge(scores_ps, r.b * PAIRS + (p + 1))
                s_ = ps_s[0:TR, p % 2, :, :, 0:S]
                ch.of(nc.vector.tensor_reduce(row_max[0:TR, r.u, 4 * p:4 * p + 4], s_, AX.X, ALU.max))
                nc.vector.tensor_reduce(least[0:TR, p:p + 1], s_, AX.XYZ, ALU.min).then_inc(pair_done, 1)

            def row_end(r):
                ch.sync()
                dve.wait_ge(pair_done, r.b * PAIRS + (PAIRS + 2))
                nc.vector.tensor_reduce(ext[0:TR, 0:1], row_max[0:TR, r.u, :], AX.X, ALU.max).then_inc(row_max_ready, 1)
                ch.of(nc.vector.tensor_reduce(ext[0:TR, 1:2], least[0:TR, :], AX.X, ALU.min))
                ch.sync()
                dve.wait_ge(row_max_ready, r.b + 1)
                ch.of(nc.vector.tensor_tensor(acc[0:TR, 0:1], acc[0:TR, 0:1], ext[0:TR, 0:1], ALU.max))
                ch.of(nc.vector.tensor_tensor(acc[0:TR, 1:2], acc[0:TR, 1:2], ext[0:TR, 1:2], ALU.min))
                ch.sync()

            ahead, per_row = 2, PAIRS + 3

            def first(r):
                first_quantiser(r)
                second_quantiser(r)

            def step(r, before):
                ch.start(before.b * per_row + ahead)
                pair(before, 0)
                pair(before, 1)
                first_quantiser(r)
                pair(before, 2)
                second_quantiser(r)
                for p in range(3, PAIRS):
                    pair(before, p)
                row_end(before)
                assert ch.n == per_row

            def last(r):
                ch.start(r.b * per_row + ahead)
                for p in range(PAIRS):
                    pair(r, p)
                row_end(r)

            rows_skewed(dve, first, step, last)
            nc.vector.tensor_scalar(acc[:, 1:2], acc[:, 1:2], -1.0, None, ALU.mult).then_inc(acc_ready, 1)
            dve.wait_ge(all_ready, 1)
            quantiser_scores(nc, dve, Chain(dve, scalars), keep["par"], extrema)


def lagged(r, before, p, lag):
    if p >= lag:
        return r, p - lag
    return (before, PAIRS + p - lag) if before is not None else None


def integer_softmax_pass(nc, io, keep):
    with ExitStack() as stack:
        c = Ctx(nc, stack, "isoft_")
        unit = [128, 2, 2, 2, S]
        qk = c.sb("qk", [128, 2, 6, S], BF16)
        v = c.sb("v", [128, 2, 2, D], BF16)
        vf = c.sb("vf", [128, 2, 2, HEADS, HD + 1])
        maxima = c.sb("maxima", [128, B, 2 * HEADS])
        rounded = c.sb("rounded", [128, B, 2 * HEADS])
        steps = c.sb("steps", [128, B, 2 * HEADS], BF16)
        mcol = c.sb("mcol", [128, 2, 2 * HEADS], BF16)
        t = c.sb("t", unit)
        d0 = c.sb("d0", unit, BF16)
        d = c.sb("d", unit, BF16)
        kf = c.sb("kf", unit)
        k = c.sb("k", unit)
        kn = c.sb("kn", unit, BF16)
        rem = c.sb("rem", unit, BF16)
        sq = c.sb("sq", unit)
        pw = c.sb("pw", unit, I32)
        e_ = c.sb("e", unit)
        inv_sum = c.sb("inv_sum", [128, 2, HEADS])
        o = c.sb("o", [128, 2, 2, D])
        ext = c.sb("ext", [128, 2])
        acc = c.sb("acc", [128, 2])
        extrema = c.sb("extrema", [128, 2])
        ps_s = c.ps("ps_s", [128, 2, 2, 2, 256])
        ps_m = c.ps("ps_m", [128, 2, 2, 256])
        ps_o = c.ps("ps_o", [128, 2, 512])

        def low(x):
            return x.bitcast(I16).rearrange("p e t (s h) -> p e t s h", h=2)[:, :, :, :, 0]

        rows_in = [c.sem(f"rows_in{u}") for u in range(2)]
        maxima_in = c.sem("maxima_in")
        rounded_ready = c.sem("rounded_ready")
        steps_ready = c.sem("steps_ready")
        ones_ready = c.sem("ones_ready")
        v_ready = c.sem("v_ready")
        mcol_ready = c.sem("mcol_ready")
        passed = c.sem("passed")
        pv_done = c.sem("pv_done")
        scores_ps = c.sem("scores_ps")
        t_ready = c.sem("t_ready")
        d0_done = c.sem("d0_done")
        d_ready = c.sem("d_ready")
        kf_ready = c.sem("kf_ready")
        k_ready = c.sem("k_ready")
        kn_ready = c.sem("kn_ready")
        rem_ready = c.sem("rem_ready")
        sq_ready = c.sem("sq_ready")
        pw_ready = c.sem("pw_ready")
        e_done = c.sem("e_done")
        unit_pv = c.sem("unit_pv")
        o_ready = c.sem("o_ready")
        o_read = c.sem("o_read")
        stored = [c.sem(f"stored{u}") for u in range(2)]
        chain = c.sem("chain")
        acc_ready = c.sem("acc_ready")
        all_ready = c.sem("all_ready")
        scalars = c.sem("scalars")
        block = stack.enter_context(nc.Block())

        @block.sync
        def _(sp):
            sp.dma_start(maxima[0:TR], io["row_max"].rearrange("b p h -> p b h")).then_inc(maxima_in, 16)

            def load(r):
                if not r.first:
                    sp.wait_ge(scores_ps, r.b * PAIRS - PAIRS)
                    sp.sem_inc(passed, 1)
                    sp.wait_ge(v_ready, r.b - 1)
                    sp.sem_inc(passed, 1)
                sp.dma_start(qk[:, r.u], io["qk"][r.b]).then_inc(rows_in[r.u], 16)
                sp.dma_start(v[0:TR, r.u], io["v"][r.b]).then_inc(rows_in[r.u], 16)

            def store(r):
                sp.wait_ge(o_ready, r.b + 1)
                sp.dma_start(io["o"][r.b], o[0:TR, r.u]).then_inc(stored[r.u], 16)

            load_store_rows(sp, load, store)
            for u in range(2):
                sp.wait_ge(stored[u], 16 + 8 * B)

        @block.tensor
        def _(pe):
            pe.sem_inc(unit_pv, 2)
            pe.sem_inc(pv_done, 2)

            def scores(r, p):
                if p == 0:
                    pe.wait_ge(rows_in[r.u], r.k * 32 + 32)
                    pe.wait_ge(mcol_ready, r.b + 1)
                pe.wait_ge(d0_done, r.b * PAIRS + (p + 1))
                for e in range(2):
                    h = 2 * p + e
                    for i in range(2):
                        col = mcol[0:TR, r.u, 2 * h + i:2 * h + i + 1].to_broadcast([TR, TR])
                        nc.tensor.matmul(ps_m[0:TR, p % 2, e, i * TR:i * TR + TR], col, keep["identb"][0:TR, 0:TR],
                                         start=True, stop=True)
                for e in range(2):
                    g, at = (2 * p + e) // 4, HPB * ((2 * p + e) % 4)
                    for i in range(2):
                        last = nc.tensor.matmul(ps_s[0:TR, p % 2, e, i, 0:S],
                                                qk[at:at + HPB, r.u, GROUPS + g, i * TR:i * TR + TR],
                                                qk[at:at + HPB, r.u, g, :], start=True, stop=True)
                last.then_inc(scores_ps, 1)

            def values(r, p):
                if p == 0:
                    pe.wait_ge(v_ready, r.b + 1)
                    pe.wait_ge(o_read, r.b + 1)
                pe.wait_ge(e_done, r.b * PAIRS + (p + 3))
                for e in range(2):
                    h = 2 * p + e
                    for i in range(2):
                        at = (i * HEADS + h) * (HD + 1)
                        for j in range(2):
                            last = nc.tensor.matmul(ps_o[0:TR, r.u, at:at + HD + 1],
                                                    e_[0:TR, p % 2, e, j, i * TR:i * TR + TR],
                                                    vf[0:TR, r.u, j, h, :], start=(j == 0), stop=(j == 1))
                last.then_inc(unit_pv, 1)
                if p == PAIRS - 1:
                    pe.wait_ge(unit_pv, r.b * PAIRS + (PAIRS + 2))
                    pe.sem_inc(pv_done, 1)

            def step(r, before):
                for p in range(PAIRS):
                    scores(r, p)
                    at = lagged(r, before, p, 3)
                    if at:
                        values(*at)

            rows_skewed(pe, lambda r: step(r, None), step, lambda r: [values(r, p) for p in range(3, PAIRS)])

        @block.scalar
        def _(act):
            act.sem_inc(d0_done, 2)
            act.sem_inc(e_done, 2)
            act.sem_inc(o_read, 2)
            for u in range(2):
                act.sem_inc(stored[u], 16)
            act.wait_ge(maxima_in, 16)
            nc.scalar.activation(rounded[0:TR], maxima[0:TR], ACT.Identity, scale=par(keep, "c_a", TR),
                                 bias=keep["magic"][0:TR, :]).then_inc(rounded_ready, 1)

            def quantise(r, p):
                n = r.b * PAIRS + (p + 1)
                act.wait_ge(scores_ps, n)
                nc.scalar.activation(t[0:TR, p % 2], ps_s[0:TR, p % 2, :, :, 0:S], ACT.Identity,
                                     scale=par(keep, "c_a", TR), bias=keep["magic"][0:TR, :]).then_inc(t_ready, 1)

            def round_k(r, p):
                act.wait_ge(kf_ready, r.b * PAIRS + (p + 1))
                nc.scalar.activation(k[0:TR, p % 2], kf[0:TR, p % 2], ACT.Identity,
                                     bias=keep["magic"][0:TR, :]).then_inc(k_ready, 1)

            def square(r, p):
                act.wait_ge(rem_ready, r.b * PAIRS + (p + 1))
                nc.scalar.activation(sq[0:TR, p % 2], rem[0:TR, p % 2], ACT.Square,
                                     bias=par(keep, "b_half", TR)).then_inc(sq_ready, 1)

            def step(r, before):
                for p in range(PAIRS):
                    quantise(r, p)
                    for f, lag in ((round_k, 1), (square, 2)):
                        at = lagged(r, before, p, lag)
                        if at:
                            f(*at)

            def last(r):
                round_k(r, PAIRS - 1)
                square(r, PAIRS - 2)
                square(r, PAIRS - 1)

            rows_skewed(act, lambda r: step(r, None), step, last)

        @block.gpsimd
        def _(pool):
            nc.gpsimd.memset(vf[:], 1.0).then_inc(ones_ready, 1)
            pool.wait_ge(ones_ready, 1)
            pool.wait_ge(steps_ready, 1)

            def prepare(r):
                pool.wait_ge(pv_done, r.b + 1)
                pool.wait_ge(rows_in[r.u], r.k * 32 + 32)
                nc.gpsimd.tensor_copy(mcol[0:TR, r.u, :], steps[0:TR, bass.ds(r.b, 1), :]).then_inc(mcol_ready, 1)
                for j in range(2):
                    last = nc.gpsimd.tensor_copy(vf[0:TR, r.u, j, :, 0:HD],
                                                 v[0:TR, r.u, j, :].rearrange("p (h d) -> p h d", h=HEADS))
                last.then_inc(v_ready, 1)

            def divide(r, p):
                pool.wait_ge(d_ready, r.b * PAIRS + (p + 1))
                pool.sem_inc(passed, 1)
                nc.gpsimd.tensor_scalar(kf[0:TR, p % 2], d[0:TR, p % 2], par(keep, "n_inv", TR), par(keep, "n_bias", TR),
                                        ALU.mult, ALU.add).then_inc(kf_ready, 1)

            def power(r, p):
                pool.wait_ge(k_ready, r.b * PAIRS + (p + 1))
                pool.wait_ge(e_done, r.b * PAIRS + (p + 1))
                pool.sem_inc(passed, 1)
                nc.gpsimd.tensor_scalar(pw[0:TR, p % 2], low(k[0:TR, p % 2]), -(2.0**23), 127.0 * 2.0**23,
                                        ALU.mult, ALU.add).then_inc(pw_ready, 1)

            def work(r, before, units):
                for p in units:
                    divide(r, p)
                    at = lagged(r, before, p, 1)
                    if at:
                        power(*at)

            mid = PAIRS // 2

            def first(r):
                prepare(r)
                work(r, None, range(mid))

            def step(r, before):
                prepare(r)
                work(before, None, range(mid, PAIRS))
                work(r, before, range(mid))

            def last(r):
                work(r, None, range(mid, PAIRS))
                power(r, PAIRS - 1)

            rows_skewed(pool, first, step, last)
            pool.wait_ge(acc_ready, 1)
            nc.gpsimd.partition_all_reduce(extrema[:], acc[:], 128, RMAX).then_inc(all_ready, 1)

        @block.vector
        def _(dve):
            ch = Chain(dve, chain)
            ch.of(nc.vector.memset(acc[:, 0:1], -BIG))
            ch.of(nc.vector.memset(acc[:, 1:2], BIG))
            ch.sync()
            dve.wait_ge(rounded_ready, 1)
            nc.vector.tensor_scalar(steps[0:TR], rounded[0:TR], par(keep, "a_top", TR), MAGIC, ALU.min, ALU.subtract)\
                .then_inc(steps_ready, 1)

            def differences(r, p):
                n = r.b * PAIRS + (p + 1)
                dve.wait_ge(t_ready, n)
                for e in range(2):
                    m = ps_m[0:TR, p % 2, e:e + 1, 0:S].to_broadcast([TR, 2, S])
                    last = nc.vector.tensor_tensor(d0[0:TR, p % 2, e], low(t[0:TR, p % 2])[:, e], m, ALU.subtract)
                last.then_inc(d0_done, 1)
                dve.wait_ge(d0_done, r.b * PAIRS + (p + 3))
                nc.vector.tensor_scalar(d[0:TR, p % 2], d0[0:TR, p % 2], 0.0, par(keep, "n_least", TR), ALU.min, ALU.max)\
                    .then_inc(d_ready, 1)

            def remainder(r, p):
                n = r.b * PAIRS + (p + 1)
                dve.wait_ge(k_ready, n)
                nc.vector.tensor_scalar(kn[0:TR, p % 2], low(k[0:TR, p % 2]), par(keep, "n_step", TR), None, ALU.mult)\
                    .then_inc(kn_ready, 1)
                dve.wait_ge(kn_ready, n)
                nc.vector.tensor_tensor(rem[0:TR, p % 2], d[0:TR, p % 2], kn[0:TR, p % 2], ALU.add).then_inc(rem_ready, 1)

            def exponential(r, p):
                n = r.b * PAIRS + (p + 1)
                dve.wait_ge(sq_ready, n)
                dve.wait_ge(pw_ready, n)
                dve.wait_ge(unit_pv, n)
                nc.vector.scalar_tensor_tensor(e_[0:TR, p % 2], sq[0:TR, p % 2], par(keep, "c_rest", TR),
                                               pw[0:TR, p % 2].bitcast(F32), ALU.add, ALU.mult).then_inc(e_done, 1)

            def normalise(r):
                sums = ps_o[0:TR, r.u, 0:2 * HEADS * (HD + 1)].rearrange("p (i h d) -> p i h d", i=2, h=HEADS)
                dve.wait_ge(pv_done, r.b + 3)
                ch.link(nc.vector.reciprocal(inv_sum[0:TR], sums[:, :, :, HD]))
                dve.wait_ge(stored[r.u], r.k * 16 + 16)
                out = o[0:TR, r.u].rearrange("p i (h d) -> p i h d", h=HEADS)
                for i in range(2):
                    last = nc.vector.scalar_tensor_tensor(
                        out[:, i], sums[:, i, :, 0:HD], par(keep, "s_v", TR),
                        inv_sum[0:TR, i].unsqueeze(2).to_broadcast([TR, HEADS, HD]), ALU.mult, ALU.mult)
                    if i == 0:
                        ch.of(last)
                last.then_inc(o_ready, 1)
                dve.wait_ge(o_ready, r.b + 1)
                dve.sem_inc(o_read, 1)
                ch.of(nc.vector.tensor_reduce(ext[0:TR, 0:1], o[0:TR, r.u], AX.XY, ALU.max))
                ch.of(nc.vector.tensor_reduce(ext[0:TR, 1:2], o[0:TR, r.u], AX.XY, ALU.min))
                ch.sync()
                ch.of(nc.vector.tensor_tensor(acc[0:TR, 0:1], acc[0:TR, 0:1], ext[0:TR, 0:1], ALU.max))
                ch.of(nc.vector.tensor_tensor(acc[0:TR, 1:2], acc[0:TR, 1:2], ext[0:TR, 1:2], ALU.min))
                ch.sync()

            ahead, per_row = 2, 6

            def step(r, before):
                if before is not None:
                    ch.start(before.b * per_row + ahead)
                for p in range(PAIRS):
                    if p == 4 and before is not None:
                        normalise(before)
                        assert ch.n == per_row
                    differences(r, p)
                    for f, lag in ((remainder, 1), (exponential, 2)):
                        at = lagged(r, before, p, lag)
                        if at:
                            f(*at)

            def last(r):
                remainder(r, PAIRS - 1)
                exponential(r, PAIRS - 2)
                exponential(r, PAIRS - 1)
                ch.start(r.b * per_row + ahead)
                normalise(r)

            rows_skewed(dve, lambda r: step(r, None), step, last)
            nc.vector.tensor_scalar(acc[:, 1:2], acc[:, 1:2], -1.0, None, ALU.mult).then_inc(acc_ready, 1)
            dve.wait_ge(all_ready, 1)
            quantiser_out(nc, dve, Chain(dve, scalars), keep["par"], extrema, "o")


def project_out_pass(nc, io, keep):
    with ExitStack() as stack:
        c = Ctx(nc, stack, "projq_")
        o = c.sb("o", [128, 2, 2, D])
        x = c.sb("x", [128, 2, 2, D])
        oi = c.sb("oi", [128, 2, 2, D], BF16)
        oiT = c.sb("oiT", [DH, 2, 2, S], BF16)
        scale = c.sb("scale", [128, D])
        bias = c.sb("bias", [128, D])
        scaled = c.sb("scaled", [128, 2, 2, D])
        y = c.sb("y", [128, 2, 2, D])
        ext = c.sb("ext", [128, 2])
        acc = c.sb("acc", [128, 2])
        extrema = c.sb("extrema", [128, 2])
        ps_t = c.ps("ps_t", [128, 2, 2, 512], BF16)
        ps_y = c.ps("ps_y", [128, 2, 2, 256])
        loaded = c.sem("loaded")
        passed = c.sem("passed")
        o_in = [c.sem(f"o_in{u}") for u in range(2)]
        x_ready = c.sem("x_ready")
        oi_ready = c.sem("oi_ready")
        oiT_ps = c.sem("oiT_ps")
        oiT_ready = c.sem("oiT_ready")
        y_ps = c.sem("y_ps")
        scaled_done = c.sem("scaled_done")
        y_ready = c.sem("y_ready")
        stored = [c.sem(f"stored{u}") for u in range(2)]
        chain = c.sem("chain")
        acc_ready = c.sem("acc_ready")
        all_ready = c.sem("all_ready")
        scalars = c.sem("scalars")
        block = stack.enter_context(nc.Block())

        @block.sync
        def _(sp):
            sp.dma_start(bias[:], io["bproj_q"].partition_broadcast(128)).then_inc(loaded, 16)

            def load(r):
                if not r.first:
                    sp.wait_ge(x_ready, r.b - 1)
                    sp.sem_inc(passed, 1)
                sp.dma_start(o[0:TR, r.u], io["o"][r.b]).then_inc(o_in[r.u], 16)

            def store(r):
                sp.wait_ge(y_ready, r.b + 1)
                sp.dma_start(io["y"][r.b], y[0:TR, r.u]).then_inc(stored[r.u], 16)

            load_store_rows(sp, load, store)
            for u in range(2):
                sp.wait_ge(stored[u], 16 + 8 * B)

        @block.tensor
        def _(pe):
            def transposes(r):
                pe.wait_ge(oi_ready, r.b + 1)
                for h in range(2):
                    for t in range(2):
                        last = nc.tensor.transpose(ps_t[0:DH, r.u, h, t * TR + t:t * TR + t + TR],
                                                   oi[0:TR, r.u, t, h * DH:h * DH + DH], keep["identb"][0:TR, 0:TR])
                last.then_inc(oiT_ps, 1)

            def project(r):
                pe.wait_ge(oiT_ready, r.b + 1)
                pe.wait_ge(scaled_done, r.b + 1)
                for t in range(2):
                    for h in range(2):
                        last = nc.tensor.matmul(ps_y[0:TR, r.u, t, 0:D], oiT[:, r.u, h, t * TR:t * TR + TR],
                                                keep["wp"][:, h, :], start=(h == 0), stop=(h == 1))
                last.then_inc(y_ps, 1)

            def step(r, before):
                transposes(r)
                project(before)

            rows_skewed(pe, transposes, step, project)

        @block.scalar
        def _(act):
            act.sem_inc(scaled_done, 2)
            for u in range(2):
                act.sem_inc(stored[u], 16)

            def scale_in(r):
                act.wait_ge(o_in[r.u], r.k * 16 + 16)
                nc.scalar.activation(x[0:TR, r.u], o[0:TR, r.u], ACT.Identity, scale=par(keep, "o_inv", TR),
                                     bias=keep["magic"][0:TR, :]).then_inc(x_ready, 1)

            def copy(r):
                act.wait_ge(oiT_ps, r.b + 1)
                for t in range(2):
                    last = nc.scalar.activation(oiT[:, r.u, :, t * TR:t * TR + TR],
                                                ps_t[0:DH, r.u, :, t * TR + t:t * TR + t + TR], ACT.Copy)
                last.then_inc(oiT_ready, 1)

            def step(r, before):
                scale_in(r)
                copy(before)

            rows_skewed(act, scale_in, step, copy)

        @block.gpsimd
        def _(pool):
            pool.wait_ge(acc_ready, 1)
            nc.gpsimd.partition_all_reduce(extrema[:], acc[:], 128, RMAX).then_inc(all_ready, 1)

        @block.vector
        def _(dve):
            ch = Chain(dve, chain)
            ch.of(nc.vector.memset(acc[:, 0:1], -BIG))
            ch.of(nc.vector.memset(acc[:, 1:2], BIG))
            ch.of(nc.vector.tensor_scalar(scale[:], keep["wp_scale"][:], par(keep, "o_scale"), None, ALU.mult))
            ch.sync()
            dve.wait_ge(loaded, 16)

            def round_in(r):
                dve.wait_ge(x_ready, r.b + 1)
                nc.vector.tensor_scalar(oi[0:TR, r.u], x[0:TR, r.u], par(keep, "o_top", TR), MAGIC, ALU.min, ALU.subtract)\
                    .then_inc(oi_ready, 1)

            def finish(r):
                ch.start(r.b * 4 + 3)
                dve.wait_ge(y_ps, r.b + 1)
                nc.vector.tensor_tensor(scaled[0:TR, r.u], ps_y[0:TR, r.u, :, 0:D],
                                        scale[0:TR].unsqueeze(1).to_broadcast([TR, 2, D]), ALU.mult).then_inc(scaled_done, 1)
                dve.wait_ge(scaled_done, r.b + 3)
                dve.wait_ge(stored[r.u], r.k * 16 + 16)
                nc.vector.tensor_tensor(y[0:TR, r.u], scaled[0:TR, r.u],
                                        bias[0:TR].unsqueeze(1).to_broadcast([TR, 2, D]), ALU.add).then_inc(y_ready, 1)
                dve.wait_ge(y_ready, r.b + 1)
                ch.of(nc.vector.tensor_reduce(ext[0:TR, 0:1], y[0:TR, r.u], AX.XY, ALU.max))
                ch.of(nc.vector.tensor_reduce(ext[0:TR, 1:2], y[0:TR, r.u], AX.XY, ALU.min))
                ch.sync()
                ch.of(nc.vector.tensor_tensor(acc[0:TR, 0:1], acc[0:TR, 0:1], ext[0:TR, 0:1], ALU.max))
                ch.of(nc.vector.tensor_tensor(acc[0:TR, 1:2], acc[0:TR, 1:2], ext[0:TR, 1:2], ALU.min))
                ch.sync()

            def step(r, before):
                round_in(r)
                finish(before)

            rows_skewed(dve, round_in, step, finish)
            nc.vector.tensor_scalar(acc[:, 1:2], acc[:, 1:2], -1.0, None, ALU.mult).then_inc(acc_ready, 1)
            dve.wait_ge(all_ready, 1)
            quantiser_out(nc, dve, Chain(dve, scalars), keep["par"], extrema, "y")


def softmax_attention_pass(nc, io, keep):
    with ExitStack() as stack:
        c = Ctx(nc, stack, "fattn_")
        w = c.sb("w", [DH + 1, 2, QKV])
        wo = c.sb("wo", [DH + 1, 2, D])
        wg = c.sb("wg", [DH + 1, 2, EXPERTS])
        gb = c.sb("gb", [DH, 2, 2, 2])
        y = c.sb("y", [128, 2, 2, D])
        h1 = c.sb("h1", [128, 2, 2, D])
        xy = c.sb("xy", [128, 2, 2, D])
        yi = c.sb("yi", [128, 2, D])
        ax = c.sb("ax", [128, 2, 2, 2, D])
        cx = c.sb("cx", [128, 2, 2, 2, D])
        z = c.sb("z", [128, 2, D])
        zT = c.sb("zT", [DH + 1, 2, S])
        qk = c.sb("qk", [128, 2, 6, S])
        v = c.sb("v", [128, 2, 2, HEADS, HD + 1])
        top = c.sb("top", [128, 3, 2])
        p_ = c.sb("p", [128, 3, 2, S])
        pT = c.sb("pT", [128, 3, 2, S])
        inv_sum = c.sb("inv_sum", [128, 2, HEADS])
        att = c.sb("att", [128, 2, D])
        attT = c.sb("attT", [DH + 1, 2, S])
        x2 = c.sb("x2", [128, 2, D])
        hx = c.sb("hx", [128, 2, 2, D])
        zn = c.sb("zn", [128, 2, 2, D])
        znT = c.sb("znT", [DH + 1, 2, S])
        logits = c.sb("logits", [128, 2, 2, EXPERTS])
        ln1, ln2, ln3 = (NormTiles(c, f"n{i}_") for i in range(1, 4))
        ps_s = c.ps("ps_s", [128, 2, 2, 256])
        ps_t = c.ps("ps_t", [128, 2, 2, 256])
        ps_a = c.ps("ps_a", [128, 2, 256])
        ps_c = c.ps("ps_c", [128, 2, 256])
        ps_o = c.ps("ps_o", [128, 2, 512])
        A_JOBS = 5

        loaded = c.sem("loaded")
        ones_ready = c.sem("ones_ready")
        passed = c.sem("passed")
        rows_in = [c.sem(f"rows_in{u}") for u in range(2)]
        cx_in = [c.sem(f"cx_in{u}") for u in range(2)]
        ax_stored = [c.sem(f"ax_stored{u}") for u in range(2)]
        stored = [c.sem(f"stored{u}") for u in range(2)]
        xy_ready = c.sem("xy_ready")
        yi_ready = c.sem("yi_ready")
        h2_ready = c.sem("h2_ready")
        xl_ready = c.sem("xl_ready")
        z_ready = c.sem("z_ready")
        a_ps = c.sem("a_ps")
        a_done = c.sem("a_done")
        scores_ps = c.sem("scores_ps")
        top_ready = c.sem("top_ready")
        p_done = c.sem("p_done")
        t_done = c.sem("t_done")
        pT_done = c.sem("pT_done")
        pv_done = c.sem("pv_done")
        o_read = c.sem("o_read")
        att_ready = c.sem("att_ready")
        attT_ps = c.sem("attT_ps")
        attT_ready = c.sem("attT_ready")
        proj_ps = c.sem("proj_ps")
        x2_ready = c.sem("x2_ready")
        hx_ready = c.sem("hx_ready")
        zn_ready = c.sem("zn_ready")
        znT_ps = c.sem("znT_ps")
        znT_ready = c.sem("znT_ready")
        gate_ps = c.sem("gate_ps")
        logits_done = c.sem("logits_done")
        chain_a = c.sem("chain_a")
        chain_c = c.sem("chain_c")
        block = stack.enter_context(nc.Block())

        def unit(r, h):
            return r.b * HEADS + h

        def lag(b1, b2, h, n):
            row, head = (b1, h - n) if h >= n else (b2, HEADS + h - n)
            return [(row, head)] if row is not None else []

        @block.sync
        def _(sp):
            for tile, name in ((w, "wqkv_f"), (wo, "wproj_f"), (wg, "wgate"), (gb, "gains")):
                sp.dma_start(tile[:], io[name]).then_inc(loaded, 16)

            def step(a, r, b1, b2):
                if a is not None:
                    if not (isinstance(a.b, int) and a.b < 2):
                        sp.wait_ge(h2_ready, a.b - 1)
                        sp.sem_inc(passed, 1)
                    sp.dma_start(y[0:TR, a.u], io["y"][a.b]).then_inc(rows_in[a.u], 16)
                    sp.dma_start(h1[0:TR, a.u], io["h1"][a.b]).then_inc(rows_in[a.u], 16)
                if r is not None:
                    sp.wait_ge(xl_ready, r.b + 1)
                    sp.sem_inc(passed, 1)
                    sp.dma_start(io["hxl"][r.b], ax[0:TR, r.u]).then_inc(ax_stored[r.u], 16)
                if b1 is not None:
                    sp.wait_ge(ax_stored[b1.u], b1.k * 16 + 32)
                    sp.sem_inc(passed, 1)
                    if not (isinstance(b1.b, int) and b1.b < 2):
                        sp.wait_ge(hx_ready, b1.b - 1)
                        sp.sem_inc(passed, 1)
                    sp.dma_start(cx[0:TR, b1.u], io["hxl"][b1.b]).then_inc(cx_in[b1.u], 16)
                if b2 is not None:
                    sp.wait_ge(hx_ready, b2.b + 1)
                    sp.sem_inc(passed, 1)
                    sp.dma_start(io["hx"][b2.b], hx[0:TR, b2.u]).then_inc(stored[b2.u], 16)
                    sp.wait_ge(zn_ready, b2.b + 1)
                    sp.sem_inc(passed, 1)
                    sp.dma_start(io["zn"][b2.b], zn[0:TR, b2.u]).then_inc(stored[b2.u], 16)
                    sp.wait_ge(logits_done, b2.b + 2)
                    sp.sem_inc(passed, 1)
                    sp.dma_start(io["logits"][b2.b], logits[0:TR, b2.u]).then_inc(stored[b2.u], 16)

            rows_deep(sp, step, 4)
            for u in range(2):
                sp.wait_ge(stored[u], 48 + 24 * B)
                sp.wait_ge(ax_stored[u], 16 + 8 * B)

        @block.tensor
        def _(pe):
            pe.wait_ge(loaded, 64)
            pe.wait_ge(ones_ready, 4)
            ident = keep["ident"][0:TR, 0:TR]

            def scores(r, h):
                pe.wait_ge(p_done, unit(r, h) + 1)
                g, at = h // 4, HPB * (h % 4)
                for t in range(2):
                    last = nc.tensor.matmul(ps_s[0:TR, h % 2, t, 0:S], qk[at:at + HPB, r.u, g, t * TR:t * TR + TR],
                                            qk[at:at + HPB, r.u, GROUPS + g, :], start=True, stop=True)
                last.then_inc(scores_ps, 1)

            def turn(r, h):
                pe.wait_ge(p_done, unit(r, h) + 3)
                pe.wait_ge(pT_done, unit(r, h) + 1)
                for t in range(2):
                    for j in range(2):
                        last = nc.tensor.transpose(ps_t[0:TR, h % 2, j, t * TR:t * TR + TR],
                                                   p_[0:TR, h % 3, t, j * TR:j * TR + TR], ident)
                last.then_inc(t_done, 1)

            def values(r, h):
                if h == 0:
                    pe.wait_ge(o_read, r.b + 1)
                pe.wait_ge(pT_done, unit(r, h) + 3)
                for t in range(2):
                    at = (t * HEADS + h) * (HD + 1)
                    for j in range(2):
                        last = nc.tensor.matmul(ps_o[0:TR, r.u, at:at + HD + 1], pT[0:TR, h % 3, j, t * TR:t * TR + TR],
                                                v[0:TR, r.u, j, h, :], start=(j == 0), stop=(j == 1))
                last.then_inc(pv_done, 1)

            def make_qkv(r, job):
                pe.wait_ge(a_done, r.b * A_JOBS + (job + 1))
                if job == 0:
                    pe.wait_ge(z_ready, r.b + 1)
                    last = turn_tokens(nc, ps_a, z, ident)
                elif job < 4:
                    if job == 1:
                        pe.wait_ge(a_done, r.b * A_JOBS + 2)
                    for m in range(2):
                        last = project_heads(nc, ps_a, w, zT, m, 2 * (job - 1) + m)
                else:
                    last = project_values(nc, ps_a, w, zT)
                last.then_inc(a_ps, 1)

            def step(r, b1, b2):
                for h in range(HEADS):
                    if b1 is not None:
                        scores(b1, h)
                    for row, head in lag(b1, b2, h, 2):
                        turn(row, head)
                    for row, head in lag(b1, b2, h, 3):
                        values(row, head)
                    if r is not None and 6 <= h < 6 + A_JOBS:
                        make_qkv(r, h - 6)
                    if b2 is None:
                        continue
                    if h == 4:
                        pe.wait_ge(logits_done, b2.b + 1)
                        pe.wait_ge(att_ready, b2.b + 1)
                        turn_tokens(nc, ps_c, att, ident).then_inc(attT_ps, 1)
                    if h == 5:
                        pe.wait_ge(attT_ready, b2.b + 1)
                        project_tokens(nc, ps_c, wo, attT, D).then_inc(proj_ps, 1)
                    if h == 10:
                        pe.wait_ge(zn_ready, b2.b + 1)
                        turn_tokens(nc, ps_c, zn[:, b2.u], ident).then_inc(znT_ps, 1)
                    if h == 11:
                        pe.wait_ge(znT_ready, b2.b + 1)
                        project_tokens(nc, ps_c, wg, znT, EXPERTS).then_inc(gate_ps, 1)

            rows_deep(pe, step, 3)

        @block.scalar
        def _(act):
            act.sem_inc(a_done, 1)
            act.sem_inc(p_done, 2)
            act.sem_inc(t_done, 3)
            act.sem_inc(pT_done, 2)
            act.sem_inc(pv_done, 3)
            act.sem_inc(o_read, 2)
            act.sem_inc(logits_done, 1)
            for u in range(2):
                act.sem_inc(ax_stored[u], 16)
                act.sem_inc(stored[u], 48)
            act.wait_ge(loaded, 64)
            act.wait_ge(ones_ready, 4)

            def exponential(r, h):
                act.wait_ge(top_ready, unit(r, h) + 1)
                act.wait_ge(t_done, unit(r, h) + 1)
                for t in range(2):
                    last = nc.scalar.activation(p_[0:TR, h % 3, t, :], ps_s[0:TR, h % 2, t, 0:S], ACT.Exp,
                                                bias=top[0:TR, h % 3, t:t + 1])
                last.then_inc(p_done, 1)

            def affine(dst, ps, norm):
                for half in range(2):
                    last = nc.scalar.activation(dst[0:DH, half, :], ps[0:DH, half, 0:S], ACT.Identity,
                                                scale=gb[:, norm, 0, half:half + 1], bias=gb[:, norm, 1, half:half + 1])
                return last

            def read_qkv(r, job):
                act.wait_ge(a_ps, r.b * A_JOBS + (job + 1))
                if job == 0:
                    last = affine(zT, ps_a, 0)
                elif job < 4:
                    m = 2 * (job - 1)
                    for i in range(2):
                        last = nc.scalar.mul(qk[:, r.u, m + i, :], ps_a[:, i, 0:S], HD**-0.5 if m + i < GROUPS else 1.0)
                else:
                    last = nc.scalar.activation(v[0:TR, r.u, :, :, 0:HD],
                                                ps_a[0:TR, :, 0:D].rearrange("p j (h d) -> p j h d", h=HEADS), ACT.Copy)
                last.then_inc(a_done, 1)

            def step(r, b1, b2):
                if r is not None:
                    act.wait_ge(rows_in[r.u], r.k * 32 + 32)
                    nc.scalar.activation(xy[0:TR, r.u], y[0:TR, r.u], ACT.Identity, scale=par(keep, "y_inv", TR),
                                         bias=keep["magic"][0:TR, :]).then_inc(xy_ready, 1)
                for h in range(HEADS):
                    if b1 is not None:
                        exponential(b1, h)
                    if r is not None and 6 <= h < 6 + A_JOBS:
                        read_qkv(r, h - 6)
                    if b2 is not None and h == 4:
                        act.wait_ge(attT_ps, b2.b + 1)
                        nc.scalar.activation(attT[0:DH], ps_c[0:DH, :, 0:S], ACT.Copy).then_inc(attT_ready, 1)
                    if b2 is not None and h == 10:
                        act.wait_ge(znT_ps, b2.b + 1)
                        affine(znT, ps_c, 1).then_inc(znT_ready, 1)

            rows_deep(act, step, 3)

        @block.gpsimd
        def _(pool):
            for n, tile in enumerate((zT[DH:DH + 1], attT[DH:DH + 1], znT[DH:DH + 1], v[:])):
                nc.gpsimd.memset(tile, 1.0).then_inc(ones_ready, 1)
                pool.wait_ge(ones_ready, n + 1)
            for ln in (ln1, ln2, ln3):
                nc.gpsimd.memset(ln.half[:], -0.5).then_inc(ln.half_ready, 1)
                pool.wait_ge(ln.half_ready, 1)

            def step(r, b1, b2):
                for row, ln in ((r, ln1), (r, ln2), (b2, ln3)):
                    if row is not None:
                        inverse_root(nc, pool, ln, row.b)

            rows_deep(pool, step, 3)

        @block.vector
        def _(dve):
            cha, chc = Chain(dve, chain_a), Chain(dve, chain_c)
            a_count, c_count = 8, 5

            def row_top(r, h):
                dve.wait_ge(scores_ps, unit(r, h) + 1)
                nc.vector.tensor_reduce(top[0:TR, h % 3, :], ps_s[0:TR, h % 2, :, 0:S], AX.X, ALU.max, negate=True)\
                    .then_inc(top_ready, 1)

            def copy_turned(r, h):
                dve.wait_ge(t_done, unit(r, h) + 4)
                dve.wait_ge(pv_done, unit(r, h) + 1)
                nc.vector.tensor_copy(pT[0:TR, h % 3], ps_t[0:TR, h % 2, :, 0:S]).then_inc(pT_done, 1)

            def stage_a(r, h):
                h2, xl = ax[:, r.u, 0], ax[:, r.u, 1]
                if h == 0:
                    cha.start(r.b * a_count)
                    dve.wait_ge(xy_ready, r.b + 1)
                    dve.wait_ge(ax_stored[r.u], r.k * 16 + 16)
                    nc.vector.tensor_scalar(yi[0:TR], xy[0:TR, r.u], par(keep, "y_top", TR), MAGIC, ALU.min, ALU.subtract)\
                        .then_inc(yi_ready, 1)
                    dve.wait_ge(yi_ready, r.b + 1)
                    nc.vector.scalar_tensor_tensor(h2[0:TR], yi[0:TR], par(keep, "y_scale", TR), h1[0:TR, r.u],
                                                   ALU.mult, ALU.add).then_inc(h2_ready, 1)
                if h == 1:
                    dve.wait_ge(h2_ready, r.b + 1)
                    norm_stats(nc, dve, cha, h2, ln1)
                if h == 2:
                    norm_apply(nc, dve, h2, xl, ln1, r.b).then_inc(xl_ready, 1)
                if h == 3:
                    dve.wait_ge(xl_ready, r.b + 1)
                    norm_stats(nc, dve, cha, xl, ln2)
                if h == 5:
                    norm_apply(nc, dve, xl, z, ln2, r.b).then_inc(z_ready, 1)
                    assert cha.n == a_count

            def stage_c(r, h):
                if h == 3:
                    chc.start(r.b * c_count)
                    dve.wait_ge(pv_done, unit(r, HEADS - 1) + 4)
                    sums = ps_o[0:TR, r.u, 0:2 * HEADS * (HD + 1)].rearrange("p (i h d) -> p i h d", i=2, h=HEADS)
                    chc.link(nc.vector.reciprocal(inv_sum[0:TR], sums[:, :, :, HD]))
                    for i in range(2):
                        last = nc.vector.tensor_tensor(att[0:TR, i].rearrange("p (h d) -> p h d", h=HEADS),
                                                       sums[:, i, :, 0:HD],
                                                       inv_sum[0:TR, i].unsqueeze(2).to_broadcast([TR, HEADS, HD]), ALU.mult)
                    last.then_inc(att_ready, 1)
                    dve.wait_ge(att_ready, r.b + 1)
                    dve.sem_inc(o_read, 1)
                if h == 7:
                    dve.wait_ge(proj_ps, r.b + 1)
                    dve.wait_ge(cx_in[r.u], r.k * 16 + 16)
                    nc.vector.tensor_tensor(x2[0:TR], ps_c[0:TR, :, 0:D], cx[0:TR, r.u, 1], ALU.add).then_inc(x2_ready, 1)
                    dve.wait_ge(x2_ready, r.b + 1)
                    dve.wait_ge(stored[r.u], r.k * 48 + 48)
                    nc.vector.tensor_tensor(hx[0:TR, r.u], x2[0:TR], cx[0:TR, r.u, 0], ALU.add).then_inc(hx_ready, 1)
                if h == 8:
                    norm_stats(nc, dve, chc, x2, ln3)
                if h == 9:
                    norm_apply(nc, dve, x2, zn[:, r.u], ln3, r.b).then_inc(zn_ready, 1)
                if h == 11:
                    dve.wait_ge(gate_ps, r.b + 1)
                    nc.vector.tensor_copy(logits[0:TR, r.u], ps_c[0:TR, :, 0:EXPERTS]).then_inc(logits_done, 1)
                    assert chc.n == c_count

            def step(r, b1, b2):
                for h in range(HEADS):
                    if b1 is not None:
                        row_top(b1, h)
                    for row, head in lag(b1, b2, h, 2):
                        copy_turned(row, head)
                    if r is not None:
                        stage_a(r, h)
                    if b2 is not None:
                        stage_c(b2, h)

            rows_deep(dve, step, 3)


class Ranks:

    def __init__(self, c, name):
        self.ps_low = c.ps(name + "ps_low", [128, NT, EXPERTS])
        self.ps_sum = c.ps(name + "ps_sum", [128, NT, EXPERTS])
        self.sums = c.sb(name + "sums", [128, NT, EXPERTS])
        self.scan = c.sb(name + "scan", [128, EXPERTS, NT])
        self.ones = c.sb(name + "ones", [128, NT])
        self.rank = c.sb(name + "rank", [128, NT, EXPERTS])
        self.mask_ready = c.sem(name + "mask_ready")
        self.counted = c.sem(name + "ranks_counted")

    def products(self, nc, pe, keep, mask, n):
        pe.wait_ge(self.mask_ready, n + 1)
        nc.tensor.matmul(self.ps_low[0:TR], keep["tri"][0:TR, 0:TR], mask, start=True, stop=True)
        nc.tensor.matmul(self.ps_sum[0:TR], keep["onesb"][0:TR, 0:TR], mask, start=True, stop=True)\
            .then_inc(self.counted, 1)

    def finish(self, nc, dve, ch, n):
        dve.wait_ge(self.counted, n + 1)
        ch.of(nc.vector.memset(self.ones[:], 1.0))
        ch.link(nc.vector.tensor_copy(self.sums[0:TR], self.ps_sum[0:TR]))
        for e in range(EXPERTS):
            ch.of(nc.vector.tensor_tensor_scan(self.scan[0:TR, e, :], self.ones[0:TR], self.sums[0:TR, :, e],
                                               0.0, ALU.mult, ALU.add))
        ch.sync()
        ch.link(nc.vector.tensor_tensor(self.rank[0:TR], self.scan[0:TR].rearrange("p e n -> p n e"), self.sums[0:TR],
                                        ALU.subtract))
        ch.link(nc.vector.tensor_tensor(self.rank[0:TR], self.rank[0:TR], self.ps_low[0:TR], ALU.add))


def by_expert(x):
    return x.unsqueeze(1).to_broadcast([TR, NT, EXPERTS])


def by_token(x):
    return x.unsqueeze(2).to_broadcast([TR, NT, EXPERTS])


def one_hot_first(nc, ch, keep, scores, best, work, first, onehot):
    ch.link(nc.vector.tensor_tensor(work, scores, by_token(best), ALU.is_equal))
    ch.link(nc.vector.tensor_tensor(work, work, by_expert(keep["falling"][0:TR]), ALU.mult))
    ch.link(nc.vector.tensor_reduce(first, work, AX.X, ALU.max))
    ch.link(nc.vector.tensor_tensor(onehot, work, by_token(first), ALU.is_equal))


def place_slots(nc, ch, keep, ranks_, base, tile_expert, tile_start, s):
    counts = ranks_.scan[0:TR, :, NT - 1]
    ch.link(nc.vector.tensor_scalar(s[0:TR, 0:8], counts, 1.0 / SLOTS, 0.5 - 0.5 / SLOTS, ALU.mult, ALU.add))
    ch.link(nc.vector.tensor_scalar(s[0:TR, 0:8], s[0:TR, 0:8], MAGIC, MAGIC, ALU.add, ALU.subtract))
    ch.link(nc.vector.tensor_scalar(s[0:TR, 0:8], s[0:TR, 0:8], float(SLOTS), None, ALU.mult))
    ch.link(nc.vector.memset(base[:], 0.0))
    for e in range(1, EXPERTS):
        ch.link(nc.vector.tensor_tensor(base[0:TR, e:e + 1], base[0:TR, e - 1:e], s[0:TR, e - 1:e], ALU.add))
    ch.link(nc.vector.tensor_tensor(ranks_.rank[0:TR], ranks_.rank[0:TR], by_expert(base[0:TR]), ALU.add))
    n = tile_start.shape[1]
    ch.link(nc.vector.memset(s[0:1, 16:16 + n], 0.0))
    for e in range(1, EXPERTS):
        ch.link(nc.vector.scalar_tensor_tensor(s[0:1, 16:16 + n], tile_start[0:1, :], base[0:1, e:e + 1],
                                               s[0:1, 16:16 + n], ALU.is_ge, ALU.add))
    ch.link(nc.vector.tensor_copy(tile_expert[0:1, 0:n], s[0:1, 16:16 + n]))


def route_two_pass(nc, io, keep):
    with ExitStack() as stack:
        c = Ctx(nc, stack, "route2_")
        logits = c.sb("logits", [128, NT, EXPERTS])
        left = c.sb("left", [128, NT, EXPERTS])
        work = c.sb("work", [128, NT, EXPERTS])
        hot = c.sb("hot", [128, 2, NT, EXPERTS])
        mask = c.sb("mask", [128, NT, EXPERTS], BF16)
        best = c.sb("best", [128, 2, NT])
        first = c.sb("first", [128, NT])
        weights = c.sb("weights", [128, NT, 2])
        gap = c.sb("gap", [128, NT])
        e2 = c.sb("e2", [128, NT])
        slot_f = c.sb("slot_f", [128, NT, 2])
        slots = c.sb("slots", [128, NT, 2], I32)
        base = c.sb("base", [128, EXPERTS])
        s = c.sb("s", [128, 16 + TILES2])
        rk = Ranks(c, "")
        loaded = c.sem("loaded")
        chain = c.sem("chain")
        gap_ready = c.sem("gap_ready")
        e2_ready = c.sem("e2_ready")
        slots_ready = c.sem("slots_ready")
        stored = c.sem("stored")
        block = stack.enter_context(nc.Block())

        @block.sync
        def _(sp):
            sp.dma_start(logits[0:TR].rearrange("p (b t) e -> p b (t e)", t=2),
                         io["logits"].rearrange("b p t e -> p b (t e)")).then_inc(loaded, 16)
            sp.wait_ge(slots_ready, 1)
            sp.dma_start(io["slots"].rearrange("b p c -> p b c"),
                         slots[0:TR].rearrange("p (b t) c -> p b (t c)", t=2)).then_inc(stored, 16)
            sp.dma_start(io["weights"].rearrange("b p c -> p b c"),
                         weights[0:TR].rearrange("p (b t) c -> p b (t c)", t=2)).then_inc(stored, 16)
            sp.wait_ge(stored, 32)

        @block.tensor
        def _(pe):
            rk.products(nc, pe, keep, mask[0:TR], 0)

        @block.scalar
        def _(act):
            act.wait_ge(gap_ready, 1)
            nc.scalar.activation(e2[0:TR], gap[0:TR], ACT.Exp).then_inc(e2_ready, 1)

        @block.vector
        def _(dve):
            ch = Chain(dve, chain)
            dve.wait_ge(loaded, 16)
            for n, source in ((0, logits), (1, left)):
                top = best[0:TR, n]
                ch.link(nc.vector.tensor_reduce(top, source[0:TR], AX.X, ALU.max))
                one_hot_first(nc, ch, keep, source[0:TR], top, work[0:TR], first[0:TR], hot[0:TR, n])
                if n == 0:
                    ch.link(nc.vector.scalar_tensor_tensor(left[0:TR], hot[0:TR, 0], -BIG, logits[0:TR], ALU.mult, ALU.add))
            nc.vector.tensor_tensor(gap[0:TR], best[0:TR, 1], best[0:TR, 0], ALU.subtract).then_inc(gap_ready, 1)
            nc.vector.tensor_tensor(mask[0:TR], hot[0:TR, 0], hot[0:TR, 1], ALU.add).then_inc(rk.mask_ready, 1)
            dve.wait_ge(e2_ready, 1)
            ch.link(nc.vector.tensor_scalar(gap[0:TR], e2[0:TR], 1.0, None, ALU.add))
            ch.link(nc.vector.reciprocal(weights[0:TR, :, 0], gap[0:TR]))
            ch.link(nc.vector.tensor_tensor(weights[0:TR, :, 1], weights[0:TR, :, 0], e2[0:TR], ALU.mult))
            rk.finish(nc, dve, ch, 0)
            place_slots(nc, ch, keep, rk, base, keep["tile_expert"], keep["tile_start"][:, 0:TILES2], s)
            for n in range(2):
                ch.link(nc.vector.tensor_tensor(work[0:TR], hot[0:TR, n], rk.rank[0:TR], ALU.mult))
                ch.link(nc.vector.tensor_reduce(slot_f[0:TR, :, n], work[0:TR], AX.X, ALU.add))
            nc.vector.tensor_copy(slots[0:TR], slot_f[0:TR]).then_inc(slots_ready, 1)


def scatter_pass(nc, io, source, choices):
    with ExitStack() as stack:
        c = Ctx(nc, stack, f"scatter{choices}_")
        x = c.sb("x", [128, 2, 2, D])
        slots = c.sb("slots", [128, 2, 2 * choices], I32)
        rows_in = [c.sem(f"rows_in{u}") for u in range(2)]
        sent = [c.sem(f"sent{u}") for u in range(2)]
        passed = c.sem("passed")
        block = stack.enter_context(nc.Block())
        per_row = 32 * choices

        @block.sync
        def _(sp):
            def load(r):
                if not r.first:
                    sp.wait_ge(sent[r.u], r.k * per_row)
                    sp.sem_inc(passed, 1)
                sp.dma_start(x[0:TR, r.u], io[source][r.b]).then_inc(rows_in[r.u], 16)
                sp.dma_start(slots[0:TR, r.u], io["slots"][r.b][:, 0:2 * choices]).then_inc(rows_in[r.u], 16)

            load(Row(0, 0, 0, first=True))
            load(Row(1, 1, 0, first=True))
            with sp.Fori(1, B // 2) as i:
                for u in range(2):
                    load(Row(i * 2 + u, u, i))

        @block.gpsimd
        def _(pool):
            def send(r):
                pool.wait_ge(rows_in[r.u], r.k * 32 + 32)
                pool.sem_inc(passed, 1)
                for t in range(2):
                    for n in range(choices):
                        at = t * choices + n
                        nc.gpsimd.indirect_dma_start(
                            io["slotted"], bass.IndirectOffsetOnAxis(ap=slots[0:TR, r.u, at:at + 1], axis=0),
                            x[0:TR, r.u, t, :], None).then_inc(sent[r.u], 16)

            rows(pool, send)
            for u in range(2):
                pool.wait_ge(sent[u], per_row * B // 2)


def experts_pass(nc, io, keep, tiles, layer):
    with ExitStack() as stack:
        c = Ctx(nc, stack, f"experts{layer}_")
        w1 = c.sb("w1", [DH + 1, EXPERTS, 2, HIDDEN])
        w2 = c.sb("w2", [128, EXPERTS, HC, D])
        b2 = c.sb("b2", [128, EXPERTS, D])
        gb = c.sb("gb", [DH, 2, 2])
        x = c.sb("x", [128, 2, D])
        xT = c.sb("xT", [DH + 1, 2, 2, SLOTS])
        g = c.sb("g", [128, 2, HIDDEN])
        gT = c.sb("gT", [128, HC, SLOTS])
        out = c.sb("out", [128, 2, D])
        ps_x = c.ps("ps_x", [128, 2, 256])
        ps_h = c.ps("ps_h", [128, 2, 512])
        ps_g = c.ps("ps_g", [128, 2, 512])
        ps_o = c.ps("ps_o", [128, 2, 512])
        loaded = c.sem("loaded")
        ones_ready = c.sem("ones_ready")
        passed = c.sem("passed")
        x_in = [c.sem(f"x_in{u}") for u in range(2)]
        xT_ps = c.sem("xT_ps")
        xT_done = c.sem("xT_done")
        h_ps = c.sem("h_ps")
        g_done = c.sem("g_done")
        gT_ps = c.sem("gT_ps")
        gT_done = c.sem("gT_done")
        o_ps = c.sem("o_ps")
        out_done = c.sem("out_done")
        stored = [c.sem(f"stored{u}") for u in range(2)]
        block = stack.enter_context(nc.Block())
        half, hc = HIDDEN // 2, HC // 2
        loads = [(w1[:, e], f"w1_{layer}", e) for e in range(EXPERTS)] + [(w2[:, e], f"w2_{layer}", e) for e in range(EXPERTS)]

        @block.sync
        def _(sp):
            sp.dma_start(gb[:], io[f"gb_{layer}"]).then_inc(loaded, 16)
            sp.dma_start(b2[:].rearrange("p e d -> p (e d)"),
                         io[f"b2_{layer}"].rearrange("e d -> (e d)").partition_broadcast(128)).then_inc(loaded, 16)
            for tile, name, e in loads:
                sp.dma_start(tile, io[name][e]).then_inc(loaded, 16)

            def step(a, r, b1, b2_):
                if a is not None:
                    if not (isinstance(a.b, int) and a.b < 2):
                        sp.wait_ge(xT_ps, a.b - 1)
                        sp.sem_inc(passed, 1)
                    sp.dma_start(x[:, a.u], io["slotted"][bass.ds(a.b * SLOTS, SLOTS), :]).then_inc(x_in[a.u], 16)
                if b2_ is not None:
                    sp.wait_ge(out_done, b2_.b + 3)
                    sp.sem_inc(passed, 1)
                    sp.dma_start(io["slot_out"][bass.ds(b2_.b * SLOTS, SLOTS), :], out[:, b2_.u]).then_inc(stored[b2_.u], 16)

            rows_deep(sp, step, 4, tiles)
            for u in range(2):
                sp.wait_ge(stored[u], 16 + 8 * tiles)

        @block.tensor
        def _(pe):
            pe.wait_ge(loaded, 16 * (2 + len(loads)))
            pe.wait_ge(ones_ready, 1)

            def turn(r):
                pe.wait_ge(x_in[r.u], r.k * 16 + 16)
                pe.wait_ge(xT_done, r.b + 1)
                for i in range(2):
                    last = nc.tensor.transpose(ps_x[0:DH, i, 0:SLOTS], x[:, r.u, i * DH:i * DH + DH], keep["ident"][:])
                last.then_inc(xT_ps, 1)

            def hidden(r, e):
                pe.wait_ge(xT_done, r.b + 2)
                for n in range(2):
                    pe.wait_ge(g_done, r.b * 2 + (n + 1))
                    cols = slice(n * half, n * half + half)
                    nc.tensor.matmul(ps_h[:, n, 0:half], xT[0:DH, r.u, 0, :],
                                     w1[0:DH, bass.ds(e, 1), 0, cols].squeeze(1), start=True, stop=False)
                    nc.tensor.matmul(ps_h[:, n, 0:half], xT[:, r.u, 1, :],
                                     w1[:, bass.ds(e, 1), 1, cols].squeeze(1), start=False, stop=True).then_inc(h_ps, 1)

            def turn_hidden(r):
                for n in range(2):
                    pe.wait_ge(g_done, r.b * 2 + (n + 3))
                    pe.wait_ge(gT_done, r.b * 2 + (n + 1))
                    for i in range(hc):
                        at = (n * hc + i) * 128
                        last = nc.tensor.transpose(ps_g[:, n, i * SLOTS:i * SLOTS + SLOTS], g[:, r.u, at:at + 128],
                                                   keep["ident"][:])
                    last.then_inc(gT_ps, 1)

            def output(r, e):
                pe.wait_ge(out_done, r.b + 1)
                for i in range(HC):
                    if i % hc == 0:
                        pe.wait_ge(gT_done, r.b * 2 + (i // hc + 3))
                    last = nc.tensor.matmul(ps_o[:, r.u, 0:D], gT[:, i, :], w2[:, bass.ds(e, 1), i, :].squeeze(1),
                                            start=(i == 0), stop=(i == HC - 1))
                last.then_inc(o_ps, 1)

            def expert(r):
                return pe.value_load(keep["tile_expert"][0:1, bass.ds(r.b, 1)], min_val=0, max_val=EXPERTS - 1)

            def step(a, r, b1):
                if a is not None:
                    turn(a)
                if b1 is not None:
                    turn_hidden(b1)
                if r is not None:
                    hidden(r, expert(r))
                if b1 is not None:
                    output(b1, expert(b1))

            rows_deep(pe, step, 3, tiles)

        @block.scalar
        def _(act):
            act.sem_inc(xT_done, 1)
            act.sem_inc(g_done, 2)
            act.sem_inc(gT_done, 2)
            act.sem_inc(out_done, 2)
            for u in range(2):
                act.sem_inc(stored[u], 16)
            act.wait_ge(loaded, 16 * (2 + len(loads)))

            def step(a, r, b1):
                if a is not None:
                    act.wait_ge(xT_ps, a.b + 1)
                    for i in range(2):
                        last = nc.scalar.activation(xT[0:DH, a.u, i, :], ps_x[0:DH, i, 0:SLOTS], ACT.Identity,
                                                    scale=gb[:, 0, i:i + 1], bias=gb[:, 1, i:i + 1])
                    last.then_inc(xT_done, 1)
                if r is not None:
                    for n in range(2):
                        act.wait_ge(h_ps, r.b * 2 + (n + 1))
                        nc.scalar.activation(g[:, r.u, n * half:n * half + half], ps_h[:, n, 0:half], ACT.Gelu)\
                            .then_inc(g_done, 1)

            rows_deep(act, step, 3, tiles)

        @block.gpsimd
        def _(pool):
            nc.gpsimd.memset(xT[DH:DH + 1], 1.0).then_inc(ones_ready, 1)

        @block.vector
        def _(dve):
            dve.wait_ge(loaded, 16 * (2 + len(loads)))

            def step(a, r, b1):
                if b1 is not None:
                    for n in range(2):
                        dve.wait_ge(gT_ps, b1.b * 2 + (n + 1))
                        nc.vector.tensor_copy(gT[:, n * hc:n * hc + hc, :],
                                              ps_g[:, n, 0:hc * SLOTS].rearrange("p (i s) -> p i s", i=hc)).then_inc(gT_done, 1)
                    e = dve.value_load(keep["tile_expert"][0:1, bass.ds(b1.b, 1)], min_val=0, max_val=EXPERTS - 1)
                    dve.wait_ge(stored[b1.u], b1.k * 16 + 16)
                    dve.wait_ge(o_ps, b1.b + 1)
                    nc.vector.tensor_tensor(out[:, b1.u], ps_o[:, b1.u, 0:D], b2[:, bass.ds(e, 1), :].squeeze(1), ALU.add)\
                        .then_inc(out_done, 1)

            rows_deep(dve, step, 3, tiles)


def memory_pass(nc, io, keep):
    with ExitStack() as stack:
        c = Ctx(nc, stack, "mem_")
        wq = c.sb("wq", [DH, 2, MEM])
        wk = c.sb("wk", [DH, 2, MEM])
        wv = c.sb("wv", [DH, 2, MEM])
        wgate = c.sb("wgate", [DH, 2, MEM_HEADS])
        wout = c.sb("wout", [128, MEM // 128, D])
        wswitch = c.sb("wswitch", [DH + 1, 2, EXPERTS])
        decay = c.sb("decay", [128, 3 * TR])
        hx = c.sb("hx", [128, 2, 2, D])
        slots = c.sb("slots", [128, 2, 4], I32)
        weights = c.sb("weights", [128, 2, 4])
        gathered = c.sb("gathered", [128, 2, 4, D])
        h3 = c.sb("h3", [128, 2, D])
        xl = c.sb("xl", [128, 2, D])
        hs = c.sb("hs", [128, 2, 2, D])
        xT = c.sb("xT", [DH, 2, S])
        qT = c.sb("qT", [128, 2, MEM // 128, S])
        kT = c.sb("kT", [128, MEM // 128, S])
        vT = c.sb("vT", [128, MEM // 128, S])
        gate = c.sb("gate", [128, 2, MEM_HEADS])
        vo = c.sb("vo", [128, 2, MEM_HEADS, D])
        sT = c.sb("sT", [128, 4, 3 * TR])
        h4 = c.sb("h4", [128, 2, 2, D])
        x5 = c.sb("x5", [128, 2, 2, D])
        x5T = c.sb("x5T", [DH + 1, 2, S])
        logits = c.sb("logits", [128, 2, 2, EXPERTS])
        ln1, ln2 = NormTiles(c, "n1_"), NormTiles(c, "n2_")
        ps_x = c.ps("ps_x", [128, 2, 256])
        ps_q = c.ps("ps_q", [128, 2, 2, 256])
        ps_s = c.ps("ps_s", [128, 2, 512])
        ps_o = c.ps("ps_o", [128, 2, 512])
        ps_c = c.ps("ps_c", [128, 2, 256])
        loaded = c.sem("loaded")
        ones_ready = c.sem("ones_ready")
        passed = c.sem("passed")
        rows_in = [c.sem(f"rows_in{u}") for u in range(2)]
        outputs_in = [c.sem(f"outputs_in{u}") for u in range(2)]
        stored = [c.sem(f"stored{u}") for u in range(2)]
        h3_ready = c.sem("h3_ready")
        xl_ready = c.sem("xl_ready")
        xT_ps = c.sem("xT_ps")
        xT_ready = c.sem("xT_ready")
        q_ps = c.sem("q_ps")
        q_done = c.sem("q_done")
        m_ps = c.sem("m_ps")
        m_done = c.sem("m_done")
        gate_exp = c.sem("gate_exp")
        scores_ps = c.sem("scores_ps")
        s_done = c.sem("s_done")
        v_done = c.sem("v_done")
        h4_done = c.sem("h4_done")
        x5_ready = c.sem("x5_ready")
        x5T_ps = c.sem("x5T_ps")
        x5T_ready = c.sem("x5T_ready")
        logits_ps = c.sem("logits_ps")
        logits_done = c.sem("logits_done")
        chain_a = c.sem("chain_a")
        chain_c = c.sem("chain_c")
        block = stack.enter_context(nc.Block())
        PAIR = MEM // 128 // 2
        loads = ((wq, "wq_1"), (wk, "wk_1"), (wv, "wv_1"), (wgate, "wgate_1"), (wout, "wout_1"), (wswitch, "wswitch"),
                 (decay[0:TR], "decay"))

        def unit(r, h):
            return r.b * MEM_HEADS + h

        def lag(b1, b2, h, n):
            row, head = (b1, h - n) if h >= n else (b2, MEM_HEADS + h - n)
            return [(row, head)] if row is not None else []

        def is_first(r):
            return isinstance(r.b, int) and r.b == 0

        @block.sync
        def _(sp):
            for tile, name in loads:
                sp.dma_start(tile[:], io[name]).then_inc(loaded, 16)

            def step(a, r, b1, b2):
                if a is not None:
                    if not (isinstance(a.b, int) and a.b < 2):
                        sp.wait_ge(h3_ready, a.b - 1)
                        sp.sem_inc(passed, 1)
                    sp.dma_start(slots[0:TR, a.u], io["slots"][a.b]).then_inc(rows_in[a.u], 16)
                    sp.dma_start(weights[0:TR, a.u], io["weights"][a.b]).then_inc(rows_in[a.u], 16)
                    sp.dma_start(hx[0:TR, a.u], io["hx"][a.b]).then_inc(rows_in[a.u], 16)
                if b2 is not None:
                    sp.wait_ge(h4_done, b2.b + 3)
                    sp.sem_inc(passed, 1)
                    sp.dma_start(io["h4"][b2.b], h4[0:TR, b2.u]).then_inc(stored[b2.u], 16)
                    sp.wait_ge(x5_ready, b2.b + 2)
                    sp.sem_inc(passed, 1)
                    sp.dma_start(io["x5"][b2.b], x5[0:TR, b2.u]).then_inc(stored[b2.u], 16)
                    sp.wait_ge(logits_done, b2.b + 2)
                    sp.sem_inc(passed, 1)
                    sp.dma_start(io["logits"][b2.b], logits[0:TR, b2.u]).then_inc(stored[b2.u], 16)

            rows_deep(sp, step, 4)
            for u in range(2):
                sp.wait_ge(stored[u], 48 + 24 * B)

        @block.tensor
        def _(pe):
            pe.wait_ge(loaded, 16 * len(loads))
            pe.wait_ge(ones_ready, 1)
            ident = keep["ident"][0:TR, 0:TR]

            def project(ps, w, m):
                for half in range(2):
                    last = nc.tensor.matmul(ps, w[:, half, m * 128:m * 128 + 128], xT[:, half, :],
                                            start=(half == 0), stop=(half == 1))
                return last

            def remember():
                for n, w in enumerate((wk, wv)):
                    if n > 0:
                        pe.wait_ge(m_done, n)
                    for m in range(4):
                        last = project(ps_s[:, m // 2, m % 2 * 256:m % 2 * 256 + S], w, m)
                    last.then_inc(m_ps, 1)
                pe.wait_ge(m_done, 2)
                for t in range(2):
                    for half in range(2):
                        last = nc.tensor.matmul(ps_s[0:TR, 0, t * 256:t * 256 + MEM_HEADS], xT[:, half, t * TR:t * TR + TR],
                                                wgate[:, half, :], start=(half == 0), stop=(half == 1))
                last.then_inc(m_ps, 1)
                for n in range(MEM_HEADS):
                    j, m = n % 2, n // 2
                    pe.wait_ge(m_done, n + 3)
                    for i in range(2):
                        last = nc.tensor.matmul(ps_s[0:TR, i, n % 2 * 256:n % 2 * 256 + D],
                                                vT[i * 64:i * 64 + 64, m, j * TR:j * TR + TR],
                                                wout[i * 64:i * 64 + 64, m, :], start=True, stop=True)
                    last.then_inc(m_ps, 1)
                pe.wait_ge(m_done, MEM_HEADS + 3)

            def scores(r, h):
                if h == 0:
                    pe.wait_ge(q_done, r.b * 2 + 4)
                pe.wait_ge(s_done, unit(r, h) + 1)
                at, m = h % 2 * 64, h // 2
                nc.tensor.matmul(ps_s[0:TR, h % 2, 0:S], kT[at:at + 64, m, 0:TR], qT[at:at + 64, r.u, m, :],
                                 start=True, stop=True)
                nc.tensor.matmul(ps_s[0:TR, h % 2, S:S + TR], kT[at:at + 64, m, TR:S], qT[at:at + 64, r.u, m, TR:S],
                                 start=True, stop=True).then_inc(scores_ps, 1)

            def values(r, h):
                if h == 0:
                    pe.wait_ge(h4_done, r.b + 2)
                pe.wait_ge(s_done, unit(r, h) + 3)
                for i, (t, j) in enumerate(((0, 0), (1, 0), (1, 1))):
                    last = nc.tensor.matmul(ps_o[0:TR, t, 0:D], sT[0:TR, h % 4, i * TR:i * TR + TR],
                                            vo[0:TR, j, h, :], start=(h == 0 and j == 0),
                                            stop=(h == MEM_HEADS - 1 and j == t))
                last.then_inc(v_done, 1)

            def step(r, b1, b2):
                for h in range(MEM_HEADS):
                    if b1 is not None:
                        scores(b1, h)
                    for row, head in lag(b1, b2, h, 2):
                        values(row, head)
                    if r is not None and h == 3:
                        pe.wait_ge(xl_ready, r.b + 1)
                        turn_tokens(nc, ps_x, xl, ident).then_inc(xT_ps, 1)
                    if r is not None and h in (5, 6):
                        if h == 5:
                            pe.wait_ge(xT_ready, r.b + 1)
                            if is_first(r):
                                remember()
                        pe.wait_ge(q_done, r.b * 2 + (h - 4))
                        for m in range(2):
                            last = project(ps_q[:, h - 5, m, 0:S], wq, 2 * (h - 5) + m)
                        last.then_inc(q_ps, 1)
                    if b2 is not None and h == 6:
                        pe.wait_ge(logits_done, b2.b + 1)
                        pe.wait_ge(x5_ready, b2.b + 2)
                        turn_tokens(nc, ps_c, x5[:, b2.u], ident).then_inc(x5T_ps, 1)
                    if b2 is not None and h == 7:
                        pe.wait_ge(x5T_ready, b2.b + 1)
                        project_tokens(nc, ps_c, wswitch, x5T, EXPERTS).then_inc(logits_ps, 1)

            rows_deep(pe, step, 3)

        @block.scalar
        def _(act):
            act.sem_inc(xT_ps, 1)
            act.sem_inc(q_done, 2)
            act.sem_inc(s_done, 2)
            act.sem_inc(v_done, 4)
            act.sem_inc(h4_done, 2)
            act.sem_inc(x5_ready, 1)
            act.sem_inc(logits_done, 1)
            for u in range(2):
                act.sem_inc(stored[u], 48)

            def remember():
                for n, tile in enumerate((kT, vT)):
                    act.wait_ge(m_ps, n + 1)
                    for j in range(2):
                        last = nc.scalar.activation(tile[:, 2 * j:2 * j + 2, :],
                                                    ps_s[:, j, :].rearrange("p (m s) -> p m s", m=2)[:, :, 0:S], ACT.Copy)
                    last.then_inc(m_done, 1)
                act.wait_ge(m_ps, 3)
                nc.scalar.activation(gate[0:TR], ps_s[0:TR, 0, :].rearrange("p (t e) -> p t e", t=2)[:, :, 0:MEM_HEADS],
                                     ACT.Exp, scale=-1.0).then_inc(gate_exp, 1)

            def step(r, b1, b2):
                if r is not None:
                    act.wait_ge(xT_ps, r.b + 2)
                    nc.scalar.activation(xT[:], ps_x[0:DH, :, 0:S], ACT.Copy).then_inc(xT_ready, 1)
                    if is_first(r):
                        remember()
                    for j in range(2):
                        act.wait_ge(q_ps, r.b * 2 + (j + 1))
                        nc.scalar.activation(qT[:, r.u, 2 * j:2 * j + 2, :], ps_q[:, j, :, 0:S], ACT.Copy)\
                            .then_inc(q_done, 1)
                if b2 is not None:
                    act.wait_ge(x5T_ps, b2.b + 1)
                    nc.scalar.activation(x5T[0:DH], ps_c[0:DH, :, 0:S], ACT.Copy).then_inc(x5T_ready, 1)
                    act.wait_ge(stored[b2.u], b2.k * 48 + 48)
                    act.wait_ge(logits_ps, b2.b + 1)
                    nc.scalar.activation(logits[0:TR, b2.u], ps_c[0:TR, :, 0:EXPERTS], ACT.Copy).then_inc(logits_done, 1)

            rows_deep(act, step, 3)

        @block.gpsimd
        def _(pool):
            nc.gpsimd.memset(x5T[DH:DH + 1], 1.0).then_inc(ones_ready, 1)
            pool.wait_ge(ones_ready, 1)
            for ln in (ln1, ln2):
                nc.gpsimd.memset(ln.half[:], -0.5).then_inc(ln.half_ready, 1)
                pool.wait_ge(ln.half_ready, 1)

            def step(a, r, b1, b2):
                if a is not None:
                    if not (isinstance(a.b, int) and a.b < 2):
                        pool.wait_ge(h3_ready, a.b - 1)
                        pool.sem_inc(passed, 1)
                    pool.wait_ge(rows_in[a.u], a.k * 48 + 48)
                    pool.sem_inc(passed, 1)
                    for i in range(4):
                        nc.gpsimd.indirect_dma_start(gathered[0:TR, a.u, i, :], None, io["slot_out"],
                                                     bass.IndirectOffsetOnAxis(ap=slots[0:TR, a.u, i:i + 1], axis=0))\
                            .then_inc(outputs_in[a.u], 16)
                for row, ln in ((r, ln1), (b2, ln2)):
                    if row is not None:
                        inverse_root(nc, pool, ln, row.b)

            rows_deep(pool, step, 4)

        @block.vector
        def _(dve):
            cha, chc = Chain(dve, chain_a), Chain(dve, chain_c)
            a_count, c_count = 9, 4
            dve.wait_ge(loaded, 16 * len(loads))

            def remember():
                dve.wait_ge(gate_exp, 1)
                ch = Chain(dve, gate_exp)
                ch.start(1)
                ch.link(nc.vector.tensor_scalar(gate[0:TR], gate[0:TR], 1.0, None, ALU.add))
                ch.link(nc.vector.reciprocal(gate[0:TR], gate[0:TR]))
                nc.vector.tensor_scalar(gate[0:TR], gate[0:TR], 0.1, None, ALU.mult).then_inc(m_done, 1)
                dve.wait_ge(m_done, 3)
                for n in range(MEM_HEADS):
                    j, m = n % 2, n // 2
                    dve.wait_ge(m_ps, n + 4)
                    for i in range(2):
                        last = nc.vector.tensor_scalar(vo[0:TR, j, 2 * m + i, :],
                                                       ps_s[0:TR, i, n % 2 * 256:n % 2 * 256 + D],
                                                       gate[0:TR, j, 2 * m + i:2 * m + i + 1], None, ALU.mult)
                    last.then_inc(m_done, 1)

            def weigh(r, h):
                dve.wait_ge(scores_ps, unit(r, h) + 1)
                dve.wait_ge(v_done, unit(r, h) + 1)
                nc.vector.tensor_tensor(sT[0:TR, h % 4, :], ps_s[0:TR, h % 2, 0:3 * TR], decay[0:TR, :], ALU.mult)\
                    .then_inc(s_done, 1)

            def stage_a(r, h):
                if h == 0:
                    cha.start(r.b * a_count)
                    dve.wait_ge(rows_in[r.u], r.k * 48 + 48)
                    dve.wait_ge(outputs_in[r.u], r.k * 64 + 64)
                    if not is_first(r):
                        cha.sync()
                        dve.sem_inc(passed, 1)
                    for n in range(2):
                        for t in range(2):
                            ins = nc.vector.scalar_tensor_tensor(
                                h3[0:TR, t], gathered[0:TR, r.u, 2 * t + n], weights[0:TR, r.u, 2 * t + n:2 * t + n + 1],
                                (hx[0:TR, r.u, t] if n == 0 else h3[0:TR, t]), ALU.mult, ALU.add)
                            cha.of(ins)
                        cha.sync()
                        dve.sem_inc(passed, 1)
                    dve.sem_inc(h3_ready, 1)
                if h == 1:
                    norm_stats(nc, dve, cha, h3, ln1)
                if h == 2:
                    dve.wait_ge(xT_ps, r.b + 1)
                    norm_apply(nc, dve, h3, xl, ln1, r.b).then_inc(xl_ready, 1)
                if h == 3:
                    dve.wait_ge(xl_ready, r.b + 1)
                    dve.wait_ge(h4_done, r.b + 1)
                    cha.of(nc.vector.tensor_tensor(hs[0:TR, r.u], h3[0:TR], xl[0:TR], ALU.add))
                    assert cha.n == a_count
                    if is_first(r):
                        remember()

            def stage_c(r, h):
                if h == 2:
                    chc.start(r.b * c_count)
                    dve.wait_ge(v_done, unit(r, MEM_HEADS - 1) + 5)
                    dve.wait_ge(stored[r.u], r.k * 48 + 48)
                    nc.vector.tensor_tensor(h4[0:TR, r.u], ps_o[0:TR, :, 0:D], hs[0:TR, r.u], ALU.add)\
                        .then_inc(h4_done, 1)
                if h == 3:
                    dve.wait_ge(h4_done, r.b + 3)
                    dve.wait_ge(x5_ready, r.b + 1)
                    norm_stats(nc, dve, chc, h4[:, r.u], ln2)
                if h == 5:
                    norm_apply(nc, dve, h4[:, r.u], x5[:, r.u], ln2, r.b).then_inc(x5_ready, 1)
                    assert chc.n == c_count

            def step(r, b1, b2):
                for h in range(MEM_HEADS):
                    if b2 is not None:
                        stage_c(b2, h)
                    if b1 is not None:
                        weigh(b1, h)
                    if r is not None:
                        stage_a(r, h)

            rows_deep(dve, step, 3)


def route_one_pass(nc, io, keep):
    with ExitStack() as stack:
        c = Ctx(nc, stack, "route1_")
        logits = c.sb("logits", [128, NT, EXPERTS])
        probs = c.sb("probs", [128, NT, EXPERTS])
        work = c.sb("work", [128, NT, EXPERTS])
        hot = c.sb("hot", [128, NT, EXPERTS])
        mask = c.sb("mask", [128, NT, EXPERTS], BF16)
        ties = c.sb("ties", [128, NT, EXPERTS], BF16)
        best = c.sb("best", [128, NT])
        first = c.sb("first", [128, NT])
        kept = c.sb("kept", [128, NT])
        factors = c.sb("factors", [128, 2, NT])
        slot_f = c.sb("slot_f", [128, NT])
        slots = c.sb("slots", [128, NT], I32)
        base = c.sb("base", [128, EXPERTS])
        threshold = c.sb("threshold", [128, EXPERTS])
        candidate = c.sb("candidate", [128, EXPERTS])
        bit = c.sb("bit", [128, 1])
        reached = c.sb("reached", [128, EXPERTS])
        reached_b = c.sb("reached_b", [128, EXPERTS], BF16)
        above = c.sb("above", [128, EXPERTS])
        s = c.sb("s", [128, 16 + TILES2])
        rk, rk_ties = Ranks(c, ""), Ranks(c, "ties_")
        ps_count = c.ps("ps_count", [128, EXPERTS])
        loaded = c.sem("loaded")
        chain = c.sem("chain")
        shifted = c.sem("shifted")
        exp_ready = c.sem("exp_ready")
        reached_ready = c.sem("reached_ready")
        counted = c.sem("counted")
        steps = c.sem("steps")
        out_ready = c.sem("out_ready")
        stored = c.sem("stored")
        block = stack.enter_context(nc.Block())

        @block.sync
        def _(sp):
            sp.dma_start(logits[0:TR].rearrange("p (b t) e -> p b (t e)", t=2),
                         io["logits"].rearrange("b p t e -> p b (t e)")).then_inc(loaded, 16)
            sp.wait_ge(out_ready, 2)
            sp.dma_start(io["slots"].rearrange("b p c -> p b c")[:, :, 0:2],
                         slots[0:TR].rearrange("p (b t) -> p b t", t=2)).then_inc(stored, 16)
            for n in range(2):
                sp.dma_start(io["weights"].rearrange("b p c -> p b c")[:, :, 2 * n:2 * n + 2],
                             factors[0:TR, n].rearrange("p (b t) -> p b t", t=2)).then_inc(stored, 16)
            sp.wait_ge(stored, 48)

        @block.tensor
        def _(pe):
            rk.products(nc, pe, keep, mask[0:TR], 0)

            def count(n):
                pe.wait_ge(reached_ready, n + 1)
                nc.tensor.matmul(ps_count[0:TR], keep["onesb"][0:TR, 0:TR], reached_b[0:TR], start=True, stop=True)\
                    .then_inc(counted, 1)

            with pe.Fori(0, BITS) as j:
                count(j)
            count(BITS)
            rk_ties.products(nc, pe, keep, ties[0:TR], 0)

        @block.scalar
        def _(act):
            act.wait_ge(shifted, 1)
            nc.scalar.activation(probs[0:TR], work[0:TR], ACT.Exp).then_inc(exp_ready, 1)

        @block.vector
        def _(dve):
            ch = Chain(dve, chain)
            dve.wait_ge(loaded, 16)
            ch.link(nc.vector.tensor_reduce(best[0:TR], logits[0:TR], AX.X, ALU.max))
            nc.vector.tensor_tensor(work[0:TR], logits[0:TR], by_token(best[0:TR]), ALU.subtract).then_inc(shifted, 1)
            dve.wait_ge(exp_ready, 1)
            ch.link(nc.vector.tensor_reduce(first[0:TR], probs[0:TR], AX.X, ALU.add))
            ch.link(nc.vector.reciprocal(first[0:TR], first[0:TR]))
            ch.link(nc.vector.tensor_tensor(probs[0:TR], probs[0:TR], by_token(first[0:TR]), ALU.mult))
            ch.link(nc.vector.tensor_reduce(best[0:TR], probs[0:TR], AX.X, ALU.max))
            one_hot_first(nc, ch, keep, probs[0:TR], best[0:TR], work[0:TR], first[0:TR], hot[0:TR])
            nc.vector.tensor_copy(mask[0:TR], hot[0:TR]).then_inc(rk.mask_ready, 1)
            ch.link(nc.vector.tensor_tensor(probs[0:TR], hot[0:TR], by_token(best[0:TR]), ALU.mult))
            ch.link(nc.vector.memset(threshold[:], 0.0))
            ch.link(nc.vector.memset(bit[:], 1.0))

            def reach(bound, op, n, steps_):
                steps_.link(nc.vector.tensor_tensor(work[0:TR], probs[0:TR], by_expert(bound), op))
                steps_.link(nc.vector.tensor_reduce(reached[0:TR], work[0:TR].rearrange("p n e -> p e n"), AX.X, ALU.add))
                nc.vector.tensor_copy(reached_b[0:TR], reached[0:TR]).then_inc(reached_ready, 1)
                dve.wait_ge(counted, n + 1)

            with dve.Fori(0, BITS) as j:
                sc = Chain(dve, steps)
                sc.start(j * 6)
                sc.link(nc.vector.tensor_tensor(candidate[0:TR], threshold[0:TR], bit[0:TR].to_broadcast([TR, EXPERTS]),
                                                ALU.add))
                reach(candidate[0:TR], ALU.is_ge, j, sc)
                sc.link(nc.vector.scalar_tensor_tensor(candidate[0:TR], ps_count[0:TR], float(CAPACITY), candidate[0:TR],
                                                       ALU.is_ge, ALU.mult))
                sc.link(nc.vector.tensor_tensor(threshold[0:TR], threshold[0:TR], candidate[0:TR], ALU.max))
                sc.link(nc.vector.tensor_scalar(bit[0:TR], bit[0:TR], 0.5, None, ALU.mult))
            sc = Chain(dve, steps)
            sc.start(BITS * 6)
            reach(threshold[0:TR], ALU.is_gt, BITS, sc)
            ch.link(nc.vector.tensor_copy(above[0:TR], ps_count[0:TR]))
            ch.link(nc.vector.tensor_tensor(logits[0:TR], probs[0:TR], by_expert(threshold[0:TR]), ALU.is_equal))
            nc.vector.tensor_tensor(ties[0:TR], logits[0:TR], hot[0:TR], ALU.mult).then_inc(rk_ties.mask_ready, 1)
            rk_ties.finish(nc, dve, ch, 0)
            ch.link(nc.vector.tensor_tensor(logits[0:TR], rk_ties.rank[0:TR], by_expert(above[0:TR]), ALU.add))
            ch.link(nc.vector.scalar_tensor_tensor(logits[0:TR], logits[0:TR], float(CAPACITY), ties[0:TR],
                                                   ALU.is_lt, ALU.mult))
            ch.link(nc.vector.tensor_tensor(work[0:TR], work[0:TR], logits[0:TR], ALU.add))
            ch.link(nc.vector.tensor_reduce(kept[0:TR], work[0:TR], AX.X, ALU.add))
            ch.link(nc.vector.tensor_tensor(factors[0:TR, 0], best[0:TR], kept[0:TR], ALU.mult))
            nc.vector.tensor_tensor(factors[0:TR, 1], best[0:TR], factors[0:TR, 0], ALU.subtract).then_inc(out_ready, 1)
            rk.finish(nc, dve, ch, 0)
            place_slots(nc, ch, keep, rk, base, keep["tile_expert"], keep["tile_start"][:, 0:TILES1], s)
            ch.link(nc.vector.tensor_tensor(work[0:TR], hot[0:TR], rk.rank[0:TR], ALU.mult))
            ch.link(nc.vector.tensor_reduce(slot_f[0:TR], work[0:TR], AX.X, ALU.add))
            nc.vector.tensor_copy(slots[0:TR], slot_f[0:TR]).then_inc(out_ready, 1)


def output_pass(nc, io):
    with ExitStack() as stack:
        c = Ctx(nc, stack, "out_")
        h4 = c.sb("h4", [128, 2, 2, D])
        x5 = c.sb("x5", [128, 2, 2, D])
        factors = c.sb("factors", [128, 2, 4])
        slots = c.sb("slots", [128, 2, 2], I32)
        gathered = c.sb("gathered", [128, 2, 2, D])
        part = c.sb("part", [128, 2, 2, D])
        out = c.sb("out", [128, 2, 2, D])
        slots_in = [c.sem(f"slots_in{u}") for u in range(2)]
        rows_in = [c.sem(f"rows_in{u}") for u in range(2)]
        outputs_in = [c.sem(f"outputs_in{u}") for u in range(2)]
        stored = [c.sem(f"stored{u}") for u in range(2)]
        passed = c.sem("passed")
        part_ready = c.sem("part_ready")
        out_ready = c.sem("out_ready")
        block = stack.enter_context(nc.Block())

        @block.sync
        def _(sp):
            def load(r):
                if not r.first:
                    sp.wait_ge(out_ready, r.b - 1)
                    sp.sem_inc(passed, 1)
                sp.dma_start(slots[0:TR, r.u], io["slots"][r.b][:, 0:2]).then_inc(slots_in[r.u], 16)
                sp.dma_start(factors[0:TR, r.u], io["weights"][r.b]).then_inc(rows_in[r.u], 16)
                sp.dma_start(h4[0:TR, r.u], io["h4"][r.b]).then_inc(rows_in[r.u], 16)
                sp.dma_start(x5[0:TR, r.u], io["x5"][r.b]).then_inc(rows_in[r.u], 16)

            def store(r):
                sp.wait_ge(out_ready, r.b + 1)
                sp.sem_inc(passed, 1)
                sp.dma_start(io["out"][r.b].rearrange("(t p) d -> p t d", t=2), out[0:TR, r.u]).then_inc(stored[r.u], 16)

            load_store_rows(sp, load, store)
            for u in range(2):
                sp.wait_ge(stored[u], 16 + 8 * B)

        @block.gpsimd
        def _(pool):
            def fetch(r):
                pool.wait_ge(slots_in[r.u], r.k * 16 + 16)
                pool.sem_inc(passed, 1)
                for t in range(2):
                    nc.gpsimd.indirect_dma_start(gathered[0:TR, r.u, t, :], None, io["slot_out"],
                                                 bass.IndirectOffsetOnAxis(ap=slots[0:TR, r.u, t:t + 1], axis=0))\
                        .then_inc(outputs_in[r.u], 16)

            rows(pool, fetch)

        @block.vector
        def _(dve):
            for u in range(2):
                dve.sem_inc(stored[u], 16)

            def combine(r):
                dve.wait_ge(rows_in[r.u], r.k * 48 + 48)
                for t in range(2):
                    last = nc.vector.scalar_tensor_tensor(part[0:TR, r.u, t], x5[0:TR, r.u, t], factors[0:TR, r.u, 2 + t:3 + t],
                                                          h4[0:TR, r.u, t], ALU.mult, ALU.add)
                last.then_inc(part_ready, 1)
                dve.wait_ge(part_ready, r.b + 1)
                dve.sem_inc(passed, 1)
                dve.wait_ge(stored[r.u], r.k * 16 + 16)
                dve.wait_ge(outputs_in[r.u], r.k * 32 + 32)
                for t in range(2):
                    last = nc.vector.scalar_tensor_tensor(out[0:TR, r.u, t], gathered[0:TR, r.u, t], factors[0:TR, r.u, t:t + 1],
                                                          part[0:TR, r.u, t], ALU.mult, ALU.add)
                last.then_inc(out_ready, 1)

            rows(dve, combine)


def scratch(nc, name, shape, dt=F32):
    return nc.dram_tensor(name, shape, dt, kind="Internal").ap()


def audio_tower(nc, io):
    for name, shape, dt in (
        ("h1", [B, TR, 2, D], F32), ("xnT", [B, DH, 2, S], F32),
        ("qk", [B, 128, 2 * GROUPS, S], BF16), ("v", [B, TR, 2, D], BF16), ("row_max", [B, TR, 2 * HEADS], F32),
        ("o", [B, TR, 2, D], F32), ("y", [B, TR, 2, D], F32),
        ("hxl", [B, TR, 2, 2, D], F32), ("hx", [B, TR, 2, D], F32), ("zn", [B, TR, 2, D], F32),
        ("logits", [B, TR, 2, EXPERTS], F32),
        ("h4", [B, TR, 2, D], F32), ("x5", [B, TR, 2, D], F32),
        ("slots", [B, TR, 4], I32), ("weights", [B, TR, 4], F32),
        ("slotted", [TILES2 * SLOTS, D], F32), ("slot_out", [TILES2 * SLOTS, D], F32),
    ):
        if name not in io:
            io[name] = scratch(nc, name, shape, dt)
    with ExitStack() as stack:
        c = Ctx(nc, stack, "kept_")
        keep = {
            "ident": c.sb("ident", [128, 128]),
            "identb": c.sb("identb", [128, 128], BF16),
            "padmask": c.sb("padmask", [128, 1]),
            "magic": c.sb("magic", [128, 1]),
            "tri": c.sb("tri", [128, 128], BF16),
            "onesb": c.sb("onesb", [128, 128], BF16),
            "falling": c.sb("falling", [128, EXPERTS]),
            "tile_start": c.sb("tile_start", [1, TILES2]),
            "tile_expert": c.sb("tile_expert", [1, TILES2], I32),
            "par": c.sb("par", [128, 128]),
            "wqkv": c.sb("wqkv", [DH + 1, 2, QKV]),
            "wp": c.sb("wp", [DH, 2, D], BF16),
            "wp_scale": c.sb("wp_scale", [128, D]),
        }
        setup_pass(nc, io, keep)
        token_pass(nc, io, keep)
        quantise_pass(nc, io, keep)
        integer_softmax_pass(nc, io, keep)
        project_out_pass(nc, io, keep)
        softmax_attention_pass(nc, io, keep)
        route_two_pass(nc, io, keep)
        scatter_pass(nc, io, "zn", 2)
        experts_pass(nc, io, keep, TILES2, 0)
        memory_pass(nc, io, keep)
        route_one_pass(nc, io, keep)
        scatter_pass(nc, io, "x5", 1)
        experts_pass(nc, io, keep, TILES1, 1)
        output_pass(nc, io)


def halves(w, bias=None):
    out = np.zeros((DH + 1, 2, w.shape[1]), np.float32)
    out[0:DH, 0], out[0:DH, 1] = w[0:DH], w[DH:D]
    if bias is not None:
        out[DH, 1] = bias
    return out


def padded_heads(w):
    out = np.zeros((*w.shape[:-1], HEADS, HPB), np.float32)
    out[..., 0:HD] = w.reshape(*w.shape[:-1], HEADS, HD)
    return out.reshape(*w.shape[:-1], HEADS * HPB)


def by_heads(w):
    return np.concatenate([padded_heads(w[..., 0:D]), padded_heads(w[..., D:2 * D]), w[..., 2 * D:]], axis=-1)


def experts_layout(x, prefix, names, layer):
    w1, b1, w2, b2 = (x[prefix + n] for n in names)
    return {
        f"w1_{layer}": np.stack([halves(w1[e], b1[e]) for e in range(EXPERTS)]),
        f"w2_{layer}": w2.reshape(EXPERTS, HC, 128, D).transpose(0, 2, 1, 3),
        f"b2_{layer}": b2,
    }


def constants():
    t = np.arange(FRAME)
    window = 0.54 - 0.46 * np.cos(2.0 * np.pi * t / (FRAME - 1))
    angle = 2.0 * np.pi * np.outer(t, np.arange(BINS)) / FRAME
    dft = np.concatenate([np.cos(angle), -np.sin(angle)], axis=1) * window[:, None]
    ago = np.arange(S)[None, :] - 1 - np.arange(TR)[:, None]
    decay = np.where(ago >= 0, float(np.float32(DECAY)) ** np.maximum(ago, 0), 0.0)
    decay = np.concatenate([decay, decay[:, 0:TR]], axis=1)
    padmask = np.where(np.arange(128) % HPB < HD, 0.0, BIG)[:, None]
    return {
        "dft": dft.astype(np.float32),
        "ident": np.eye(128, dtype=np.float32),
        "padmask": padmask.astype(np.float32),
        "tri": np.triu(np.ones((128, 128), np.float32), 1),
        "falling": np.tile(np.arange(EXPERTS, 0, -1, dtype=np.float32), (128, 1)),
        "decay": decay.astype(np.float32),
        "tile_start": np.arange(TILES2, dtype=np.float32)[None] * SLOTS,
    }


def layouts(x):
    x = {k: np.asarray(v) for k, v in x.items()}
    mel = x["L0_tok_mel_filters"].T
    out = {
        "x": x["x"],
        "mel": np.concatenate([mel, mel], axis=0),
        "dct": x["L0_tok_dct"].T,
        "wtok": np.concatenate([x["L0_tok_w_proj"], x["L0_tok_b_proj"][None]], axis=0),
        "wqkv": halves(by_heads(x["L0_attn_w_qkv"].T), by_heads(x["L0_attn_b_qkv"])),
        "bproj_q": x["L0_attn_b_proj"],
        "wproj_q": halves(x["L0_attn_w_proj"].T)[0:DH],
    }
    gains = np.stack([np.stack([x[f"L0_ffn_ln{n}_{p}"].reshape(2, DH).T for p in "gb"], axis=1) for n in (1, 2)], axis=1)
    out.update({
        "gains": gains,
        "wqkv_f": halves(by_heads(x["L0_ffn_qkv_w"])),
        "wproj_f": halves(x["L0_ffn_proj_w"], x["L0_ffn_proj_b"]),
        "wgate": halves(x["L0_ffn_gate_w"], x["L0_ffn_gate_b"]),
    })
    out.update(experts_layout(x, "L0_ffn_", "w1 b1 w2 b2".split(), 0))
    out.update(experts_layout(x, "L1_ffn_", "w1 b1 w2 b2".split(), 1))
    out["gb_1"] = np.stack([np.ones((DH, 2)), np.zeros((DH, 2))], axis=1).astype(np.float32)
    out.update({
        "wq_1": halves(x["L1_attn_w_query"].T)[0:DH],
        "wk_1": halves(x["L1_attn_w_key"].T)[0:DH],
        "wv_1": halves(x["L1_attn_w_value"].T)[0:DH],
        "wgate_1": halves(x["L1_attn_w_gate"].T)[0:DH],
        "wout_1": x["L1_attn_w_out"].T.reshape(MEM // 128, 128, D).transpose(1, 0, 2),
        "wswitch": halves(x["L1_ffn_switch_w"], x["L1_ffn_switch_b"]),
    })
    out["gb_0"] = np.ascontiguousarray(gains[:, 1])
    out.update(constants())
    return {k: np.ascontiguousarray(v) for k, v in out.items()}


def kernel(**inputs):
    import concourse.bacc as bacc
    from concourse.bass_utils import run_bass_kernel_spmd

    nc = bacc.Bacc("TRN2", target_bir_lowering=False, num_devices=1)
    arrays = layouts(inputs)
    io = {n: nc.dram_tensor(f"in_{n}", a.shape, mybir.dt.from_np(a.dtype), kind="ExternalInput").ap()
          for n, a in arrays.items()}
    io["out"] = nc.dram_tensor("out", (B, S, D), F32, kind="ExternalOutput").ap()
    audio_tower(nc, io)
    result = run_bass_kernel_spmd(nc, [{f"in_{n}": a for n, a in arrays.items()}], core_ids=[0])
    return result.results[0]["out"]
```

```python
from contextlib import ExitStack
from itertools import zip_longest

import numpy as np

import concourse.bass as bass
from concourse import mybir

F32 = mybir.dt.float32
BF16 = mybir.dt.bfloat16
I32 = mybir.dt.int32
I16 = mybir.dt.int16
ALU = mybir.AluOpType
ACT = mybir.ActivationFunctionType
AX = mybir.AxisListType
RMAX = bass.bass_isa.ReduceOp.max

B, AUDIO, HOP, FRAME = 32, 40000, 160, 100
S = 1 + (AUDIO - FRAME) // HOP
TR = S // 2
N = B * S
NT = N // TR
BINS = FRAME // 2 + 1
FILTERS, MFCC = 40, 13
D = 192
DH = D // 2
HEADS, HD = 12, 16
GROUPS = HEADS // 4
HPB = 32
PAIRS = HEADS // 2
QK = 2 * GROUPS * 128
QKV = QK + D
EXPERTS = 8
HIDDEN = 768
HC = HIDDEN // 128
SLOTS = 128
TILES2 = (2 * N + EXPERTS * (SLOTS - 1)) // SLOTS
TILES1 = (N + EXPERTS * (SLOTS - 1)) // SLOTS
FILLS = 12
CAPACITY = int(1.25 * N / EXPERTS)
EPS = 1e-5
MAGIC = 1.5 * 2.0**23
BIG = 3.0e38
BITS = 28
MEM_HEADS, MEM = 8, 512
DECAY = 0.95
PARTS_Q, PARTS_K = (0, 0, 0, 1, 1, 2), (0, 1, 2, 0, 1, 0)
STACK = len(PARTS_Q) * HD
COEF_A, COEF_B, COEF_C = 0.35815147, 0.96963238, 1.0
LN2 = 0.6931471805599453
N_EXP = 30


class Ctx:

    def __init__(self, nc, ctx, prefix):
        self.nc, self.ctx, self.prefix = nc, ctx, prefix
        self.sems = []
        ctx.callback(self.clear)

    def clear(self):
        with self.nc.Block() as block:
            @block.sync
            def _(sp):
                for sem in self.sems:
                    sp.sem_clear(sem)

    def sb(self, name, shape, dt=F32):
        return self.ctx.enter_context(self.nc.sbuf_tensor(self.prefix + name, shape, dt))

    def ps(self, name, shape, dt=F32):
        return self.ctx.enter_context(self.nc.psum_tensor(self.prefix + name, shape, dt))

    def sem(self, name):
        self.sems.append(self.ctx.enter_context(self.nc.semaphore(self.prefix + name)))
        return self.sems[-1]


class Chain:

    def __init__(self, eng, sem):
        self.eng, self.sem, self.n, self.base = eng, sem, 0, 0

    def start(self, base):
        self.base, self.n = base, 0

    def of(self, ins):
        self.n += 1
        ins.then_inc(self.sem, 1)
        return ins

    def sync(self):
        self.eng.wait_ge(self.sem, self.base + self.n)

    def link(self, ins):
        self.of(ins)
        self.sync()


class Row:

    def __init__(self, b, u, k, first=False):
        self.b, self.u, self.k, self.first = b, u, k, first


def rows(eng, body):
    with eng.Fori(0, B // 2) as i:
        for u in range(2):
            body(Row(i * 2 + u, u, i))


def rows_skewed(eng, first, step, last):
    first(Row(0, 0, 0))
    with eng.Fori(0, B // 2 - 1) as i:
        step(Row(i * 2 + 1, 1, i), Row(i * 2, 0, i))
        step(Row(i * 2 + 2, 0, i + 1), Row(i * 2 + 1, 1, i))
    end = Row(B - 1, 1, B // 2 - 1)
    step(end, Row(B - 2, 0, B // 2 - 1))
    last(end)


def load_store_rows(sp, load, store):
    load(Row(0, 0, 0, first=True))
    load(Row(1, 1, 0, first=True))
    with sp.Fori(0, B // 2 - 1) as i:
        for u in range(2):
            load(Row(i * 2 + (u + 2), u, i + 1))
            store(Row(i * 2 + u, u, i))
    store(Row(B - 2, 0, B // 2 - 1))
    store(Row(B - 1, 1, B // 2 - 1))


def rows_deep(eng, step, depth, n=B):
    start = depth // 2 * 2

    def at(a):
        return Row(a, a % 2, a // 2) if 0 <= a < n else None

    for a in range(start):
        step(*[at(a - j) for j in range(depth)])
    with eng.Fori(0, (n - start) // 2) as i:
        for u in range(2):
            step(*[Row(i * 2 + (start + u - j), (u - j) % 2, i + (start + u - j) // 2) for j in range(depth)])
    for a in range(n, n + depth - 1):
        step(*[at(a - j) for j in range(depth)])


class NormTiles:

    def __init__(self, c, name=""):
        self.st = c.sb(name + "st", [128, 2, 6])
        self.mv = c.sb(name + "mv", [128, 2, 2])
        self.ve = c.sb(name + "ve", [128, 2])
        self.half = c.sb(name + "half", [128, 2])
        self.rstd = c.sb(name + "rstd", [128, 2])
        self.half_ready = c.sem(name + "half_ready")
        self.ve_ready = c.sem(name + "ve_ready")
        self.passed = c.sem(name + "ln_passed")
        self.rstd_ready = c.sem(name + "rstd_ready")


def inverse_root(nc, pool, ln, n):
    pool.wait_ge(ln.ve_ready, n + 1)
    nc.gpsimd.tensor_tensor(ln.rstd[0:TR, :], ln.ve[0:TR, :], ln.half[0:TR, :], ALU.pow).then_inc(ln.rstd_ready, 1)


def norm_stats(nc, dve, ch, src, ln):
    for t in range(2):
        ch.of(nc.vector.bn_stats(ln.st[0:TR, t, :], src[0:TR, t, :]))
    ch.sync()
    dve.sem_inc(ln.passed, 1)
    for t in range(2):
        ch.of(nc.vector.bn_aggr(ln.mv[0:TR, t, :], ln.st[0:TR, t, :]))
    ch.sync()
    nc.vector.tensor_scalar(ln.ve[0:TR, :], ln.mv[0:TR, :, 1], EPS, None, ALU.add).then_inc(ln.ve_ready, 1)


def norm_apply(nc, dve, src, dst, ln, n):
    dve.wait_ge(ln.rstd_ready, n + 1)
    for t in range(2):
        last = nc.vector.tensor_scalar(dst[0:TR, t, :], src[0:TR, t, :], ln.mv[0:TR, t, 0:1], ln.rstd[0:TR, t:t + 1],
                                       ALU.subtract, ALU.mult)
    return last


PAR = {n: i for i, n in enumerate(
    "inv1 top1 ratio_q ratio_k ratio_v top_q top_k top_v s_q s_k s_v "
    "c_a a_top n_inv n_bias n_step n_least b_half c_rest "
    "o_inv o_top o_scale y_inv y_top y_scale".split())}


def par(keep, name, p=128):
    i = PAR[name]
    return keep["par"][0:p, i:i + 1]


class Scalars:

    def __init__(self, nc, ch, tile, first):
        self.nc, self.ch, self.tile, self.at = nc, ch, tile, first

    def new(self, w=1):
        self.at += w
        assert self.at <= self.tile.shape[1]
        return self.tile[:, self.at - w:self.at]

    def ts(self, x, s1, op0, s2=None, op1=None, out=None):
        out = self.new(x.shape[1]) if out is None else out
        self.ch.link(self.nc.vector.tensor_scalar(out, x, s1, s2, op0, *([op1] if op1 is not None else [])))
        return out

    def tt(self, x, y, op, out=None):
        out = self.new(x.shape[1]) if out is None else out
        self.ch.link(self.nc.vector.tensor_tensor(out, x, y, op))
        return out

    def inverse(self, x, out=None):
        out = self.new(x.shape[1]) if out is None else out
        self.ch.link(self.nc.vector.reciprocal(out, x))
        return out

    def round(self, x):
        return self.ts(x, MAGIC, ALU.add, MAGIC, ALU.subtract)

    def floor(self, x):
        near = self.ts(x, 2.0**23, ALU.add, 2.0**23, ALU.subtract)
        return self.tt(near, self.tt(near, x, ALU.is_gt), ALU.subtract)

    def scale(self, top, minus_least):
        return self.ts(self.tt(top, minus_least, ALU.add), 1.0 / 255.0, ALU.mult, 1e-8, ALU.max)


def quantisers_qkv(nc, dve, ch, tile, extrema):
    s = Scalars(nc, ch, tile, len(PAR))
    col = lambda n: tile[:, PAR[n]:PAR[n] + 1]
    cols = lambda n: tile[:, PAR[n]:PAR[n] + 3]
    top, low = extrema[:, 0:3], extrema[:, 3:6]
    both = [s.tt(s.tt(e[:, 0:1], e[:, 1:2], ALU.max), e[:, 2:3], ALU.max) for e in (top, low)]
    s1 = s.scale(*both)
    inv1 = s.inverse(s1, out=col("inv1"))
    zero1 = s.round(s.tt(both[1], inv1, ALU.mult))
    most1 = s.ts(zero1, -1.0, ALU.mult, 255.0, ALU.add)
    s.ts(most1, MAGIC, ALU.add, out=col("top1"))
    q_top = s.ts(s.round(s.ts(top, inv1, ALU.mult)), most1, ALU.min, s1, ALU.mult)
    q_low = s.ts(s.round(s.ts(low, inv1, ALU.mult)), s1, ALU.mult)
    s2 = s.ts(s.scale(q_top, q_low), 1.0, ALU.mult, out=cols("s_q"))
    inv2 = s.inverse(s2)
    s.ts(inv2, s1, ALU.mult, out=cols("ratio_q"))
    zero2 = s.round(s.tt(q_low, inv2, ALU.mult))
    s.ts(s.ts(zero2, -1.0, ALU.mult, 255.0, ALU.add), MAGIC, ALU.add, out=cols("top_q"))


def quantiser_scores(nc, dve, ch, tile, extrema):
    s = Scalars(nc, ch, tile, len(PAR))
    col = lambda n: tile[:, PAR[n]:PAR[n] + 1]
    unit = s.ts(s.tt(col("s_q"), col("s_k"), ALU.mult), HD**-0.5, ALU.mult)
    top, low = (s.tt(extrema[:, i:i + 1], unit, ALU.mult) for i in range(2))
    inv = s.inverse(s.scale(top, low))
    s.tt(unit, inv, ALU.mult, out=col("c_a"))
    zero = s.round(s.tt(low, inv, ALU.mult))
    s.ts(s.ts(zero, -1.0, ALU.mult, 255.0, ALU.add), MAGIC, ALU.add, out=col("a_top"))
    steps = s.ts(inv, LN2, ALU.mult)
    near = s.ts(steps, 2.0**23, ALU.add, 2.0**23, ALU.subtract)
    up = s.tt(near, s.tt(near, steps, ALU.is_lt), ALU.add)
    n = s.ts(up, 512.0, ALU.min, out=col("n_step"))
    s.ts(n, -float(N_EXP), ALU.mult, out=col("n_least"))
    n_inv = s.inverse(n)
    s.ts(n_inv, -1.0, ALU.mult, out=col("n_inv"))
    s.ts(n_inv, 0.5, ALU.mult, -0.5, ALU.add, out=col("n_bias"))
    b_int = s.floor(s.ts(inv, COEF_B / COEF_A, ALU.mult))
    c_int = s.floor(s.ts(s.tt(inv, inv, ALU.mult), COEF_C / COEF_A, ALU.mult))
    b_half = s.ts(b_int, 0.5, ALU.mult, out=col("b_half"))
    s.tt(c_int, s.tt(b_half, b_half, ALU.mult), ALU.subtract, out=col("c_rest"))


def quantiser_out(nc, dve, ch, tile, extrema, name):
    s = Scalars(nc, ch, tile, len(PAR))
    col = lambda n: tile[:, PAR[n]:PAR[n] + 1]
    scale = s.ts(s.scale(extrema[:, 0:1], extrema[:, 1:2]), 1.0, ALU.mult, out=col(name + "_scale"))
    inv = s.inverse(scale, out=col(name + "_inv"))
    zero = s.round(s.tt(extrema[:, 1:2], inv, ALU.mult))
    s.ts(s.ts(zero, -1.0, ALU.mult, 255.0, ALU.add), MAGIC, ALU.add, out=col(name + "_top"))


def turn_tokens(nc, ps, x, ident):
    for half in range(2):
        for t in range(2):
            last = nc.tensor.transpose(ps[0:DH, half, t * TR:t * TR + TR], x[0:TR, t, half * DH:half * DH + DH], ident)
    return last


def project_tokens(nc, ps, w, xT, width):
    for t in range(2):
        nc.tensor.matmul(ps[0:TR, t, 0:width], xT[0:DH, 0, t * TR:t * TR + TR], w[0:DH, 0, 0:width],
                         start=True, stop=False)
        last = nc.tensor.matmul(ps[0:TR, t, 0:width], xT[:, 1, t * TR:t * TR + TR], w[:, 1, 0:width],
                                start=False, stop=True)
    return last


def project_heads(nc, ps, w, xT, slot, m):
    nc.tensor.matmul(ps[:, slot, 0:S], w[0:DH, 0, m * 128:m * 128 + 128], xT[0:DH, 0, :], start=True, stop=False)
    return nc.tensor.matmul(ps[:, slot, 0:S], w[0:DH + 1, 1, m * 128:m * 128 + 128], xT[:, 1, :], start=False, stop=True)


def project_values(nc, ps, w, xT):
    for t in range(2):
        nc.tensor.matmul(ps[0:TR, t, 0:D], xT[0:DH, 0, t * TR:t * TR + TR], w[0:DH, 0, QK:QKV], start=True, stop=False)
        last = nc.tensor.matmul(ps[0:TR, t, 0:D], xT[:, 1, t * TR:t * TR + TR], w[0:DH + 1, 1, QK:QKV],
                                start=False, stop=True)
    return last


def setup_pass(nc, io, keep):
    with ExitStack() as stack:
        c = Ctx(nc, stack, "setup_")
        amax = c.sb("amax", [128, 2, QKV])
        scale = c.sb("scale", [128, QKV])
        inv = c.sb("inv", [128, QKV])
        q = c.sb("q", [128, 2, QKV])
        wp = c.sb("wp", [128, 2, D])
        loaded = c.sem("loaded")
        cleared = c.sem("cleared")
        reduced = c.sem("reduced")
        steps = c.sem("steps")
        block = stack.enter_context(nc.Block())
        names = ["ident", "padmask", "falling", "tile_start"]
        tri = c.sb("tri", [128, 128])

        @block.sync
        def _(sp):
            for n in names:
                sp.dma_start(keep[n][:], io[n]).then_inc(loaded, 16)
            sp.dma_start(keep["wqkv"][:], io["wqkv"]).then_inc(loaded, 16)
            sp.dma_start(tri[:], io["tri"]).then_inc(loaded, 16)
            sp.wait_ge(cleared, 1)
            sp.dma_start(wp[0:DH], io["wproj_q"]).then_inc(loaded, 16)

        @block.gpsimd
        def _(pool):
            pool.wait_ge(loaded, 16 * (len(names) + 3))
            nc.gpsimd.partition_all_reduce(amax[0:DH].rearrange("p a n -> p (a n)"),
                                           keep["wqkv"][0:DH].rearrange("p a n -> p (a n)"), DH,
                                           bass.bass_isa.ReduceOp.absmax).then_inc(reduced, 1)
            pool.wait_ge(steps, 6)
            nc.gpsimd.partition_all_reduce(amax[:, :, 0:D], wp[:, :, :], 128,
                                           bass.bass_isa.ReduceOp.absmax).then_inc(reduced, 1)

        @block.vector
        def _(dve):
            nc.vector.memset(wp[:], 0.0).then_inc(cleared, 1)
            nc.vector.memset(keep["magic"][:], MAGIC)
            nc.vector.memset(keep["onesb"][:], 1.0)
            ch = Chain(dve, steps)

            def quantise(w, a, sc, iv, qq):
                ch.link(nc.vector.tensor_tensor(sc, a[:, 0, :], a[:, 1, :], ALU.max))
                ch.link(nc.vector.tensor_scalar(sc, sc, 1.0 / 127.0, 1e-8, ALU.mult, ALU.max))
                ch.link(nc.vector.reciprocal(iv, sc))
                for h in range(2):
                    ch.link(nc.vector.tensor_tensor(qq[:, h, :], w[:, h, :], iv, ALU.mult))
                ch.link(nc.vector.tensor_scalar(qq, qq, MAGIC, MAGIC, ALU.add, ALU.subtract))

            dve.wait_ge(reduced, 1)
            quantise(keep["wqkv"][0:DH], amax[0:DH], scale[0:DH, :], inv[0:DH, :], q[0:DH])
            ch.link(nc.vector.tensor_scalar(q[0:DH], q[0:DH], 127.0, -128.0, ALU.min, ALU.max))
            for h in range(2):
                ch.link(nc.vector.tensor_tensor(keep["wqkv"][0:DH, h, :], q[0:DH, h, :], scale[0:DH, :], ALU.mult))
            dve.wait_ge(reduced, 2)
            quantise(wp, amax[:, :, 0:D], keep["wp_scale"][:], inv[:, 0:D], q[:, :, 0:D])
            ch.link(nc.vector.tensor_scalar(keep["wp"][:], q[0:DH, :, 0:D], 127.0, -128.0, ALU.min, ALU.max))
            ch.link(nc.vector.tensor_copy(keep["identb"][:], keep["ident"][:]))
            ch.link(nc.vector.tensor_copy(keep["tri"][:], tri[:]))


def token_pass(nc, io, keep):
    with ExitStack() as stack:
        c = Ctx(nc, stack, "tok_")
        frames = c.sb("frames", [128, 2, 2, FRAME])
        frT = c.sb("frT", [FRAME, S])
        power = c.sb("power", [2 * BINS, S])
        logmel = c.sb("logmel", [FILTERS, S])
        mfcc = c.sb("mfcc", [MFCC + 1, S])
        dft = c.sb("dft", [FRAME, 2 * BINS])
        mel = c.sb("mel", [2 * BINS, FILTERS])
        dct = c.sb("dct", [FILTERS, MFCC])
        wtok = c.sb("wtok", [MFCC + 1, D])
        tiny = c.sb("tiny", [128, 1])
        zeros = c.sb("zeros", [128, TILES2 // FILLS * D])
        zeroed = c.sem("zeroed")
        filled = c.sem("filled")
        h1 = c.sb("h1", [128, 2, 2, D])
        ln = NormTiles(c)
        xn = c.sb("xn", [128, 2, 2, D])
        xnT = c.sb("xnT", [DH + 1, 2, 2, S])
        ext = c.sb("ext", [128, 10])
        acc = c.sb("acc", [128, 10])
        merged = c.sb("merged", [128, 6])
        extrema = c.sb("extrema", [128, 6])

        ps_fr = c.ps("ps_fr", [128, 2, 256])
        ps_mel = c.ps("ps_mel", [128, 2, 256])
        ps_h = c.ps("ps_h", [128, 2, 256])
        ps_xT = c.ps("ps_xT", [128, 2, 256])
        ps_qk = c.ps("ps_qk", [128, 6, 256])
        ps_v = c.ps("ps_v", [128, 2, 256])

        loaded = c.sem("loaded")
        inited = c.sem("inited")
        frames_in = [c.sem(f"frames_in{u}") for u in range(2)]
        frT_ps = c.sem("frT_ps")
        frT_ready = c.sem("frT_ready")
        dft_ps = c.sem("dft_ps")
        power_ready = c.sem("power_ready")
        mel_ps = c.sem("mel_ps")
        log_ready = c.sem("log_ready")
        mfcc_ps = c.sem("mfcc_ps")
        mfcc_ready = c.sem("mfcc_ready")
        h_ps = c.sem("h_ps")
        passed = c.sem("passed")
        h1_done = c.sem("h1_done")
        h1_stored = [c.sem(f"h1_stored{u}") for u in range(2)]
        xn_ready = c.sem("xn_ready")
        xT_ps = c.sem("xT_ps")
        xnT_ready = c.sem("xnT_ready")
        xnT_stored = [c.sem(f"xnT_stored{u}") for u in range(2)]
        part_ps = c.sem("part_ps")
        part_done = c.sem("part_done")
        chain_f = c.sem("chain_f")
        chain_b = c.sem("chain_b")
        pads_out = c.sem("pads_out")
        acc_ready = c.sem("acc_ready")
        all_ready = c.sem("all_ready")
        scalars = c.sem("scalars")
        n_wload = 4

        block = stack.enter_context(nc.Block())

        @block.sync
        def _(sp):
            sp.dma_start(dft[:], io["dft"]).then_inc(loaded, 16)
            sp.dma_start(mel[:], io["mel"]).then_inc(loaded, 16)
            sp.dma_start(dct[:], io["dct"]).then_inc(loaded, 16)
            sp.dma_start(wtok[:], io["wtok"]).then_inc(loaded, 16)

            def load(r):
                b, u = r.b, r.u
                if not r.first:
                    sp.wait_ge(frT_ps, b - 1)
                    sp.sem_inc(passed, 1)
                src = io["x"][b].rearrange("(t p s) -> p t s", t=2, p=TR)[:, :, 0:FRAME]
                sp.dma_start(frames[0:TR, u, :, :], src).then_inc(frames_in[u], 16)

            def store(r):
                b, u = r.b, r.u
                sp.wait_ge(h1_done, b + 2)
                sp.dma_start(io["h1"][b], h1[0:TR, u, :, :]).then_inc(h1_stored[u], 16)
                sp.wait_ge(xnT_ready, b + 1)
                sp.dma_start(io["xnT"][b], xnT[0:DH, u, :, :]).then_inc(xnT_stored[u], 16)

            load_store_rows(sp, load, store)
            for u in range(2):
                sp.wait_ge(h1_stored[u], 16 + 8 * B)
                sp.wait_ge(xnT_stored[u], 16 + 8 * B)

        @block.tensor
        def _(pe):
            pe.wait_ge(loaded, 16 * n_wload)
            pe.wait_ge(inited, 3)

            def front(r):
                b, u = r.b, r.u
                """The steps from frames to h1, each waiting for the one before on ScalarE."""
                def transposes():
                    pe.wait_ge(frames_in[u], r.k * 16 + 16)
                    for t in range(2):
                        last = nc.tensor.transpose(ps_fr[0:FRAME, 0, t * TR:t * TR + TR], frames[0:TR, u, t, :],
                                                   keep["ident"][0:TR, 0:TR])
                    last.then_inc(frT_ps, 1)

                def spectrum():
                    pe.wait_ge(frT_ready, b + 1)
                    nc.tensor.matmul(ps_fr[0:2 * BINS, 1, 0:S], dft[:], frT[:], start=True, stop=True).then_inc(dft_ps, 1)

                def filters():
                    pe.wait_ge(power_ready, b + 1)
                    nc.tensor.matmul(ps_mel[0:FILTERS, 0, 0:S], mel[:], power[:], start=True, stop=True).then_inc(mel_ps, 1)

                def cepstrum():
                    pe.wait_ge(log_ready, b + 1)
                    pe.sem_inc(passed, 1)
                    nc.tensor.matmul(ps_mel[0:MFCC, 1, 0:S], dct[:], logmel[:], start=True, stop=True).then_inc(mfcc_ps, 1)

                def project():
                    pe.wait_ge(mfcc_ready, b + 1)
                    pe.wait_ge(h1_done, b + 1)
                    for t in range(2):
                        last = nc.tensor.matmul(ps_h[0:TR, t, 0:D], mfcc[:, t * TR:t * TR + TR], wtok[:], start=True, stop=True)
                    last.then_inc(h_ps, 1)

                return [transposes, spectrum, filters, cepstrum, project]

            def back(r):
                b, u = r.b, r.u
                """The normed tokens transposed, then q and k by rows of heads, v by tokens."""
                def transposes():
                    pe.wait_ge(xn_ready, b + 1)
                    for half_ in range(2):
                        for t in range(2):
                            last = nc.tensor.transpose(ps_xT[0:DH, half_, t * TR:t * TR + TR],
                                                       xn[0:TR, u, t, half_ * DH:half_ * DH + DH], keep["ident"][0:TR, 0:TR])
                    last.then_inc(xT_ps, 1)

                def heads(pair, part):
                    def do():
                        if part == 0:
                            pe.wait_ge(xnT_ready, b + 1)
                        pe.wait_ge(part_done, b * 4 + (part + 1))
                        for m in (2 * pair, 2 * pair + 1):
                            last = project_heads(nc, ps_qk, keep["wqkv"], xnT[:, u], m, m)
                        last.then_inc(part_ps, 1)
                    return do

                def values():
                    pe.wait_ge(part_done, b * 4 + 2)
                    project_values(nc, ps_v, keep["wqkv"], xnT[:, u]).then_inc(part_ps, 1)

                return [transposes, heads(0, 0), values, heads(1, 2), heads(2, 3)]

            def step(r, b1, b2):
                for f, g in zip_longest(back(b2) if b2 is not None else [], front(r) if r is not None else []):
                    for job in (f, g):
                        if job is not None:
                            job()

            rows_deep(pe, step, 3)

        @block.scalar
        def _(act):
            for u in range(2):
                act.sem_inc(xnT_stored[u], 16)
            act.wait_ge(inited, 3)

            def front(r):
                b, u = r.b, r.u
                act.wait_ge(frT_ps, b + 1)
                nc.scalar.activation(frT[:], ps_fr[0:FRAME, 0, 0:S], ACT.Copy).then_inc(frT_ready, 1)
                act.wait_ge(dft_ps, b + 1)
                nc.scalar.activation(power[:], ps_fr[0:2 * BINS, 1, 0:S], ACT.Square).then_inc(power_ready, 1)
                act.wait_ge(mel_ps, b + 1)
                nc.scalar.activation(logmel[:], ps_mel[0:FILTERS, 0, 0:S], ACT.Ln, bias=tiny[0:FILTERS, :]).then_inc(log_ready, 1)
                act.wait_ge(mfcc_ps, b + 1)
                nc.scalar.activation(mfcc[0:MFCC, :], ps_mel[0:MFCC, 1, 0:S], ACT.Copy).then_inc(mfcc_ready, 1)

            def back(r):
                b, u = r.b, r.u
                act.wait_ge(xT_ps, b + 1)
                act.wait_ge(xnT_stored[u], r.k * 16 + 16)
                nc.scalar.activation(xnT[0:DH, u, :, :], ps_xT[0:DH, :, 0:S], ACT.Copy).then_inc(xnT_ready, 1)

            def step(r, b1, b2):
                if b2 is not None:
                    back(b2)
                if r is not None:
                    front(r)

            act.wait_ge(zeroed, 1)
            for n in range(FILLS):
                act.dma_start(io["slotted"].rearrange("(n p s) d -> n p (s d)", n=FILLS, p=128)[n], zeros[:]).then_inc(filled, 16)
            rows_deep(act, step, 3)
            act.wait_ge(filled, 16 * FILLS)

        @block.gpsimd
        def _(pool):
            nc.gpsimd.memset(zeros[:], 0.0).then_inc(zeroed, 1)
            pool.wait_ge(zeroed, 1)
            nc.gpsimd.memset(ln.half[:], -0.5).then_inc(ln.half_ready, 1)
            nc.gpsimd.memset(mfcc[:], 1.0).then_inc(inited, 1)
            pool.wait_ge(ln.half_ready, 1)

            def body(r):
                b, u = r.b, r.u
                inverse_root(nc, pool, ln, b)

            rows(pool, body)
            pool.wait_ge(acc_ready, 1)
            nc.gpsimd.partition_all_reduce(extrema[:], merged[:], 128, RMAX).then_inc(all_ready, 1)

        @block.vector
        def _(dve):
            chf, chb = Chain(dve, chain_f), Chain(dve, chain_b)
            for u in range(2):
                dve.sem_inc(h1_stored[u], 16)
            dve.sem_inc(h1_done, 1)
            dve.sem_inc(part_done, 4)
            nc.vector.memset(tiny[:], 1e-6).then_inc(inited, 1)
            for tile in (ext, acc):
                chb.of(nc.vector.memset(tile[:, 0:5], -BIG))
                chb.of(nc.vector.memset(tile[:, 5:10], BIG))
            nc.vector.memset(xnT[DH:DH + 1, :, :, :], 1.0).then_inc(inited, 1)
            chb.sync()
            ahead, in_front, in_back = 4, 4, 6

            def front(r):
                b, u = r.b, r.u
                chf.start(b * in_front)
                dve.wait_ge(h_ps, b + 1)
                dve.wait_ge(h1_stored[u], r.k * 16 + 16)
                nc.vector.tensor_copy(h1[0:TR, u, :, :], ps_h[0:TR, :, 0:D]).then_inc(h1_done, 1)
                dve.wait_ge(h1_done, b + 2)
                norm_stats(nc, dve, chf, h1[:, u], ln)
                norm_apply(nc, dve, h1[:, u], xn[:, u], ln, b).then_inc(xn_ready, 1)
                assert chf.n == in_front

            def back(r):
                b, u = r.b, r.u
                chb.start(b * in_back + ahead)
                for n, (source, p, at) in enumerate(((ps_qk[:, 0:2, 0:S], 128, 0), (ps_v[0:TR, :, 0:D], TR, 2),
                                                     (ps_qk[:, 2:4, 0:S], 128, 3), (ps_qk[:, 4:6, 0:S], 128, 1))):
                    axes, w = (AX.X, 2) if at == 3 else (AX.XY, 1)
                    dve.wait_ge(part_ps, b * 4 + (n + 1))
                    chb.of(nc.vector.tensor_reduce(ext[0:p, at:at + w], source, axes, ALU.max))
                    nc.vector.tensor_reduce(ext[0:p, at + 5:at + 5 + w], source, axes, ALU.min).then_inc(part_done, 1)
                chb.sync()
                dve.wait_ge(part_done, b * 4 + 8)
                chb.of(nc.vector.tensor_tensor(acc[:, 0:5], acc[:, 0:5], ext[:, 0:5], ALU.max))
                chb.of(nc.vector.tensor_tensor(acc[:, 5:10], acc[:, 5:10], ext[:, 5:10], ALU.min))
                chb.sync()
                assert chb.n == in_back

            def step(r, b1, b2):
                if b2 is not None:
                    back(b2)
                if r is not None:
                    front(r)

            rows_deep(dve, step, 3)
            chb.start(B * in_back + ahead)
            chb.link(nc.vector.tensor_tensor(merged[:, 0:2], acc[:, 0:2], acc[:, 3:5], ALU.max))
            chb.link(nc.vector.tensor_tensor(merged[:, 3:5], acc[:, 5:7], acc[:, 8:10], ALU.min))
            chb.link(nc.vector.tensor_copy(merged[:, 2:3], acc[:, 2:3]))
            chb.link(nc.vector.tensor_copy(merged[:, 5:6], acc[:, 7:8]))
            nc.vector.tensor_scalar(merged[:, 0:2], merged[:, 0:2], keep["padmask"][:, 0:1], None, ALU.subtract).then_inc(pads_out, 1)
            nc.vector.tensor_scalar(merged[:, 3:5], merged[:, 3:5], keep["padmask"][:, 0:1], None, ALU.add).then_inc(pads_out, 1)
            dve.wait_ge(pads_out, 2)
            nc.vector.tensor_scalar(merged[:, 3:6], merged[:, 3:6], -1.0, None, ALU.mult).then_inc(acc_ready, 1)
            dve.wait_ge(all_ready, 1)
            quantisers_qkv(nc, dve, Chain(dve, scalars), keep["par"], extrema)


def quantise_pass(nc, io, keep):
    with ExitStack() as stack:
        c = Ctx(nc, stack, "quant_")
        xnT = c.sb("xnT", [DH + 1, 2, 2, S])
        x1 = c.sb("x1", [128, 6, S])
        v1 = c.sb("v1", [128, 2, D])
        i1 = c.sb("i1", [128, 6, S], BF16)
        j1 = c.sb("j1", [128, 2, D], BF16)
        x2 = c.sb("x2", [128, 6, S])
        v2 = c.sb("v2", [128, 2, D])
        qk = c.sb("qk", [128, 2, 6, S], BF16)
        v = c.sb("v", [128, 2, 2, D], BF16)
        row_max = c.sb("row_max", [128, 2, 2 * HEADS])
        least = c.sb("least", [128, PAIRS])
        ext = c.sb("ext", [128, 2])
        acc = c.sb("acc", [128, 2])
        extrema = c.sb("extrema", [128, 2])
        ps_qk = c.ps("ps_qk", [128, 6, 256])
        ps_v = c.ps("ps_v", [128, 2, 256])
        ps_s = c.ps("ps_s", [128, 2, 2, 2, 256])

        passed = c.sem("passed")
        inited = c.sem("inited")
        xnT_in = [c.sem(f"xnT_in{u}") for u in range(2)]
        stored = [c.sem(f"stored{u}") for u in range(2)]
        max_stored = [c.sem(f"max_stored{u}") for u in range(2)]
        qkv_ps = c.sem("qkv_ps")
        x1_done = c.sem("x1_done")
        v1_done = c.sem("v1_done")
        i1_ready = c.sem("i1_ready")
        x2_ready = c.sem("x2_ready")
        qk_ready = c.sem("qk_ready")
        v_ready = c.sem("v_ready")
        scores_ps = c.sem("scores_ps")
        pair_done = c.sem("pair_done")
        row_max_ready = c.sem("row_max_ready")
        chain = c.sem("chain")
        acc_ready = c.sem("acc_ready")
        all_ready = c.sem("all_ready")
        scalars = c.sem("scalars")
        block = stack.enter_context(nc.Block())

        @block.sync
        def _(sp):
            def step(l, a, r, b1):
                if l is not None:
                    if not (isinstance(l.b, int) and l.b < 2):
                        sp.wait_ge(qkv_ps, l.b - 1)
                        sp.sem_inc(passed, 1)
                    sp.dma_start(xnT[0:DH, l.u, :, :], io["xnT"][l.b]).then_inc(xnT_in[l.u], 16)
                if r is not None:
                    sp.wait_ge(qk_ready, r.b + 1)
                    sp.sem_inc(passed, 1)
                    sp.dma_start(io["qk"][r.b], qk[:, r.u, :, :]).then_inc(stored[r.u], 16)
                    sp.wait_ge(v_ready, r.b + 1)
                    sp.sem_inc(passed, 1)
                    sp.dma_start(io["v"][r.b], v[0:TR, r.u, :, :]).then_inc(stored[r.u], 16)
                if b1 is not None:
                    sp.wait_ge(row_max_ready, b1.b + 1)
                    sp.sem_inc(passed, 1)
                    sp.dma_start(io["row_max"][b1.b], row_max[0:TR, b1.u, :]).then_inc(max_stored[b1.u], 16)

            rows_deep(sp, step, 4)
            for u in range(2):
                sp.wait_ge(stored[u], 32 + 16 * B)
                sp.wait_ge(max_stored[u], 16 + 8 * B)

        @block.tensor
        def _(pe):
            pe.wait_ge(inited, 1)

            def project(r, n):
                if n < 3:
                    if n == 0:
                        pe.wait_ge(xnT_in[r.u], r.k * 16 + 16)
                        pe.wait_ge(x1_done, r.b + 1)
                    for m in (2 * n, 2 * n + 1):
                        project_heads(nc, ps_qk, keep["wqkv"], xnT[:, r.u], m, m)
                else:
                    pe.wait_ge(v1_done, r.b + 1)
                    project_values(nc, ps_v, keep["wqkv"], xnT[:, r.u]).then_inc(qkv_ps, 1)

            def scores(r, p):
                if p == 0:
                    pe.wait_ge(qk_ready, r.b + 1)
                pe.wait_ge(pair_done, r.b * PAIRS + (p + 1))
                for e in range(2):
                    g, at = (2 * p + e) // 4, HPB * ((2 * p + e) % 4)
                    for t in range(2):
                        last = nc.tensor.matmul(ps_s[0:TR, p % 2, e, t, 0:S], qk[at:at + HPB, r.u, g, t * TR:t * TR + TR],
                                                qk[at:at + HPB, r.u, GROUPS + g, :], start=True, stop=True)
                last.then_inc(scores_ps, 1)

            def step(a, r, b1):
                for p in range(PAIRS):
                    if b1 is not None:
                        scores(b1, p)
                    if a is not None and 1 <= p < 5:
                        project(a, p - 1)

            rows_deep(pe, step, 3)

        @block.scalar
        def _(act):
            act.sem_inc(x1_done, 1)
            act.sem_inc(v1_done, 1)
            act.sem_inc(pair_done, 2)
            for u in range(2):
                act.sem_inc(stored[u], 32)
                act.sem_inc(max_stored[u], 16)

            magic, inv1 = keep["magic"], par(keep, "inv1")

            def step(a, r, b1):
                if r is not None:
                    act.wait_ge(i1_ready, r.b + 1)
                    nc.scalar.activation(x2[:, 0:3, :], i1[:, 0:3, :], ACT.Identity, scale=par(keep, "ratio_q"), bias=magic[:])
                    nc.scalar.activation(x2[:, 3:6, :], i1[:, 3:6, :], ACT.Identity, scale=par(keep, "ratio_k"), bias=magic[:])
                    nc.scalar.activation(v2[0:TR], j1[0:TR], ACT.Identity, scale=par(keep, "ratio_v", TR),
                                         bias=magic[0:TR, :]).then_inc(x2_ready, 1)
                if a is not None:
                    act.wait_ge(qkv_ps, a.b + 1)
                    nc.scalar.activation(x1[:], ps_qk[:, :, 0:S], ACT.Identity, scale=inv1, bias=magic[:]).then_inc(x1_done, 1)
                    nc.scalar.activation(v1[0:TR], ps_v[0:TR, :, 0:D], ACT.Identity, scale=par(keep, "inv1", TR),
                                         bias=magic[0:TR, :]).then_inc(v1_done, 1)

            rows_deep(act, step, 3)

        @block.gpsimd
        def _(pool):
            nc.gpsimd.memset(xnT[DH:DH + 1, :, :, :], 1.0).then_inc(inited, 1)
            pool.wait_ge(acc_ready, 1)
            nc.gpsimd.partition_all_reduce(extrema[:], acc[:], 128, RMAX).then_inc(all_ready, 1)

        @block.vector
        def _(dve):
            ch = Chain(dve, chain)
            ch.of(nc.vector.memset(acc[:, 0:1], -BIG))
            ch.of(nc.vector.memset(acc[:, 1:2], BIG))
            ch.sync()

            def first_quantiser(r):
                dve.wait_ge(x1_done, r.b + 2)
                nc.vector.tensor_scalar(i1[:], x1[:], par(keep, "top1"), MAGIC, ALU.min, ALU.subtract)
                dve.wait_ge(v1_done, r.b + 2)
                nc.vector.tensor_scalar(j1[0:TR], v1[0:TR], par(keep, "top1", TR), MAGIC, ALU.min, ALU.subtract)\
                    .then_inc(i1_ready, 1)

            def second_quantiser(r):
                dve.wait_ge(x2_ready, r.b + 1)
                dve.wait_ge(stored[r.u], r.k * 32 + 32)
                nc.vector.tensor_scalar(qk[:, r.u, 0:3, :], x2[:, 0:3, :], par(keep, "top_q"), MAGIC, ALU.min, ALU.subtract)
                nc.vector.tensor_scalar(qk[:, r.u, 3:6, :], x2[:, 3:6, :], par(keep, "top_k"), MAGIC, ALU.min, ALU.subtract)\
                    .then_inc(qk_ready, 1)
                nc.vector.tensor_scalar(v[0:TR, r.u], v2[0:TR], par(keep, "top_v", TR), MAGIC, ALU.min, ALU.subtract)\
                    .then_inc(v_ready, 1)

            def pair(r, p):
                if p == 0:
                    dve.wait_ge(max_stored[r.u], r.k * 16 + 16)
                dve.wait_ge(scores_ps, r.b * PAIRS + (p + 1))
                s_ = ps_s[0:TR, p % 2, :, :, 0:S]
                ch.of(nc.vector.tensor_reduce(row_max[0:TR, r.u, 4 * p:4 * p + 4], s_, AX.X, ALU.max))
                nc.vector.tensor_reduce(least[0:TR, p:p + 1], s_, AX.XYZ, ALU.min).then_inc(pair_done, 1)

            def row_end(r):
                ch.sync()
                dve.wait_ge(pair_done, r.b * PAIRS + (PAIRS + 2))
                nc.vector.tensor_reduce(ext[0:TR, 0:1], row_max[0:TR, r.u, :], AX.X, ALU.max).then_inc(row_max_ready, 1)
                ch.of(nc.vector.tensor_reduce(ext[0:TR, 1:2], least[0:TR, :], AX.X, ALU.min))
                ch.sync()
                dve.wait_ge(row_max_ready, r.b + 1)
                ch.of(nc.vector.tensor_tensor(acc[0:TR, 0:1], acc[0:TR, 0:1], ext[0:TR, 0:1], ALU.max))
                ch.of(nc.vector.tensor_tensor(acc[0:TR, 1:2], acc[0:TR, 1:2], ext[0:TR, 1:2], ALU.min))
                ch.sync()

            ahead, per_row = 2, PAIRS + 3

            def step(a, r, b1):
                if r is not None:
                    first_quantiser(r)
                if b1 is not None:
                    ch.start(b1.b * per_row + ahead)
                for p in range(PAIRS):
                    if b1 is not None:
                        pair(b1, p)
                    if r is not None and p == 2:
                        second_quantiser(r)
                if b1 is not None:
                    row_end(b1)
                    assert ch.n == per_row

            rows_deep(dve, step, 3)
            nc.vector.tensor_scalar(acc[:, 1:2], acc[:, 1:2], -1.0, None, ALU.mult).then_inc(acc_ready, 1)
            dve.wait_ge(all_ready, 1)
            quantiser_scores(nc, dve, Chain(dve, scalars), keep["par"], extrema)


def lagged(r, before, p, lag):
    if p >= lag:
        return r, p - lag
    return (before, PAIRS + p - lag) if before is not None else None


def integer_softmax_pass(nc, io, keep):
    with ExitStack() as stack:
        c = Ctx(nc, stack, "isoft_")
        unit = [128, 2, 2, 2, S]
        qk = c.sb("qk", [128, 2, 6, S], BF16)
        v = c.sb("v", [128, 2, 2, D], BF16)
        vf = c.sb("vf", [128, 2, 2, HEADS, HD + 1])
        maxima = c.sb("maxima", [128, B, 2 * HEADS])
        rounded = c.sb("rounded", [128, B, 2 * HEADS])
        steps = c.sb("steps", [128, B, 2 * HEADS], BF16)
        mcol = c.sb("mcol", [128, 2, 2 * HEADS], BF16)
        t = c.sb("t", unit)
        d0 = c.sb("d0", unit, BF16)
        d = c.sb("d", unit, BF16)
        kf = c.sb("kf", unit)
        k = c.sb("k", unit)
        kn = c.sb("kn", unit, BF16)
        rem = c.sb("rem", unit, BF16)
        sq = c.sb("sq", unit)
        pw = c.sb("pw", unit, I32)
        e_ = c.sb("e", unit)
        inv_sum = c.sb("inv_sum", [128, 2, HEADS])
        o = c.sb("o", [128, 2, 2, D])
        ext = c.sb("ext", [128, 2])
        acc = c.sb("acc", [128, 2])
        extrema = c.sb("extrema", [128, 2])
        ps_s = c.ps("ps_s", [128, 2, 2, 2, 256])
        ps_m = c.ps("ps_m", [128, 2, 2, 256])
        ps_o = c.ps("ps_o", [128, 2, 512])

        def low(x):
            return x.bitcast(I16).rearrange("p e t (s h) -> p e t s h", h=2)[:, :, :, :, 0]

        rows_in = [c.sem(f"rows_in{u}") for u in range(2)]
        maxima_in = c.sem("maxima_in")
        rounded_ready = c.sem("rounded_ready")
        steps_ready = c.sem("steps_ready")
        ones_ready = c.sem("ones_ready")
        v_ready = c.sem("v_ready")
        mcol_ready = c.sem("mcol_ready")
        passed = c.sem("passed")
        pv_done = c.sem("pv_done")
        scores_ps = c.sem("scores_ps")
        t_ready = c.sem("t_ready")
        d0_done = c.sem("d0_done")
        d_ready = c.sem("d_ready")
        kf_ready = c.sem("kf_ready")
        k_ready = c.sem("k_ready")
        kn_ready = c.sem("kn_ready")
        rem_ready = c.sem("rem_ready")
        sq_ready = c.sem("sq_ready")
        pw_ready = c.sem("pw_ready")
        e_done = c.sem("e_done")
        unit_pv = c.sem("unit_pv")
        o_ready = c.sem("o_ready")
        o_read = c.sem("o_read")
        stored = [c.sem(f"stored{u}") for u in range(2)]
        chain = c.sem("chain")
        acc_ready = c.sem("acc_ready")
        all_ready = c.sem("all_ready")
        scalars = c.sem("scalars")
        block = stack.enter_context(nc.Block())

        @block.sync
        def _(sp):
            sp.dma_start(maxima[0:TR], io["row_max"].rearrange("b p h -> p b h")).then_inc(maxima_in, 16)

            def load(r):
                if not r.first:
                    sp.wait_ge(scores_ps, r.b * PAIRS - PAIRS)
                    sp.sem_inc(passed, 1)
                    sp.wait_ge(v_ready, r.b - 1)
                    sp.sem_inc(passed, 1)
                sp.dma_start(qk[:, r.u], io["qk"][r.b]).then_inc(rows_in[r.u], 16)
                sp.dma_start(v[0:TR, r.u], io["v"][r.b]).then_inc(rows_in[r.u], 16)

            def store(r):
                sp.wait_ge(o_ready, r.b + 1)
                sp.dma_start(io["o"][r.b], o[0:TR, r.u]).then_inc(stored[r.u], 16)

            load_store_rows(sp, load, store)
            for u in range(2):
                sp.wait_ge(stored[u], 16 + 8 * B)

        @block.tensor
        def _(pe):
            pe.sem_inc(unit_pv, 2)
            pe.sem_inc(pv_done, 2)

            def scores(r, p):
                if p == 0:
                    pe.wait_ge(rows_in[r.u], r.k * 32 + 32)
                    pe.wait_ge(mcol_ready, r.b + 1)
                pe.wait_ge(d0_done, r.b * PAIRS + (p + 1))
                for e in range(2):
                    h = 2 * p + e
                    for i in range(2):
                        col = mcol[0:TR, r.u, 2 * h + i:2 * h + i + 1].to_broadcast([TR, TR])
                        nc.tensor.matmul(ps_m[0:TR, p % 2, e, i * TR:i * TR + TR], col, keep["identb"][0:TR, 0:TR],
                                         start=True, stop=True)
                for e in range(2):
                    g, at = (2 * p + e) // 4, HPB * ((2 * p + e) % 4)
                    for i in range(2):
                        last = nc.tensor.matmul(ps_s[0:TR, p % 2, e, i, 0:S],
                                                qk[at:at + HPB, r.u, GROUPS + g, i * TR:i * TR + TR],
                                                qk[at:at + HPB, r.u, g, :], start=True, stop=True)
                last.then_inc(scores_ps, 1)

            def values(r, p):
                if p == 0:
                    pe.wait_ge(v_ready, r.b + 1)
                    pe.wait_ge(o_read, r.b + 1)
                pe.wait_ge(e_done, r.b * PAIRS + (p + 3))
                for e in range(2):
                    h = 2 * p + e
                    for i in range(2):
                        at = (i * HEADS + h) * (HD + 1)
                        for j in range(2):
                            last = nc.tensor.matmul(ps_o[0:TR, r.u, at:at + HD + 1],
                                                    e_[0:TR, p % 2, e, j, i * TR:i * TR + TR],
                                                    vf[0:TR, r.u, j, h, :], start=(j == 0), stop=(j == 1))
                last.then_inc(unit_pv, 1)
                if p == PAIRS - 1:
                    pe.wait_ge(unit_pv, r.b * PAIRS + (PAIRS + 2))
                    pe.sem_inc(pv_done, 1)

            def step(r, before):
                for p in range(PAIRS):
                    scores(r, p)
                    at = lagged(r, before, p, 4)
                    if at:
                        values(*at)

            rows_skewed(pe, lambda r: step(r, None), step, lambda r: [values(r, p) for p in range(2, PAIRS)])

        @block.scalar
        def _(act):
            act.sem_inc(d0_done, 2)
            act.sem_inc(e_done, 2)
            act.sem_inc(o_read, 2)
            for u in range(2):
                act.sem_inc(stored[u], 16)
            act.wait_ge(maxima_in, 16)
            nc.scalar.activation(rounded[0:TR], maxima[0:TR], ACT.Identity, scale=par(keep, "c_a", TR),
                                 bias=keep["magic"][0:TR, :]).then_inc(rounded_ready, 1)

            def quantise(r, p):
                n = r.b * PAIRS + (p + 1)
                act.wait_ge(scores_ps, n)
                nc.scalar.activation(t[0:TR, p % 2], ps_s[0:TR, p % 2, :, :, 0:S], ACT.Identity,
                                     scale=par(keep, "c_a", TR), bias=keep["magic"][0:TR, :]).then_inc(t_ready, 1)

            def round_k(r, p):
                act.wait_ge(kf_ready, r.b * PAIRS + (p + 1))
                nc.scalar.activation(k[0:TR, p % 2], kf[0:TR, p % 2], ACT.Identity,
                                     bias=keep["magic"][0:TR, :]).then_inc(k_ready, 1)

            def square(r, p):
                act.wait_ge(rem_ready, r.b * PAIRS + (p + 1))
                nc.scalar.activation(sq[0:TR, p % 2], rem[0:TR, p % 2], ACT.Square,
                                     bias=par(keep, "b_half", TR)).then_inc(sq_ready, 1)

            def step(r, before):
                for p in range(PAIRS):
                    quantise(r, p)
                    for f, lag in ((round_k, 1), (square, 2)):
                        at = lagged(r, before, p, lag)
                        if at:
                            f(*at)

            def last(r):
                round_k(r, PAIRS - 1)
                square(r, PAIRS - 2)
                square(r, PAIRS - 1)

            rows_skewed(act, lambda r: step(r, None), step, last)

        @block.gpsimd
        def _(pool):
            nc.gpsimd.memset(vf[:], 1.0).then_inc(ones_ready, 1)
            pool.wait_ge(ones_ready, 1)
            pool.wait_ge(steps_ready, 1)

            def prepare(r):
                pool.wait_ge(pv_done, r.b + 1)
                pool.wait_ge(rows_in[r.u], r.k * 32 + 32)
                nc.gpsimd.tensor_copy(mcol[0:TR, r.u, :], steps[0:TR, bass.ds(r.b, 1), :]).then_inc(mcol_ready, 1)
                for j in range(2):
                    last = nc.gpsimd.tensor_copy(vf[0:TR, r.u, j, :, 0:HD],
                                                 v[0:TR, r.u, j, :].rearrange("p (h d) -> p h d", h=HEADS))
                last.then_inc(v_ready, 1)

            def divide(r, p):
                pool.wait_ge(d_ready, r.b * PAIRS + (p + 1))
                pool.sem_inc(passed, 1)
                nc.gpsimd.tensor_scalar(kf[0:TR, p % 2], d[0:TR, p % 2], par(keep, "n_inv", TR), par(keep, "n_bias", TR),
                                        ALU.mult, ALU.add).then_inc(kf_ready, 1)

            def multiply(r, p):
                pool.wait_ge(k_ready, r.b * PAIRS + (p + 1))
                pool.sem_inc(passed, 1)
                nc.gpsimd.tensor_scalar(kn[0:TR, p % 2], low(k[0:TR, p % 2]), par(keep, "n_step", TR), 0.0, ALU.mult, ALU.add)\
                    .then_inc(kn_ready, 1)

            def power(r, p):
                pool.wait_ge(k_ready, r.b * PAIRS + (p + 1))
                pool.wait_ge(e_done, r.b * PAIRS + (p + 1))
                pool.sem_inc(passed, 1)
                nc.gpsimd.tensor_scalar(pw[0:TR, p % 2], low(k[0:TR, p % 2]), -(2.0**23), 127.0 * 2.0**23,
                                        ALU.mult, ALU.add).then_inc(pw_ready, 1)

            def work(r, before, units):
                for p in units:
                    at = lagged(r, before, p, 1)
                    if at:
                        multiply(*at)
                    divide(r, p)
                    if at:
                        power(*at)

            mid = PAIRS // 2

            def first(r):
                prepare(r)
                work(r, None, range(mid))

            def step(r, before):
                prepare(r)
                work(before, None, range(mid, PAIRS))
                work(r, before, range(mid))

            def last(r):
                work(r, None, range(mid, PAIRS))
                multiply(r, PAIRS - 1)
                power(r, PAIRS - 1)

            rows_skewed(pool, first, step, last)
            pool.wait_ge(acc_ready, 1)
            nc.gpsimd.partition_all_reduce(extrema[:], acc[:], 128, RMAX).then_inc(all_ready, 1)

        @block.vector
        def _(dve):
            ch = Chain(dve, chain)
            ch.of(nc.vector.memset(acc[:, 0:1], -BIG))
            ch.of(nc.vector.memset(acc[:, 1:2], BIG))
            ch.sync()
            dve.wait_ge(rounded_ready, 1)
            nc.vector.tensor_scalar(steps[0:TR], rounded[0:TR], par(keep, "a_top", TR), MAGIC, ALU.min, ALU.subtract)\
                .then_inc(steps_ready, 1)

            def differences(r, p):
                n = r.b * PAIRS + (p + 1)
                dve.wait_ge(t_ready, n)
                for e in range(2):
                    m = ps_m[0:TR, p % 2, e:e + 1, 0:S].to_broadcast([TR, 2, S])
                    last = nc.vector.tensor_tensor(d0[0:TR, p % 2, e], low(t[0:TR, p % 2])[:, e], m, ALU.subtract)
                last.then_inc(d0_done, 1)
                dve.wait_ge(d0_done, r.b * PAIRS + (p + 3))
                nc.vector.tensor_scalar(d[0:TR, p % 2], d0[0:TR, p % 2], 0.0, par(keep, "n_least", TR), ALU.min, ALU.max)\
                    .then_inc(d_ready, 1)

            def remainder(r, p):
                n = r.b * PAIRS + (p + 1)
                dve.wait_ge(kn_ready, n)
                nc.vector.tensor_tensor(rem[0:TR, p % 2], d[0:TR, p % 2], kn[0:TR, p % 2], ALU.add).then_inc(rem_ready, 1)

            def exponential(r, p):
                n = r.b * PAIRS + (p + 1)
                dve.wait_ge(sq_ready, n)
                dve.wait_ge(pw_ready, n)
                dve.wait_ge(unit_pv, n)
                nc.vector.scalar_tensor_tensor(e_[0:TR, p % 2], sq[0:TR, p % 2], par(keep, "c_rest", TR),
                                               pw[0:TR, p % 2].bitcast(F32), ALU.add, ALU.mult).then_inc(e_done, 1)

            def normalise(r):
                sums = ps_o[0:TR, r.u, 0:2 * HEADS * (HD + 1)].rearrange("p (i h d) -> p i h d", i=2, h=HEADS)
                dve.wait_ge(pv_done, r.b + 3)
                ch.link(nc.vector.reciprocal(inv_sum[0:TR], sums[:, :, :, HD]))
                dve.wait_ge(stored[r.u], r.k * 16 + 16)
                out = o[0:TR, r.u].rearrange("p i (h d) -> p i h d", h=HEADS)
                for i in range(2):
                    last = nc.vector.scalar_tensor_tensor(
                        out[:, i], sums[:, i, :, 0:HD], par(keep, "s_v", TR),
                        inv_sum[0:TR, i].unsqueeze(2).to_broadcast([TR, HEADS, HD]), ALU.mult, ALU.mult)
                    if i == 0:
                        ch.of(last)
                last.then_inc(o_ready, 1)
                dve.wait_ge(o_ready, r.b + 1)
                dve.sem_inc(o_read, 1)
                ch.of(nc.vector.tensor_reduce(ext[0:TR, 0:1], o[0:TR, r.u], AX.XY, ALU.max))
                ch.of(nc.vector.tensor_reduce(ext[0:TR, 1:2], o[0:TR, r.u], AX.XY, ALU.min))
                ch.sync()
                ch.of(nc.vector.tensor_tensor(acc[0:TR, 0:1], acc[0:TR, 0:1], ext[0:TR, 0:1], ALU.max))
                ch.of(nc.vector.tensor_tensor(acc[0:TR, 1:2], acc[0:TR, 1:2], ext[0:TR, 1:2], ALU.min))
                ch.sync()

            ahead, per_row = 2, 6

            def step(r, before):
                if before is not None:
                    ch.start(before.b * per_row + ahead)
                for p in range(PAIRS):
                    if p == 4 and before is not None:
                        normalise(before)
                        assert ch.n == per_row
                    differences(r, p)
                    for f, lag in ((exponential, 2), (remainder, 1)):
                        at = lagged(r, before, p, lag)
                        if at:
                            f(*at)

            def last(r):
                exponential(r, PAIRS - 2)
                remainder(r, PAIRS - 1)
                exponential(r, PAIRS - 1)
                ch.start(r.b * per_row + ahead)
                normalise(r)

            rows_skewed(dve, lambda r: step(r, None), step, last)
            nc.vector.tensor_scalar(acc[:, 1:2], acc[:, 1:2], -1.0, None, ALU.mult).then_inc(acc_ready, 1)
            dve.wait_ge(all_ready, 1)
            quantiser_out(nc, dve, Chain(dve, scalars), keep["par"], extrema, "o")


def project_out_pass(nc, io, keep):
    with ExitStack() as stack:
        c = Ctx(nc, stack, "projq_")
        o = c.sb("o", [128, 2, 2, D])
        x = c.sb("x", [128, 2, 2, D])
        oi = c.sb("oi", [128, 2, 2, D], BF16)
        oiT = c.sb("oiT", [DH, 2, 2, S], BF16)
        scale = c.sb("scale", [128, D])
        bias = c.sb("bias", [128, D])
        scaled = c.sb("scaled", [128, 2, 2, D])
        y = c.sb("y", [128, 2, 2, D])
        ext = c.sb("ext", [128, 2])
        acc = c.sb("acc", [128, 2])
        extrema = c.sb("extrema", [128, 2])
        ps_t = c.ps("ps_t", [128, 2, 2, 512], BF16)
        ps_y = c.ps("ps_y", [128, 2, 2, 256])
        loaded = c.sem("loaded")
        passed = c.sem("passed")
        o_in = [c.sem(f"o_in{u}") for u in range(2)]
        x_ready = c.sem("x_ready")
        oi_ready = c.sem("oi_ready")
        oiT_ps = c.sem("oiT_ps")
        oiT_ready = c.sem("oiT_ready")
        y_ps = c.sem("y_ps")
        scaled_done = c.sem("scaled_done")
        y_ready = c.sem("y_ready")
        stored = [c.sem(f"stored{u}") for u in range(2)]
        chain = c.sem("chain")
        acc_ready = c.sem("acc_ready")
        all_ready = c.sem("all_ready")
        scalars = c.sem("scalars")
        block = stack.enter_context(nc.Block())

        @block.sync
        def _(sp):
            sp.dma_start(bias[:], io["bproj_q"].partition_broadcast(128)).then_inc(loaded, 16)

            def store(r):
                sp.wait_ge(y_ready, r.b + 1)
                sp.dma_start(io["y"][r.b], y[0:TR, r.u]).then_inc(stored[r.u], 16)

            rows(sp, store)
            for u in range(2):
                sp.wait_ge(stored[u], 16 + 8 * B)

        @block.tensor
        def _(pe):
            def transposes(r):
                pe.wait_ge(oi_ready, r.b + 1)
                for h in range(2):
                    for t in range(2):
                        last = nc.tensor.transpose(ps_t[0:DH, r.u, h, t * TR + t:t * TR + t + TR],
                                                   oi[0:TR, r.u, t, h * DH:h * DH + DH], keep["identb"][0:TR, 0:TR])
                last.then_inc(oiT_ps, 1)

            def project(r):
                pe.wait_ge(oiT_ready, r.b + 1)
                pe.wait_ge(scaled_done, r.b + 1)
                for t in range(2):
                    for h in range(2):
                        last = nc.tensor.matmul(ps_y[0:TR, r.u, t, 0:D], oiT[:, r.u, h, t * TR:t * TR + TR],
                                                keep["wp"][:, h, :], start=(h == 0), stop=(h == 1))
                last.then_inc(y_ps, 1)

            def step(r, before):
                project(before)
                transposes(r)

            rows_skewed(pe, transposes, step, project)

        @block.scalar
        def _(act):
            act.sem_inc(scaled_done, 2)
            for u in range(2):
                act.sem_inc(stored[u], 16)

            def load(r):
                if not r.first:
                    act.wait_ge(x_ready, r.b - 1)
                    act.sem_inc(passed, 1)
                act.dma_start(o[0:TR, r.u], io["o"][r.b]).then_inc(o_in[r.u], 16)

            def scale_in(r):
                act.wait_ge(o_in[r.u], r.k * 16 + 16)
                nc.scalar.activation(x[0:TR, r.u], o[0:TR, r.u], ACT.Identity, scale=par(keep, "o_inv", TR),
                                     bias=keep["magic"][0:TR, :]).then_inc(x_ready, 1)

            def copy(r):
                act.wait_ge(oiT_ps, r.b + 1)
                for t in range(2):
                    last = nc.scalar.activation(oiT[:, r.u, :, t * TR:t * TR + TR],
                                                ps_t[0:DH, r.u, :, t * TR + t:t * TR + t + TR], ACT.Copy)
                last.then_inc(oiT_ready, 1)

            def step(r, before):
                scale_in(r)
                if not isinstance(before.b, int):
                    load(Row(before.b + 2, before.u, before.k + 1))
                copy(before)

            load(Row(0, 0, 0, first=True))
            load(Row(1, 1, 0, first=True))
            rows_skewed(act, scale_in, step, copy)

        @block.gpsimd
        def _(pool):
            pool.wait_ge(acc_ready, 1)
            nc.gpsimd.partition_all_reduce(extrema[:], acc[:], 128, RMAX).then_inc(all_ready, 1)

        @block.vector
        def _(dve):
            ch = Chain(dve, chain)
            ch.of(nc.vector.memset(acc[:, 0:1], -BIG))
            ch.of(nc.vector.memset(acc[:, 1:2], BIG))
            ch.of(nc.vector.tensor_scalar(scale[:], keep["wp_scale"][:], par(keep, "o_scale"), None, ALU.mult))
            ch.sync()
            dve.wait_ge(loaded, 16)

            def round_in(r):
                dve.wait_ge(x_ready, r.b + 1)
                nc.vector.tensor_scalar(oi[0:TR, r.u], x[0:TR, r.u], par(keep, "o_top", TR), MAGIC, ALU.min, ALU.subtract)\
                    .then_inc(oi_ready, 1)

            def finish(r):
                ch.start(r.b * 4 + 3)
                dve.wait_ge(y_ps, r.b + 1)
                nc.vector.tensor_tensor(scaled[0:TR, r.u], ps_y[0:TR, r.u, :, 0:D],
                                        scale[0:TR].unsqueeze(1).to_broadcast([TR, 2, D]), ALU.mult).then_inc(scaled_done, 1)
                dve.wait_ge(scaled_done, r.b + 3)
                dve.wait_ge(stored[r.u], r.k * 16 + 16)
                nc.vector.tensor_tensor(y[0:TR, r.u], scaled[0:TR, r.u],
                                        bias[0:TR].unsqueeze(1).to_broadcast([TR, 2, D]), ALU.add).then_inc(y_ready, 1)
                dve.wait_ge(y_ready, r.b + 1)
                ch.of(nc.vector.tensor_reduce(ext[0:TR, 0:1], y[0:TR, r.u], AX.XY, ALU.max))
                ch.of(nc.vector.tensor_reduce(ext[0:TR, 1:2], y[0:TR, r.u], AX.XY, ALU.min))
                ch.sync()
                ch.of(nc.vector.tensor_tensor(acc[0:TR, 0:1], acc[0:TR, 0:1], ext[0:TR, 0:1], ALU.max))
                ch.of(nc.vector.tensor_tensor(acc[0:TR, 1:2], acc[0:TR, 1:2], ext[0:TR, 1:2], ALU.min))
                ch.sync()

            def step(r, before):
                round_in(r)
                finish(before)

            rows_skewed(dve, round_in, step, finish)
            nc.vector.tensor_scalar(acc[:, 1:2], acc[:, 1:2], -1.0, None, ALU.mult).then_inc(acc_ready, 1)
            dve.wait_ge(all_ready, 1)
            quantiser_out(nc, dve, Chain(dve, scalars), keep["par"], extrema, "y")


def softmax_attention_pass(nc, io, keep):
    with ExitStack() as stack:
        c = Ctx(nc, stack, "fattn_")
        w = c.sb("w", [DH, 2, 3 * D])
        wo = c.sb("wo", [128, GROUPS, D])
        spread = c.sb("spread", [128, 128])
        wg = c.sb("wg", [DH + 1, 2, EXPERTS])
        gb = c.sb("gb", [DH, 2, 2, 2])
        y = c.sb("y", [128, 2, 2, D])
        h1 = c.sb("h1", [128, 2, 2, D])
        xy = c.sb("xy", [128, 2, 2, D])
        yi = c.sb("yi", [128, 2, D])
        ax = c.sb("ax", [128, 2, 2, 2, D])
        cx = c.sb("cx", [128, 2, 2, 2, D])
        z = c.sb("z", [128, 2, D])
        zT = c.sb("zT", [DH, 2, S])
        xs = c.sb("xs", [128, 2, 2, D])
        rest = c.sb("rest", [128, 2, 2, D])
        part = [c.sb(f"part_{n}", [128, 2, 2, D], BF16) for n in "hml"]
        stacks = c.sb("stacks", [128, 2, 2, 2, HEADS, len(PARTS_Q), HD], BF16)
        qk = c.sb("qk", [STACK + 3, 2, 2, HEADS, 2, TR], BF16)
        v = c.sb("v", [128, 2, 2, HEADS, HPB])
        top = c.sb("top", [128, 2, HEADS])
        top_rest = c.sb("top_rest", [128, 2, HEADS])
        top_parts = c.sb("top_parts", [128, 2, 3, HEADS], BF16)
        topT = c.sb("topT", [3 * HEADS, 2, 2, TR], BF16)
        pT = c.sb("pT", [128, 3, 2, S])
        oT = c.sb("oT", [128, GROUPS, S])
        inv_sum = c.sb("inv_sum", [128, 2, S])
        attT = c.sb("attT", [128, GROUPS, S])
        x2 = c.sb("x2", [128, 2, D])
        hx = c.sb("hx", [128, 2, 2, D])
        zn = c.sb("zn", [128, 2, 2, D])
        znT = c.sb("znT", [DH + 1, 2, S])
        logits = c.sb("logits", [128, 2, 2, EXPERTS])
        ln1, ln2, ln3 = (NormTiles(c, f"n{i}_") for i in range(1, 4))
        ps_s = c.ps("ps_s", [128, 2, 2, 256])
        ps_t = c.ps("ps_t", [128, 2, 2, 256])
        ps_a = c.ps("ps_a", [128, 512])
        ps_ab = ps_a[:].bitcast(BF16)
        ps_k = c.ps("ps_k", [128, 512])
        ps_kb = ps_k[:].bitcast(BF16)
        ps_v = ps_k[:].rearrange("p (t d) -> p t d", t=2)
        ps_c = c.ps("ps_c", [128, 2, 256])
        ps_o = c.ps("ps_o", [128, 512])
        A_JOBS = 3
        K_JOBS = HEADS // 2 + 1
        V_JOB = 3
        A_SLOT, K_SLOTS = 5, (0, 2, 3, 4, 6, 8, 10)

        loaded = c.sem("loaded")
        ones_ready = c.sem("ones_ready")
        passed = c.sem("passed")
        rows_in = [c.sem(f"rows_in{u}") for u in range(2)]
        cx_in = [c.sem(f"cx_in{u}") for u in range(2)]
        ax_stored = [c.sem(f"ax_stored{u}") for u in range(2)]
        stored = [c.sem(f"stored{u}") for u in range(2)]
        xy_ready = c.sem("xy_ready")
        yi_ready = c.sem("yi_ready")
        h2_ready = c.sem("h2_ready")
        xl_ready = c.sem("xl_ready")
        z_ready = c.sem("z_ready")
        a_ps = c.sem("a_ps")
        a_done = c.sem("a_done")
        parts_ready = c.sem("parts_ready")
        h_ready = c.sem("h_ready")
        q_stacked = c.sem("q_stacked")
        stacks_ready = c.sem("stacks_ready")
        k_ps = c.sem("k_ps")
        k_done = c.sem("k_done")
        scores_ps = c.sem("scores_ps")
        top_done = c.sem("top_done")
        top_parts_ready = c.sem("top_parts_ready")
        topT_ps = c.sem("topT_ps")
        topT_ready = c.sem("topT_ready")
        top_in = [c.sem(f"top_in{u}") for u in range(2)]
        scoresT_ps = c.sem("scoresT_ps")
        p_done = c.sem("p_done")
        pv_done = c.sem("pv_done")
        oT_ready = c.sem("oT_ready")
        sums_ps = c.sem("sums_ps")
        inverse_ready = c.sem("inverse_ready")
        half_ready = c.sem("half_ready")
        att_ready = c.sem("att_ready")
        proj_ps = c.sem("proj_ps")
        x2_ready = c.sem("x2_ready")
        hx_ready = c.sem("hx_ready")
        zn_ready = c.sem("zn_ready")
        znT_ps = c.sem("znT_ps")
        znT_ready = c.sem("znT_ready")
        gate_ps = c.sem("gate_ps")
        logits_done = c.sem("logits_done")
        chain_a = c.sem("chain_a")
        chain_c = c.sem("chain_c")
        chain_t = c.sem("chain_t")
        block = stack.enter_context(nc.Block())

        def parted(n, i):
            return part[n][0:TR, i].rearrange("p t (h d) -> p (t h) d", h=HEADS)

        def stacked(u, i):
            return stacks[0:TR, u, i].rearrange("p t h c d -> p (t h) c d")

        def job_of(pair):
            return pair + (pair >= V_JOB)

        def unit(r, h):
            return r.b * HEADS + h

        def lag(b1, b2, h, n):
            row, head = (b1, h - n) if h >= n else (b2, HEADS + h - n)
            return [(row, head)] if row is not None else []

        @block.sync
        def _(sp):
            for tile, name in ((w, "wqkv_f"), (wo, "wproj_f"), (spread, "spread"), (wg, "wgate"), (gb, "gains")):
                sp.dma_start(tile[:], io[name]).then_inc(loaded, 16)

            def step(a, r, q1, b1, b2):
                if a is not None:
                    if not (isinstance(a.b, int) and a.b < 2):
                        sp.wait_ge(h2_ready, a.b - 1)
                        sp.sem_inc(passed, 1)
                    sp.dma_start(y[0:TR, a.u], io["y"][a.b]).then_inc(rows_in[a.u], 16)
                    sp.dma_start(h1[0:TR, a.u], io["h1"][a.b]).then_inc(rows_in[a.u], 16)
                if r is not None:
                    sp.wait_ge(xl_ready, r.b + 1)
                    sp.sem_inc(passed, 1)
                    sp.dma_start(io["hxl"][r.b], ax[0:TR, r.u]).then_inc(ax_stored[r.u], 16)
                if b1 is not None:
                    sp.wait_ge(ax_stored[b1.u], b1.k * 16 + 32)
                    sp.sem_inc(passed, 1)
                    if not (isinstance(b1.b, int) and b1.b < 2):
                        sp.wait_ge(hx_ready, b1.b - 1)
                        sp.sem_inc(passed, 1)
                    sp.dma_start(cx[0:TR, b1.u], io["hxl"][b1.b]).then_inc(cx_in[b1.u], 16)
                if b2 is not None:
                    sp.wait_ge(hx_ready, b2.b + 1)
                    sp.sem_inc(passed, 1)
                    sp.dma_start(io["hx"][b2.b], hx[0:TR, b2.u]).then_inc(stored[b2.u], 16)
                    sp.wait_ge(zn_ready, b2.b + 1)
                    sp.sem_inc(passed, 1)
                    sp.dma_start(io["zn"][b2.b], zn[0:TR, b2.u]).then_inc(stored[b2.u], 16)
                    sp.wait_ge(logits_done, b2.b + 2)
                    sp.sem_inc(passed, 1)
                    sp.dma_start(io["logits"][b2.b], logits[0:TR, b2.u]).then_inc(stored[b2.u], 16)

            rows_deep(sp, step, 5)
            for u in range(2):
                sp.wait_ge(stored[u], 48 + 24 * B)
                sp.wait_ge(ax_stored[u], 16 + 8 * B)

        @block.tensor
        def _(pe):
            pe.wait_ge(loaded, 80)
            pe.wait_ge(ones_ready, 4)
            ident = keep["ident"][0:TR, 0:TR]

            def scores(r, h):
                if h % 2 == 0:
                    pe.wait_ge(k_done, r.b * K_JOBS + (job_of(h // 2) + 2))
                pe.wait_ge(top_done, unit(r, h) + 1)
                for t in range(2):
                    last = nc.tensor.matmul(ps_s[0:TR, h % 2, t, 0:S], qk[0:STACK, r.u, 0, h, t, :],
                                            qk[0:STACK, r.u, 1, h].rearrange("p t s -> p (t s)"), start=True, stop=True)
                last.then_inc(scores_ps, 1)

            def turn_top(r):
                after = r.b + 1 if not isinstance(r.b, int) else min(r.b + 1, B - 1)
                pe.wait_ge(a_done, after * A_JOBS + (A_JOBS + 1))
                pe.wait_ge(top_parts_ready, r.b + 1)
                pe.sem_inc(passed, 1)
                for t in range(2):
                    last = nc.tensor.transpose(ps_ab[0:3 * HEADS, t * (TR + 1):t * (TR + 1) + TR],
                                               top_parts[0:TR, t].rearrange("p n h -> p (n h)"), keep["identb"][0:TR, 0:TR])
                last.then_inc(topT_ps, 1)

            def scores_turned(r, h):
                if h == 0:
                    pe.wait_ge(top_in[r.u], r.k * 48 + 48)
                pe.wait_ge(p_done, unit(r, h) + 1)
                for j in range(2):
                    last = nc.tensor.matmul(ps_t[0:TR, h % 2, j, 0:S], qk[:, r.u, 1, h, j, :],
                                            qk[:, r.u, 0, h].rearrange("p t s -> p (t s)"), start=True, stop=True)
                last.then_inc(scoresT_ps, 1)

            def values(r, h):
                g, at = h // 4, h % 4 * HPB
                if h % 4 == 0:
                    pe.wait_ge(oT_ready, r.b * GROUPS + (g + 1))
                pe.wait_ge(p_done, unit(r, h) + 3)
                for j in range(2):
                    last = nc.tensor.matmul(ps_o[at:at + HPB, 0:S], v[0:TR, r.u, j, h, :],
                                            pT[0:TR, h % 3, j, :], start=(j == 0), stop=(j == 1))
                last.then_inc(pv_done, 1)

            def sums(r, groups):
                pe.wait_ge(oT_ready, r.b * GROUPS + (groups[-1] + 2))
                for n, g in enumerate(groups):
                    last = nc.tensor.matmul(ps_c[:, n, 0:S], spread[:], oT[:, g, :], start=True, stop=True)
                last.then_inc(sums_ps, 1)

            def project_out(r):
                pe.wait_ge(att_ready, r.b + 2)
                for t in range(2):
                    for g in range(GROUPS):
                        last = nc.tensor.matmul(ps_c[0:TR, t, 0:D], attT[:, g, t * TR:t * TR + TR], wo[:, g, :],
                                                start=(g == 0), stop=(g == GROUPS - 1))
                last.then_inc(proj_ps, 1)

            def make_qk(r, job):
                pe.wait_ge(a_done, r.b * A_JOBS + (job + 1))
                if job == 0:
                    if not (isinstance(r.b, int) and r.b < 2):
                        pe.wait_ge(topT_ready, r.b - 1)
                    pe.wait_ge(z_ready, r.b + 1)
                    last = turn_tokens(nc, ps_a[:].rearrange("p (h s) -> p h s", h=2), z, ident)
                else:
                    t = job - 1
                    for half in range(2):
                        last = nc.tensor.matmul(ps_a[0:TR, 0:2 * D], zT[0:DH, half, t * TR:t * TR + TR],
                                                w[0:DH, half, 0:2 * D], start=(half == 0), stop=(half == 1))
                last.then_inc(a_ps, 1)

            def make_stacks(r, job):
                pe.wait_ge(k_done, r.b * K_JOBS + (job + 1))
                if job == V_JOB:
                    for t in range(2):
                        for half in range(2):
                            last = nc.tensor.matmul(ps_v[0:TR, t, 0:D], zT[0:DH, half, t * TR:t * TR + TR],
                                                    w[0:DH, half, 2 * D:3 * D], start=(half == 0), stop=(half == 1))
                else:
                    if job == 0:
                        pe.wait_ge(q_stacked, r.b + 2)
                        pe.wait_ge(stacks_ready, r.b + 2)
                    pair = job - (job > V_JOB)
                    for e in range(2):
                        for i in range(2):
                            for t in range(2):
                                at = (2 * e + i) * 256 + t * (TR + 1)
                                last = nc.tensor.transpose(
                                    ps_kb[0:STACK, at:at + TR],
                                    stacks[0:TR, r.u, i, t, 2 * pair + e].rearrange("p c d -> p (c d)"),
                                    keep["identb"][0:TR, 0:TR])
                last.then_inc(k_ps, 1)

            def step(r, q1, b1, b2):
                for h in range(HEADS):
                    for row, head in lag(q1, b1, h, 1):
                        scores(row, head)
                    for row, head in lag(b1, b2, h, 2):
                        scores_turned(row, head)
                    if r is not None and A_SLOT <= h < A_SLOT + A_JOBS:
                        make_qk(r, h - A_SLOT)
                    if q1 is not None and h in K_SLOTS:
                        make_stacks(q1, K_SLOTS.index(h))
                    for row, head in lag(b1, b2, h, 4):
                        values(row, head)
                    if b1 is not None and h == 0:
                        turn_top(b1)
                    if b2 is None:
                        continue
                    if h == 1:
                        pe.wait_ge(logits_done, b2.b + 1)
                        sums(b2, (0, 1))
                    if h == 5:
                        pe.wait_ge(inverse_ready, b2.b * 2 + 1)
                        sums(b2, (2,))
                    if h == 6:
                        project_out(b2)
                    if h == 10:
                        pe.wait_ge(zn_ready, b2.b + 1)
                        turn_tokens(nc, ps_c, zn[:, b2.u], ident).then_inc(znT_ps, 1)
                    if h == 11:
                        pe.wait_ge(znT_ready, b2.b + 1)
                        project_tokens(nc, ps_c, wg, znT, EXPERTS).then_inc(gate_ps, 1)

            rows_deep(pe, step, 4)

        @block.scalar
        def _(act):
            act.sem_inc(a_done, 1)
            act.sem_inc(top_done, 2)
            act.sem_inc(p_done, 2)
            act.sem_inc(pv_done, 3)
            act.sem_inc(oT_ready, 1)
            act.sem_inc(att_ready, 1)
            act.sem_inc(parts_ready, 1)
            act.sem_inc(stacks_ready, 1)
            act.sem_inc(q_stacked, 1)
            act.sem_inc(k_ps, 2 * K_JOBS)
            act.sem_inc(k_done, 1)
            act.sem_inc(logits_done, 1)
            for u in range(2):
                act.sem_inc(ax_stored[u], 16)
                act.sem_inc(stored[u], 48)
            act.wait_ge(loaded, 80)
            act.wait_ge(ones_ready, 4)

            def exponential(r, h):
                act.wait_ge(scoresT_ps, unit(r, h) + 1)
                act.wait_ge(pv_done, unit(r, h) + 1)
                nc.scalar.activation(pT[0:TR, h % 3], ps_t[0:TR, h % 2, :, 0:S], ACT.Exp).then_inc(p_done, 1)

            def read_group(r, g):
                if g == 0:
                    act.wait_ge(att_ready, r.b + 1)
                act.wait_ge(pv_done, unit(r, 4 * g + 3) + 4)
                nc.scalar.activation(oT[:, g, :], ps_o[:, 0:S], ACT.Copy).then_inc(oT_ready, 1)

            def read_top(r):
                act.wait_ge(topT_ps, r.b + 1)
                nc.scalar.activation(topT[:, r.u], ps_ab[0:3 * HEADS, 0:2 * TR + 2].rearrange("p (t s) -> p t s", t=2)
                                     [:, :, 0:TR], ACT.Copy).then_inc(topT_ready, 1)
                act.wait_ge(topT_ready, r.b + 1)
                act.sem_inc(passed, 1)
                for n in range(3):
                    act.dma_start(qk[STACK + n:STACK + n + 1, r.u, 0],
                                  topT[n * HEADS:n * HEADS + HEADS, r.u]).then_inc(top_in[r.u], 16)

            def affine(dst, ps, norm):
                for half in range(2):
                    last = nc.scalar.activation(dst[0:DH, half, :], ps[0:DH, half, 0:S], ACT.Identity,
                                                scale=gb[:, norm, 0, half:half + 1], bias=gb[:, norm, 1, half:half + 1])
                return last

            def read_qk(r, job):
                act.wait_ge(a_ps, r.b * A_JOBS + (job + 1))
                if job == 0:
                    last = affine(zT, ps_a[:].rearrange("p (h s) -> p h s", h=2), 0)
                else:
                    if job == 1:
                        act.wait_ge(parts_ready, r.b + 1)
                    for i, scale in enumerate((HD**-0.5, 1.0)):
                        last = nc.scalar.mul(xs[0:TR, i, job - 1], ps_a[0:TR, i * D:i * D + D], scale)
                last.then_inc(a_done, 1)

            def read_stacks(r, job):
                act.wait_ge(k_ps, r.b * K_JOBS + (2 * K_JOBS + job + 1))
                if job == V_JOB:
                    last = nc.scalar.activation(v[0:TR, r.u, :, :, 0:HD],
                                                ps_v[0:TR, :, 0:D].rearrange("p j (h d) -> p j h d", h=HEADS), ACT.Copy)
                else:
                    pair = job - (job > V_JOB)
                    for e in range(2):
                        turned = ps_kb[0:STACK, 512 * e:512 * e + 512].rearrange("p (i c) -> p i c", i=2)\
                            [:, :, 0:2 * TR + 2].rearrange("p i (t s) -> p i t s", t=2)[:, :, :, 0:TR]
                        last = nc.scalar.activation(qk[0:STACK, r.u, :, 2 * pair + e], turned, ACT.Copy)
                last.then_inc(k_done, 1)

            def step(r, q1, b1, b2):
                if r is not None:
                    act.wait_ge(rows_in[r.u], r.k * 32 + 32)
                    nc.scalar.activation(xy[0:TR, r.u], y[0:TR, r.u], ACT.Identity, scale=par(keep, "y_inv", TR),
                                         bias=keep["magic"][0:TR, :]).then_inc(xy_ready, 1)
                for h in range(HEADS):
                    for row, head in lag(b1, b2, h, 2):
                        exponential(row, head)
                    if r is not None and A_SLOT <= h < A_SLOT + A_JOBS:
                        read_qk(r, h - A_SLOT)
                    if q1 is not None and h in K_SLOTS:
                        read_stacks(q1, K_SLOTS.index(h))
                    if b1 is not None and h == 0:
                        read_top(b1)
                    for row, head in lag(b1, b2, h, 4):
                        if head % 4 == 3:
                            read_group(row, head // 4)
                    if b2 is not None and h == 10:
                        act.wait_ge(znT_ps, b2.b + 1)
                        affine(znT, ps_c, 1).then_inc(znT_ready, 1)

            rows_deep(act, step, 4)

        @block.gpsimd
        def _(pool):
            for n, tile in enumerate((znT[DH:DH + 1], qk[STACK:STACK + 3, :, 1])):
                nc.gpsimd.memset(tile, 1.0).then_inc(ones_ready, 1)
                pool.wait_ge(ones_ready, n + 1)
            nc.gpsimd.memset(v[:], 0.0).then_inc(ones_ready, 1)
            pool.wait_ge(ones_ready, 3)
            nc.gpsimd.memset(v[:, :, :, :, HD:HD + 1], 1.0).then_inc(ones_ready, 1)
            pool.wait_ge(ones_ready, 4)
            for ln in (ln1, ln2, ln3):
                nc.gpsimd.memset(ln.half[:], -0.5).then_inc(ln.half_ready, 1)
                pool.wait_ge(ln.half_ready, 1)

            def stack(r):
                pool.wait_ge(h_ready, r.b + 1)
                pool.sem_inc(passed, 1)
                pool.wait_ge(k_ps, r.b * K_JOBS + K_JOBS)
                pool.sem_inc(passed, 1)
                for place in range(len(PARTS_K)):
                    if PARTS_K[place] == 0:
                        last = nc.gpsimd.tensor_copy(stacked(r.u, 1)[:, :, place], parted(0, 1))
                last.then_inc(stacks_ready, 1)

            def step(r, q1, b1, b2):
                for row, ln in ((r, ln1), (r, ln2), (b2, ln3)):
                    if row is not None:
                        inverse_root(nc, pool, ln, row.b)
                if r is not None:
                    stack(r)

            rows_deep(pool, step, 4)

        @block.vector
        def _(dve):
            cha, chc, cht = Chain(dve, chain_a), Chain(dve, chain_c), Chain(dve, chain_t)
            a_count, c_count = 10, 4

            def row_top(r, h):
                dve.wait_ge(scores_ps, unit(r, h) + 1)
                nc.vector.tensor_reduce(top[0:TR, :, h], ps_s[0:TR, h % 2, :, 0:S], AX.X, ALU.max, negate=True)\
                    .then_inc(top_done, 1)

            def split_top(r):
                cht.start(r.b * 3)
                dve.wait_ge(top_done, unit(r, HEADS - 1) + 3)
                cht.link(nc.vector.tensor_copy(top_parts[0:TR, :, 0], top[0:TR]))
                cht.link(nc.vector.tensor_tensor(top_rest[0:TR], top[0:TR], top_parts[0:TR, :, 0], ALU.subtract))
                cht.link(nc.vector.tensor_copy(top_parts[0:TR, :, 1], top_rest[0:TR]))
                nc.vector.tensor_tensor(top_parts[0:TR, :, 2], top_rest[0:TR], top_parts[0:TR, :, 1], ALU.subtract)\
                    .then_inc(top_parts_ready, 1)

            def stack_q(r, n):
                places = [place for place in range(len(PARTS_Q)) if PARTS_Q[place] == n]
                return nc.vector.tensor_copy(stacked(r.u, 0)[:, :, places[0]:places[-1] + 1],
                                             parted(n, 0).unsqueeze(2).to_broadcast([TR, 2 * HEADS, len(places), HD]))

            def stage_a(r, h):
                h2, xl = ax[:, r.u, 0], ax[:, r.u, 1]
                if h == 0:
                    cha.start(r.b * a_count)
                    dve.wait_ge(xy_ready, r.b + 1)
                    dve.wait_ge(ax_stored[r.u], r.k * 16 + 16)
                    nc.vector.tensor_scalar(yi[0:TR], xy[0:TR, r.u], par(keep, "y_top", TR), MAGIC, ALU.min, ALU.subtract)\
                        .then_inc(yi_ready, 1)
                    dve.wait_ge(yi_ready, r.b + 1)
                    nc.vector.scalar_tensor_tensor(h2[0:TR], yi[0:TR], par(keep, "y_scale", TR), h1[0:TR, r.u],
                                                   ALU.mult, ALU.add).then_inc(h2_ready, 1)
                if h == 1:
                    dve.wait_ge(h2_ready, r.b + 1)
                    norm_stats(nc, dve, cha, h2, ln1)
                if h == 2:
                    norm_apply(nc, dve, h2, xl, ln1, r.b).then_inc(xl_ready, 1)
                if h == 3:
                    dve.wait_ge(xl_ready, r.b + 1)
                    norm_stats(nc, dve, cha, xl, ln2)
                if h == 4:
                    norm_apply(nc, dve, xl, z, ln2, r.b).then_inc(z_ready, 1)
                if h == 8:
                    dve.wait_ge(a_done, r.b * A_JOBS + (A_JOBS + 1))
                    dve.wait_ge(stacks_ready, r.b + 1)
                    dve.wait_ge(q_stacked, r.b + 1)
                    nc.vector.tensor_copy(part[0][0:TR], xs[0:TR]).then_inc(h_ready, 1)
                    dve.wait_ge(h_ready, r.b + 1)
                    cha.of(nc.vector.tensor_tensor(rest[0:TR], xs[0:TR], part[0][0:TR], ALU.subtract))
                    dve.wait_ge(k_ps, r.b * K_JOBS + K_JOBS)
                    stack_q(r, 0)
                if h == 9:
                    cha.sync()
                    cha.link(nc.vector.tensor_copy(part[1][0:TR], rest[0:TR]))
                    nc.vector.tensor_tensor(part[2][0:TR], rest[0:TR], part[1][0:TR], ALU.subtract).then_inc(parts_ready, 1)
                    stack_q(r, 1)
                if h == 10:
                    dve.wait_ge(parts_ready, r.b + 2)
                    for place in range(len(PARTS_K)):
                        if PARTS_K[place] > 0:
                            nc.vector.tensor_copy(stacked(r.u, 1)[:, :, place], parted(PARTS_K[place], 1))
                    stack_q(r, 2).then_inc(q_stacked, 1)
                    assert cha.n == a_count

            def stage_c(r, h):
                if h in (2, 5):
                    groups, n = ((0, 1), 1) if h == 2 else ((2,), 2)
                    dve.wait_ge(sums_ps, r.b * 2 + n)
                    nc.vector.reciprocal(inv_sum[:, 0:len(groups)], ps_c[:, 0:len(groups), 0:S]).then_inc(inverse_ready, 1)
                    dve.wait_ge(inverse_ready, r.b * 2 + n)
                    last = nc.vector.tensor_tensor(attT[:, groups[0]:groups[-1] + 1], oT[:, groups[0]:groups[-1] + 1],
                                                   inv_sum[:, 0:len(groups)], ALU.mult)
                    if h == 2:
                        last.then_inc(half_ready, 1)
                        dve.wait_ge(half_ready, r.b + 1)
                    else:
                        last.then_inc(att_ready, 1)
                if h == 7:
                    dve.wait_ge(proj_ps, r.b + 1)
                    dve.wait_ge(cx_in[r.u], r.k * 16 + 16)
                    nc.vector.tensor_tensor(x2[0:TR], ps_c[0:TR, :, 0:D], cx[0:TR, r.u, 1], ALU.add).then_inc(x2_ready, 1)
                    dve.wait_ge(x2_ready, r.b + 1)
                    chc.start(r.b * c_count)
                    norm_stats(nc, dve, chc, x2, ln3)
                    dve.wait_ge(stored[r.u], r.k * 48 + 48)
                    nc.vector.tensor_tensor(hx[0:TR, r.u], x2[0:TR], cx[0:TR, r.u, 0], ALU.add).then_inc(hx_ready, 1)
                if h == 8:
                    norm_apply(nc, dve, x2, zn[:, r.u], ln3, r.b).then_inc(zn_ready, 1)
                if h == 11:
                    dve.wait_ge(gate_ps, r.b + 1)
                    nc.vector.tensor_copy(logits[0:TR, r.u], ps_c[0:TR, :, 0:EXPERTS]).then_inc(logits_done, 1)
                    assert chc.n == c_count

            def step(r, q1, b1, b2):
                for h in range(HEADS):
                    for row, head in lag(q1, b1, h, 1):
                        row_top(row, head)
                    if b1 is not None and h == 0:
                        split_top(b1)
                    if r is not None:
                        stage_a(r, h)
                    if b2 is not None:
                        stage_c(b2, h)

            rows_deep(dve, step, 4)


class Ranks:

    def __init__(self, c, name):
        self.ps_low = c.ps(name + "ps_low", [128, NT, EXPERTS])
        self.ps_sum = c.ps(name + "ps_sum", [128, NT, EXPERTS])
        self.sums = c.sb(name + "sums", [128, NT, EXPERTS])
        self.scan = c.sb(name + "scan", [128, EXPERTS, NT])
        self.ones = c.sb(name + "ones", [128, NT])
        self.rank = c.sb(name + "rank", [128, NT, EXPERTS])
        self.mask_ready = c.sem(name + "mask_ready")
        self.counted = c.sem(name + "ranks_counted")

    def products(self, nc, pe, keep, mask, n):
        pe.wait_ge(self.mask_ready, n + 1)
        nc.tensor.matmul(self.ps_low[0:TR], keep["tri"][0:TR, 0:TR], mask, start=True, stop=True)
        nc.tensor.matmul(self.ps_sum[0:TR], keep["onesb"][0:TR, 0:TR], mask, start=True, stop=True)\
            .then_inc(self.counted, 1)

    def finish(self, nc, dve, ch, n):
        dve.wait_ge(self.counted, n + 1)
        ch.of(nc.vector.memset(self.ones[:], 1.0))
        ch.link(nc.vector.tensor_copy(self.sums[0:TR], self.ps_sum[0:TR]))
        for e in range(EXPERTS):
            ch.of(nc.vector.tensor_tensor_scan(self.scan[0:TR, e, :], self.ones[0:TR], self.sums[0:TR, :, e],
                                               0.0, ALU.mult, ALU.add))
        ch.sync()
        ch.link(nc.vector.tensor_tensor(self.rank[0:TR], self.scan[0:TR].rearrange("p e n -> p n e"), self.sums[0:TR],
                                        ALU.subtract))
        ch.link(nc.vector.tensor_tensor(self.rank[0:TR], self.rank[0:TR], self.ps_low[0:TR], ALU.add))


def by_expert(x):
    return x.unsqueeze(1).to_broadcast([TR, NT, EXPERTS])


def by_token(x):
    return x.unsqueeze(2).to_broadcast([TR, NT, EXPERTS])


def one_hot_first(nc, ch, keep, scores, best, work, first, onehot):
    ch.link(nc.vector.tensor_tensor(work, scores, by_token(best), ALU.is_equal))
    ch.link(nc.vector.tensor_tensor(work, work, by_expert(keep["falling"][0:TR]), ALU.mult))
    ch.link(nc.vector.tensor_reduce(first, work, AX.X, ALU.max))
    ch.link(nc.vector.tensor_tensor(onehot, work, by_token(first), ALU.is_equal))


def place_slots(nc, ch, keep, ranks_, base, tile_expert, tile_start, s):
    counts = ranks_.scan[0:TR, :, NT - 1]
    ch.link(nc.vector.tensor_scalar(s[0:TR, 0:8], counts, 1.0 / SLOTS, 0.5 - 0.5 / SLOTS, ALU.mult, ALU.add))
    ch.link(nc.vector.tensor_scalar(s[0:TR, 0:8], s[0:TR, 0:8], MAGIC, MAGIC, ALU.add, ALU.subtract))
    ch.link(nc.vector.tensor_scalar(s[0:TR, 0:8], s[0:TR, 0:8], float(SLOTS), None, ALU.mult))
    ch.link(nc.vector.memset(base[:], 0.0))
    for e in range(1, EXPERTS):
        ch.link(nc.vector.tensor_tensor(base[0:TR, e:e + 1], base[0:TR, e - 1:e], s[0:TR, e - 1:e], ALU.add))
    ch.link(nc.vector.tensor_tensor(ranks_.rank[0:TR], ranks_.rank[0:TR], by_expert(base[0:TR]), ALU.add))
    n = tile_start.shape[1]
    ch.link(nc.vector.memset(s[0:1, 16:16 + n], 0.0))
    for e in range(1, EXPERTS):
        ch.link(nc.vector.scalar_tensor_tensor(s[0:1, 16:16 + n], tile_start[0:1, :], base[0:1, e:e + 1],
                                               s[0:1, 16:16 + n], ALU.is_ge, ALU.add))
    ch.link(nc.vector.tensor_copy(tile_expert[0:1, 0:n], s[0:1, 16:16 + n]))


def route_two_pass(nc, io, keep, expert_weights):
    with ExitStack() as stack:
        c = Ctx(nc, stack, "route2_")
        logits = c.sb("logits", [128, NT, EXPERTS])
        left = c.sb("left", [128, NT, EXPERTS])
        work = c.sb("work", [128, NT, EXPERTS])
        hot = c.sb("hot", [128, 2, NT, EXPERTS])
        mask = c.sb("mask", [128, NT, EXPERTS], BF16)
        best = c.sb("best", [128, 2, NT])
        first = c.sb("first", [128, NT])
        weights = c.sb("weights", [128, NT, 2])
        gap = c.sb("gap", [128, NT])
        e2 = c.sb("e2", [128, NT])
        slot_f = c.sb("slot_f", [128, NT, 2])
        slots = c.sb("slots", [128, NT, 2], I32)
        base = c.sb("base", [128, EXPERTS])
        s = c.sb("s", [128, 16 + TILES2])
        rk = Ranks(c, "")
        loaded = c.sem("loaded")
        chain = c.sem("chain")
        gap_ready = c.sem("gap_ready")
        e2_ready = c.sem("e2_ready")
        slots_ready = c.sem("slots_ready")
        stored = c.sem("stored")
        block = stack.enter_context(nc.Block())

        @block.sync
        def _(sp):
            sp.dma_start(logits[0:TR].rearrange("p (b t) e -> p b (t e)", t=2),
                         io["logits"].rearrange("b p t e -> p b (t e)")).then_inc(loaded, 16)
            expert_weights.load(sp, io)
            sp.wait_ge(slots_ready, 1)
            sp.dma_start(io["slots"].rearrange("b p c -> p b c"),
                         slots[0:TR].rearrange("p (b t) c -> p b (t c)", t=2)).then_inc(stored, 16)
            sp.dma_start(io["weights"].rearrange("b p c -> p b c"),
                         weights[0:TR].rearrange("p (b t) c -> p b (t c)", t=2)).then_inc(stored, 16)
            sp.wait_ge(stored, 32)

        @block.tensor
        def _(pe):
            rk.products(nc, pe, keep, mask[0:TR], 0)

        @block.scalar
        def _(act):
            act.wait_ge(gap_ready, 1)
            nc.scalar.activation(e2[0:TR], gap[0:TR], ACT.Exp).then_inc(e2_ready, 1)

        @block.vector
        def _(dve):
            ch = Chain(dve, chain)
            dve.wait_ge(loaded, 16)
            for n, source in ((0, logits), (1, left)):
                top = best[0:TR, n]
                ch.link(nc.vector.tensor_reduce(top, source[0:TR], AX.X, ALU.max))
                one_hot_first(nc, ch, keep, source[0:TR], top, work[0:TR], first[0:TR], hot[0:TR, n])
                if n == 0:
                    ch.link(nc.vector.scalar_tensor_tensor(left[0:TR], hot[0:TR, 0], -BIG, logits[0:TR], ALU.mult, ALU.add))
            nc.vector.tensor_tensor(gap[0:TR], best[0:TR, 1], best[0:TR, 0], ALU.subtract).then_inc(gap_ready, 1)
            nc.vector.tensor_tensor(mask[0:TR], hot[0:TR, 0], hot[0:TR, 1], ALU.add).then_inc(rk.mask_ready, 1)
            dve.wait_ge(e2_ready, 1)
            ch.link(nc.vector.tensor_scalar(gap[0:TR], e2[0:TR], 1.0, None, ALU.add))
            ch.link(nc.vector.reciprocal(weights[0:TR, :, 0], gap[0:TR]))
            ch.link(nc.vector.tensor_tensor(weights[0:TR, :, 1], weights[0:TR, :, 0], e2[0:TR], ALU.mult))
            rk.finish(nc, dve, ch, 0)
            place_slots(nc, ch, keep, rk, base, keep["tile_expert"], keep["tile_start"][:, 0:TILES2], s)
            for n in range(2):
                ch.link(nc.vector.tensor_tensor(work[0:TR], hot[0:TR, n], rk.rank[0:TR], ALU.mult))
                ch.link(nc.vector.tensor_reduce(slot_f[0:TR, :, n], work[0:TR], AX.X, ALU.add))
            nc.vector.tensor_copy(slots[0:TR], slot_f[0:TR]).then_inc(slots_ready, 1)


class ExpertWeights:

    def __init__(self, nc, stack, layer):
        c = Ctx(nc, stack, f"weights{layer}_")
        self.layer = layer
        self.w1 = c.sb("w1", [DH + 1, EXPERTS, 2, HIDDEN])
        self.w2 = c.sb("w2", [128, EXPERTS, HC, D])
        self.b2 = c.sb("b2", [128, EXPERTS, D])
        self.gb = c.sb("gb", [DH, 2, 2])
        self.loaded = c.sem("loaded")

    def load(self, eng, io):
        eng.dma_start(self.gb[:], io[f"gb_{self.layer}"]).then_inc(self.loaded, 16)
        eng.dma_start(self.b2[:].rearrange("p e d -> p (e d)"),
                      io[f"b2_{self.layer}"].rearrange("e d -> (e d)").partition_broadcast(128)).then_inc(self.loaded, 16)
        for e in range(EXPERTS):
            eng.dma_start(self.w1[:, e], io[f"w1_{self.layer}"][e]).then_inc(self.loaded, 16)
            eng.dma_start(self.w2[:, e], io[f"w2_{self.layer}"][e]).then_inc(self.loaded, 16)

    def wait(self, eng):
        eng.wait_ge(self.loaded, 16 * (2 + 2 * EXPERTS))


def experts_pass(nc, io, keep, weights, tiles, source, choices):
    with ExitStack() as stack:
        c = Ctx(nc, stack, f"experts{choices}_")
        w1, w2, b2, gb = weights.w1, weights.w2, weights.b2, weights.gb
        rows_x = c.sb("rows_x", [128, 2, 2, D])
        slots = c.sb("slots", [128, 2, 2 * choices], I32)
        x = c.sb("x", [128, 2, D])
        xT = c.sb("xT", [DH + 1, 2, 2, SLOTS])
        g = c.sb("g", [128, 2, HIDDEN])
        gT = c.sb("gT", [128, HC, SLOTS])
        out = c.sb("out", [128, 2, D])
        ps_x = c.ps("ps_x", [128, 2, 256])
        ps_h = c.ps("ps_h", [128, 2, 512])
        ps_g = c.ps("ps_g", [128, 2, 512])
        ps_o = c.ps("ps_o", [128, 2, 512])
        rows_in = [c.sem(f"rows_in{u}") for u in range(2)]
        sent = [c.sem(f"sent{u}") for u in range(2)]
        per_row = 32 * choices
        ones_ready = c.sem("ones_ready")
        passed = c.sem("passed")
        x_in = [c.sem(f"x_in{u}") for u in range(2)]
        xT_ps = c.sem("xT_ps")
        xT_done = c.sem("xT_done")
        h_ps = c.sem("h_ps")
        g_done = c.sem("g_done")
        gT_ps = c.sem("gT_ps")
        gT_done = c.sem("gT_done")
        o_ps = c.sem("o_ps")
        out_done = c.sem("out_done")
        stored = [c.sem(f"stored{u}") for u in range(2)]
        block = stack.enter_context(nc.Block())
        half, hc = HIDDEN // 2, HC // 2

        @block.sync
        def _(sp):
            def load(r):
                if not r.first:
                    sp.wait_ge(sent[r.u], r.k * per_row)
                    sp.sem_inc(passed, 1)
                sp.dma_start(rows_x[0:TR, r.u], io[source][r.b]).then_inc(rows_in[r.u], 16)
                sp.dma_start(slots[0:TR, r.u], io["slots"][r.b][:, 0:2 * choices]).then_inc(rows_in[r.u], 16)

            load(Row(0, 0, 0, first=True))
            load(Row(1, 1, 0, first=True))
            with sp.Fori(1, B // 2) as i:
                for u in range(2):
                    load(Row(i * 2 + u, u, i))
            for u in range(2):
                sp.wait_ge(sent[u], per_row * B // 2)

            def step(a, r, b1, b2_):
                if a is not None:
                    if not (isinstance(a.b, int) and a.b < 2):
                        sp.wait_ge(xT_ps, a.b - 1)
                        sp.sem_inc(passed, 1)
                    sp.dma_start(x[:, a.u], io["slotted"][bass.ds(a.b * SLOTS, SLOTS), :]).then_inc(x_in[a.u], 16)
                if b2_ is not None:
                    sp.wait_ge(out_done, b2_.b + 3)
                    sp.sem_inc(passed, 1)
                    sp.dma_start(io["slot_out"][bass.ds(b2_.b * SLOTS, SLOTS), :], out[:, b2_.u]).then_inc(stored[b2_.u], 16)

            rows_deep(sp, step, 4, tiles)
            for u in range(2):
                sp.wait_ge(stored[u], 16 + 8 * tiles)

        @block.tensor
        def _(pe):
            weights.wait(pe)
            pe.wait_ge(ones_ready, 1)

            def turn(r):
                pe.wait_ge(x_in[r.u], r.k * 16 + 16)
                pe.wait_ge(xT_done, r.b + 1)
                for i in range(2):
                    last = nc.tensor.transpose(ps_x[0:DH, i, 0:SLOTS], x[:, r.u, i * DH:i * DH + DH], keep["ident"][:])
                last.then_inc(xT_ps, 1)

            def hidden(r, e):
                pe.wait_ge(xT_done, r.b + 2)
                for n in range(2):
                    pe.wait_ge(g_done, r.b * 2 + (n + 1))
                    cols = slice(n * half, n * half + half)
                    nc.tensor.matmul(ps_h[:, n, 0:half], xT[0:DH, r.u, 0, :],
                                     w1[0:DH, bass.ds(e, 1), 0, cols].squeeze(1), start=True, stop=False)
                    nc.tensor.matmul(ps_h[:, n, 0:half], xT[:, r.u, 1, :],
                                     w1[:, bass.ds(e, 1), 1, cols].squeeze(1), start=False, stop=True).then_inc(h_ps, 1)

            def turn_hidden(r):
                for n in range(2):
                    pe.wait_ge(g_done, r.b * 2 + (n + 3))
                    pe.wait_ge(gT_done, r.b * 2 + (n + 1))
                    for i in range(hc):
                        at = (n * hc + i) * 128
                        last = nc.tensor.transpose(ps_g[:, n, i * SLOTS:i * SLOTS + SLOTS], g[:, r.u, at:at + 128],
                                                   keep["ident"][:])
                    last.then_inc(gT_ps, 1)

            def output(r, e):
                pe.wait_ge(out_done, r.b + 1)
                for i in range(HC):
                    if i % hc == 0:
                        pe.wait_ge(gT_done, r.b * 2 + (i // hc + 3))
                    last = nc.tensor.matmul(ps_o[:, r.u, 0:D], gT[:, i, :], w2[:, bass.ds(e, 1), i, :].squeeze(1),
                                            start=(i == 0), stop=(i == HC - 1))
                last.then_inc(o_ps, 1)

            def expert(r):
                return pe.value_load(keep["tile_expert"][0:1, bass.ds(r.b, 1)], min_val=0, max_val=EXPERTS - 1)

            def step(a, r, b1):
                if a is not None:
                    turn(a)
                if b1 is not None:
                    turn_hidden(b1)
                if r is not None:
                    hidden(r, expert(r))
                if b1 is not None:
                    output(b1, expert(b1))

            rows_deep(pe, step, 3, tiles)

        @block.scalar
        def _(act):
            act.sem_inc(xT_done, 1)
            act.sem_inc(g_done, 2)
            act.sem_inc(gT_done, 2)
            act.sem_inc(out_done, 2)
            for u in range(2):
                act.sem_inc(stored[u], 16)
            weights.wait(act)

            def step(a, r, b1):
                if a is not None:
                    act.wait_ge(xT_ps, a.b + 1)
                    for i in range(2):
                        last = nc.scalar.activation(xT[0:DH, a.u, i, :], ps_x[0:DH, i, 0:SLOTS], ACT.Identity,
                                                    scale=gb[:, 0, i:i + 1], bias=gb[:, 1, i:i + 1])
                    last.then_inc(xT_done, 1)
                if r is not None:
                    for n in range(2):
                        act.wait_ge(h_ps, r.b * 2 + (n + 1))
                        nc.scalar.activation(g[:, r.u, n * half:n * half + half], ps_h[:, n, 0:half], ACT.Gelu)\
                            .then_inc(g_done, 1)

            rows_deep(act, step, 3, tiles)

        @block.gpsimd
        def _(pool):
            nc.gpsimd.memset(xT[DH:DH + 1], 1.0).then_inc(ones_ready, 1)

            def send(r):
                pool.wait_ge(rows_in[r.u], r.k * 32 + 32)
                pool.sem_inc(passed, 1)
                for t in range(2):
                    for n in range(choices):
                        at = t * choices + n
                        nc.gpsimd.indirect_dma_start(
                            io["slotted"], bass.IndirectOffsetOnAxis(ap=slots[0:TR, r.u, at:at + 1], axis=0),
                            rows_x[0:TR, r.u, t, :], None).then_inc(sent[r.u], 16)

            rows(pool, send)

        @block.vector
        def _(dve):
            weights.wait(dve)

            def step(a, r, b1):
                if b1 is not None:
                    for n in range(2):
                        dve.wait_ge(gT_ps, b1.b * 2 + (n + 1))
                        nc.vector.tensor_copy(gT[:, n * hc:n * hc + hc, :],
                                              ps_g[:, n, 0:hc * SLOTS].rearrange("p (i s) -> p i s", i=hc)).then_inc(gT_done, 1)
                    e = dve.value_load(keep["tile_expert"][0:1, bass.ds(b1.b, 1)], min_val=0, max_val=EXPERTS - 1)
                    dve.wait_ge(stored[b1.u], b1.k * 16 + 16)
                    dve.wait_ge(o_ps, b1.b + 1)
                    nc.vector.tensor_tensor(out[:, b1.u], ps_o[:, b1.u, 0:D], b2[:, bass.ds(e, 1), :].squeeze(1), ALU.add)\
                        .then_inc(out_done, 1)

            rows_deep(dve, step, 3, tiles)


def memory_pass(nc, io, keep):
    with ExitStack() as stack:
        c = Ctx(nc, stack, "mem_")
        wq = c.sb("wq", [DH, 2, MEM])
        wk = c.sb("wk", [DH, 2, MEM])
        wv = c.sb("wv", [DH, 2, MEM])
        wgate = c.sb("wgate", [DH, 2, MEM_HEADS])
        wout = c.sb("wout", [128, MEM // 128, D])
        wswitch = c.sb("wswitch", [DH + 1, 2, EXPERTS])
        decay = c.sb("decay", [128, 3 * TR])
        hx = c.sb("hx", [128, 2, 2, D])
        slots = c.sb("slots", [128, 2, 4], I32)
        weights = c.sb("weights", [128, 2, 4])
        gathered = c.sb("gathered", [128, 2, 4, D])
        h3 = c.sb("h3", [128, 2, D])
        xl = c.sb("xl", [128, 2, D])
        hs = c.sb("hs", [128, 2, 2, D])
        xT = c.sb("xT", [DH, 2, S])
        qT = c.sb("qT", [128, 2, MEM // 128, S])
        kT = c.sb("kT", [128, MEM // 128, S])
        vT = c.sb("vT", [128, MEM // 128, S])
        gate = c.sb("gate", [128, 2, MEM_HEADS])
        vo = c.sb("vo", [128, 2, MEM_HEADS, D])
        sT = c.sb("sT", [128, 4, 3 * TR])
        h4 = c.sb("h4", [128, 2, 2, D])
        x5 = c.sb("x5", [128, 2, 2, D])
        x5T = c.sb("x5T", [DH + 1, 2, S])
        logits = c.sb("logits", [128, 2, 2, EXPERTS])
        ln1, ln2 = NormTiles(c, "n1_"), NormTiles(c, "n2_")
        ps_x = c.ps("ps_x", [128, 2, 256])
        ps_q = c.ps("ps_q", [128, 2, 2, 256])
        ps_s = c.ps("ps_s", [128, 2, 512])
        ps_o = c.ps("ps_o", [128, 2, 512])
        ps_c = c.ps("ps_c", [128, 2, 256])
        loaded = c.sem("loaded")
        ones_ready = c.sem("ones_ready")
        passed = c.sem("passed")
        rows_in = [c.sem(f"rows_in{u}") for u in range(2)]
        outputs_in = [c.sem(f"outputs_in{u}") for u in range(2)]
        stored = [c.sem(f"stored{u}") for u in range(2)]
        h3_ready = c.sem("h3_ready")
        xl_ready = c.sem("xl_ready")
        xT_ps = c.sem("xT_ps")
        xT_ready = c.sem("xT_ready")
        q_ps = c.sem("q_ps")
        q_done = c.sem("q_done")
        m_ps = c.sem("m_ps")
        m_done = c.sem("m_done")
        gate_exp = c.sem("gate_exp")
        scores_ps = c.sem("scores_ps")
        s_done = c.sem("s_done")
        v_done = c.sem("v_done")
        h4_done = c.sem("h4_done")
        x5_ready = c.sem("x5_ready")
        x5T_ps = c.sem("x5T_ps")
        x5T_ready = c.sem("x5T_ready")
        logits_ps = c.sem("logits_ps")
        logits_done = c.sem("logits_done")
        chain_a = c.sem("chain_a")
        chain_c = c.sem("chain_c")
        block = stack.enter_context(nc.Block())
        PAIR = MEM // 128 // 2
        loads = ((wq, "wq_1"), (wk, "wk_1"), (wv, "wv_1"), (wgate, "wgate_1"), (wout, "wout_1"), (wswitch, "wswitch"),
                 (decay[0:TR], "decay"))

        def unit(r, h):
            return r.b * MEM_HEADS + h

        def lag(b1, b2, h, n):
            row, head = (b1, h - n) if h >= n else (b2, MEM_HEADS + h - n)
            return [(row, head)] if row is not None else []

        def is_first(r):
            return isinstance(r.b, int) and r.b == 0

        @block.sync
        def _(sp):
            for tile, name in loads:
                sp.dma_start(tile[:], io[name]).then_inc(loaded, 16)

            def step(a, r, b1, b2):
                if a is not None:
                    if not (isinstance(a.b, int) and a.b < 2):
                        sp.wait_ge(h3_ready, a.b - 1)
                        sp.sem_inc(passed, 1)
                    sp.dma_start(slots[0:TR, a.u], io["slots"][a.b]).then_inc(rows_in[a.u], 16)
                    sp.dma_start(weights[0:TR, a.u], io["weights"][a.b]).then_inc(rows_in[a.u], 16)
                    sp.dma_start(hx[0:TR, a.u], io["hx"][a.b]).then_inc(rows_in[a.u], 16)
                if b2 is not None:
                    sp.wait_ge(h4_done, b2.b + 3)
                    sp.sem_inc(passed, 1)
                    sp.dma_start(io["h4"][b2.b], h4[0:TR, b2.u]).then_inc(stored[b2.u], 16)
                    sp.wait_ge(x5_ready, b2.b + 2)
                    sp.sem_inc(passed, 1)
                    sp.dma_start(io["x5"][b2.b], x5[0:TR, b2.u]).then_inc(stored[b2.u], 16)
                    sp.wait_ge(logits_done, b2.b + 2)
                    sp.sem_inc(passed, 1)
                    sp.dma_start(io["logits"][b2.b], logits[0:TR, b2.u]).then_inc(stored[b2.u], 16)

            rows_deep(sp, step, 4)
            for u in range(2):
                sp.wait_ge(stored[u], 48 + 24 * B)

        @block.tensor
        def _(pe):
            pe.wait_ge(loaded, 16 * len(loads))
            pe.wait_ge(ones_ready, 1)
            ident = keep["ident"][0:TR, 0:TR]

            def project(ps, w, m):
                for half in range(2):
                    last = nc.tensor.matmul(ps, w[:, half, m * 128:m * 128 + 128], xT[:, half, :],
                                            start=(half == 0), stop=(half == 1))
                return last

            def remember():
                for n, w in enumerate((wk, wv)):
                    if n > 0:
                        pe.wait_ge(m_done, n)
                    for m in range(4):
                        last = project(ps_s[:, m // 2, m % 2 * 256:m % 2 * 256 + S], w, m)
                    last.then_inc(m_ps, 1)
                pe.wait_ge(m_done, 2)
                for t in range(2):
                    for half in range(2):
                        last = nc.tensor.matmul(ps_s[0:TR, 0, t * 256:t * 256 + MEM_HEADS], xT[:, half, t * TR:t * TR + TR],
                                                wgate[:, half, :], start=(half == 0), stop=(half == 1))
                last.then_inc(m_ps, 1)
                for n in range(MEM_HEADS):
                    j, m = n % 2, n // 2
                    pe.wait_ge(m_done, n + 3)
                    for i in range(2):
                        last = nc.tensor.matmul(ps_s[0:TR, i, n % 2 * 256:n % 2 * 256 + D],
                                                vT[i * 64:i * 64 + 64, m, j * TR:j * TR + TR],
                                                wout[i * 64:i * 64 + 64, m, :], start=True, stop=True)
                    last.then_inc(m_ps, 1)
                pe.wait_ge(m_done, MEM_HEADS + 3)

            def scores(r, h):
                if h in (0, MEM_HEADS // 2):
                    pe.wait_ge(q_done, r.b * 2 + (3 if h == 0 else 4))
                pe.wait_ge(s_done, unit(r, h) + 1)
                at, m = h % 2 * 64, h // 2
                nc.tensor.matmul(ps_s[0:TR, h % 2, 0:S], kT[at:at + 64, m, 0:TR], qT[at:at + 64, r.u, m, :],
                                 start=True, stop=True)
                nc.tensor.matmul(ps_s[0:TR, h % 2, S:S + TR], kT[at:at + 64, m, TR:S], qT[at:at + 64, r.u, m, TR:S],
                                 start=True, stop=True).then_inc(scores_ps, 1)

            def values(r, h):
                if h == 0:
                    pe.wait_ge(h4_done, r.b + 2)
                pe.wait_ge(s_done, unit(r, h) + 3)
                for i, (t, j) in enumerate(((0, 0), (1, 0), (1, 1))):
                    last = nc.tensor.matmul(ps_o[0:TR, t, 0:D], sT[0:TR, h % 4, i * TR:i * TR + TR],
                                            vo[0:TR, j, h, :], start=(h == 0 and j == 0),
                                            stop=(h == MEM_HEADS - 1 and j == t))
                last.then_inc(v_done, 1)

            def queries(r, n):
                pe.wait_ge(q_done, r.b * 2 + (n + 1))
                for m in range(2):
                    last = project(ps_q[:, n, m, 0:S], wq, 2 * n + m)
                last.then_inc(q_ps, 1)

            def step(r, b1, b2):
                for h in range(MEM_HEADS):
                    if b1 is not None:
                        scores(b1, h)
                    if b1 is not None and h == 2:
                        queries(b1, 1)
                    for row, head in lag(b1, b2, h, 2):
                        values(row, head)
                    if r is not None and h == 3:
                        pe.wait_ge(xl_ready, r.b + 1)
                        turn_tokens(nc, ps_x, xl, ident).then_inc(xT_ps, 1)
                    if r is not None and h == 5:
                        pe.wait_ge(xT_ready, r.b + 1)
                        if is_first(r):
                            remember()
                        queries(r, 0)
                    if b2 is not None and h == 6:
                        pe.wait_ge(logits_done, b2.b + 1)
                        pe.wait_ge(x5_ready, b2.b + 2)
                        turn_tokens(nc, ps_c, x5[:, b2.u], ident).then_inc(x5T_ps, 1)
                    if b2 is not None and h == 7:
                        pe.wait_ge(x5T_ready, b2.b + 1)
                        project_tokens(nc, ps_c, wswitch, x5T, EXPERTS).then_inc(logits_ps, 1)

            rows_deep(pe, step, 3)

        @block.scalar
        def _(act):
            act.sem_inc(xT_ps, 1)
            act.sem_inc(q_done, 2)
            act.sem_inc(s_done, 2)
            act.sem_inc(v_done, 4)
            act.sem_inc(h4_done, 2)
            act.sem_inc(x5_ready, 1)
            act.sem_inc(logits_done, 1)
            for u in range(2):
                act.sem_inc(stored[u], 48)

            def remember():
                for n, tile in enumerate((kT, vT)):
                    act.wait_ge(m_ps, n + 1)
                    for j in range(2):
                        last = nc.scalar.activation(tile[:, 2 * j:2 * j + 2, :],
                                                    ps_s[:, j, :].rearrange("p (m s) -> p m s", m=2)[:, :, 0:S], ACT.Copy)
                    last.then_inc(m_done, 1)
                act.wait_ge(m_ps, 3)
                nc.scalar.activation(gate[0:TR], ps_s[0:TR, 0, :].rearrange("p (t e) -> p t e", t=2)[:, :, 0:MEM_HEADS],
                                     ACT.Exp, scale=-1.0).then_inc(gate_exp, 1)

            def read_queries(r, n):
                act.wait_ge(q_ps, r.b * 2 + (n + 1))
                nc.scalar.activation(qT[:, r.u, 2 * n:2 * n + 2, :], ps_q[:, n, :, 0:S], ACT.Copy).then_inc(q_done, 1)

            def step(r, b1, b2):
                if b1 is not None:
                    read_queries(b1, 1)
                if r is not None:
                    act.wait_ge(xT_ps, r.b + 2)
                    nc.scalar.activation(xT[:], ps_x[0:DH, :, 0:S], ACT.Copy).then_inc(xT_ready, 1)
                    if is_first(r):
                        remember()
                    read_queries(r, 0)
                if b2 is not None:
                    act.wait_ge(x5T_ps, b2.b + 1)
                    nc.scalar.activation(x5T[0:DH], ps_c[0:DH, :, 0:S], ACT.Copy).then_inc(x5T_ready, 1)
                    act.wait_ge(stored[b2.u], b2.k * 48 + 48)
                    act.wait_ge(logits_ps, b2.b + 1)
                    nc.scalar.activation(logits[0:TR, b2.u], ps_c[0:TR, :, 0:EXPERTS], ACT.Copy).then_inc(logits_done, 1)

            rows_deep(act, step, 3)

        @block.gpsimd
        def _(pool):
            nc.gpsimd.memset(x5T[DH:DH + 1], 1.0).then_inc(ones_ready, 1)
            pool.wait_ge(ones_ready, 1)
            for ln in (ln1, ln2):
                nc.gpsimd.memset(ln.half[:], -0.5).then_inc(ln.half_ready, 1)
                pool.wait_ge(ln.half_ready, 1)

            def step(a, r, b1, b2):
                if r is not None:
                    inverse_root(nc, pool, ln1, r.b)
                if a is not None:
                    if not (isinstance(a.b, int) and a.b < 2):
                        pool.wait_ge(h3_ready, a.b - 1)
                        pool.sem_inc(passed, 1)
                    pool.wait_ge(rows_in[a.u], a.k * 48 + 48)
                    pool.sem_inc(passed, 1)
                    for i in range(4):
                        nc.gpsimd.indirect_dma_start(gathered[0:TR, a.u, i, :], None, io["slot_out"],
                                                     bass.IndirectOffsetOnAxis(ap=slots[0:TR, a.u, i:i + 1], axis=0))\
                            .then_inc(outputs_in[a.u], 16)
                if b2 is not None:
                    inverse_root(nc, pool, ln2, b2.b)

            rows_deep(pool, step, 4)

        @block.vector
        def _(dve):
            cha, chc = Chain(dve, chain_a), Chain(dve, chain_c)
            a_count, c_count = 9, 4
            dve.wait_ge(loaded, 16 * len(loads))

            def remember():
                dve.wait_ge(gate_exp, 1)
                ch = Chain(dve, gate_exp)
                ch.start(1)
                ch.link(nc.vector.tensor_scalar(gate[0:TR], gate[0:TR], 1.0, None, ALU.add))
                ch.link(nc.vector.reciprocal(gate[0:TR], gate[0:TR]))
                nc.vector.tensor_scalar(gate[0:TR], gate[0:TR], 0.1, None, ALU.mult).then_inc(m_done, 1)
                dve.wait_ge(m_done, 3)
                for n in range(MEM_HEADS):
                    j, m = n % 2, n // 2
                    dve.wait_ge(m_ps, n + 4)
                    for i in range(2):
                        last = nc.vector.tensor_scalar(vo[0:TR, j, 2 * m + i, :],
                                                       ps_s[0:TR, i, n % 2 * 256:n % 2 * 256 + D],
                                                       gate[0:TR, j, 2 * m + i:2 * m + i + 1], None, ALU.mult)
                    last.then_inc(m_done, 1)

            def weigh(r, h):
                dve.wait_ge(scores_ps, unit(r, h) + 1)
                dve.wait_ge(v_done, unit(r, h) + 1)
                nc.vector.tensor_tensor(sT[0:TR, h % 4, :], ps_s[0:TR, h % 2, 0:3 * TR], decay[0:TR, :], ALU.mult)\
                    .then_inc(s_done, 1)

            def stage_a(r, h):
                if h == 0:
                    cha.start(r.b * a_count)
                    dve.wait_ge(rows_in[r.u], r.k * 48 + 48)
                    dve.wait_ge(outputs_in[r.u], r.k * 64 + 64)
                    if not is_first(r):
                        cha.sync()
                        dve.sem_inc(passed, 1)
                    for n in range(2):
                        for t in range(2):
                            ins = nc.vector.scalar_tensor_tensor(
                                h3[0:TR, t], gathered[0:TR, r.u, 2 * t + n], weights[0:TR, r.u, 2 * t + n:2 * t + n + 1],
                                (hx[0:TR, r.u, t] if n == 0 else h3[0:TR, t]), ALU.mult, ALU.add)
                            cha.of(ins)
                        cha.sync()
                        dve.sem_inc(passed, 1)
                    dve.sem_inc(h3_ready, 1)
                if h == 1:
                    norm_stats(nc, dve, cha, h3, ln1)
                if h == 2:
                    dve.wait_ge(xT_ps, r.b + 1)
                    norm_apply(nc, dve, h3, xl, ln1, r.b).then_inc(xl_ready, 1)
                if h == 3:
                    dve.wait_ge(xl_ready, r.b + 1)
                    dve.wait_ge(h4_done, r.b + 1)
                    cha.of(nc.vector.tensor_tensor(hs[0:TR, r.u], h3[0:TR], xl[0:TR], ALU.add))
                    assert cha.n == a_count
                    if is_first(r):
                        remember()

            def stage_c(r, h):
                if h == 2:
                    chc.start(r.b * c_count)
                    dve.wait_ge(v_done, unit(r, MEM_HEADS - 1) + 5)
                    dve.wait_ge(stored[r.u], r.k * 48 + 48)
                    nc.vector.tensor_tensor(h4[0:TR, r.u], ps_o[0:TR, :, 0:D], hs[0:TR, r.u], ALU.add)\
                        .then_inc(h4_done, 1)
                if h == 3:
                    dve.wait_ge(h4_done, r.b + 3)
                    dve.wait_ge(x5_ready, r.b + 1)
                    norm_stats(nc, dve, chc, h4[:, r.u], ln2)
                if h == 5:
                    norm_apply(nc, dve, h4[:, r.u], x5[:, r.u], ln2, r.b).then_inc(x5_ready, 1)
                    assert chc.n == c_count

            def step(r, b1, b2):
                for h in range(MEM_HEADS):
                    if b2 is not None:
                        stage_c(b2, h)
                    if b1 is not None:
                        weigh(b1, h)
                    if r is not None:
                        stage_a(r, h)

            rows_deep(dve, step, 3)


def route_one_pass(nc, io, keep, expert_weights):
    with ExitStack() as stack:
        c = Ctx(nc, stack, "route1_")
        logits = c.sb("logits", [128, NT, EXPERTS])
        probs = c.sb("probs", [128, NT, EXPERTS])
        work = c.sb("work", [128, NT, EXPERTS])
        hot = c.sb("hot", [128, NT, EXPERTS])
        mask = c.sb("mask", [128, NT, EXPERTS], BF16)
        ties = c.sb("ties", [128, NT, EXPERTS], BF16)
        best = c.sb("best", [128, NT])
        first = c.sb("first", [128, NT])
        kept = c.sb("kept", [128, NT])
        factors = c.sb("factors", [128, 2, NT])
        slot_f = c.sb("slot_f", [128, NT])
        slots = c.sb("slots", [128, NT], I32)
        base = c.sb("base", [128, EXPERTS])
        threshold = c.sb("threshold", [128, EXPERTS])
        candidate = c.sb("candidate", [128, EXPERTS])
        bit = c.sb("bit", [128, 1])
        reached = c.sb("reached", [128, EXPERTS])
        reached_b = c.sb("reached_b", [128, EXPERTS], BF16)
        above = c.sb("above", [128, EXPERTS])
        s = c.sb("s", [128, 16 + TILES2])
        rk, rk_ties = Ranks(c, ""), Ranks(c, "ties_")
        ps_count = c.ps("ps_count", [128, EXPERTS])
        loaded = c.sem("loaded")
        chain = c.sem("chain")
        shifted = c.sem("shifted")
        exp_ready = c.sem("exp_ready")
        reached_ready = c.sem("reached_ready")
        counted = c.sem("counted")
        steps = c.sem("steps")
        out_ready = c.sem("out_ready")
        stored = c.sem("stored")
        block = stack.enter_context(nc.Block())

        @block.sync
        def _(sp):
            sp.dma_start(logits[0:TR].rearrange("p (b t) e -> p b (t e)", t=2),
                         io["logits"].rearrange("b p t e -> p b (t e)")).then_inc(loaded, 16)
            expert_weights.load(sp, io)
            sp.wait_ge(out_ready, 2)
            sp.dma_start(io["slots"].rearrange("b p c -> p b c")[:, :, 0:2],
                         slots[0:TR].rearrange("p (b t) -> p b t", t=2)).then_inc(stored, 16)
            for n in range(2):
                sp.dma_start(io["weights"].rearrange("b p c -> p b c")[:, :, 2 * n:2 * n + 2],
                             factors[0:TR, n].rearrange("p (b t) -> p b t", t=2)).then_inc(stored, 16)
            sp.wait_ge(stored, 48)

        @block.tensor
        def _(pe):
            rk.products(nc, pe, keep, mask[0:TR], 0)

            def count(n):
                pe.wait_ge(reached_ready, n + 1)
                nc.tensor.matmul(ps_count[0:TR], keep["onesb"][0:TR, 0:TR], reached_b[0:TR], start=True, stop=True)\
                    .then_inc(counted, 1)

            with pe.Fori(0, BITS) as j:
                count(j)
            count(BITS)
            rk_ties.products(nc, pe, keep, ties[0:TR], 0)

        @block.scalar
        def _(act):
            act.wait_ge(shifted, 1)
            nc.scalar.activation(probs[0:TR], work[0:TR], ACT.Exp).then_inc(exp_ready, 1)

        @block.vector
        def _(dve):
            ch = Chain(dve, chain)
            dve.wait_ge(loaded, 16)
            ch.link(nc.vector.tensor_reduce(best[0:TR], logits[0:TR], AX.X, ALU.max))
            nc.vector.tensor_tensor(work[0:TR], logits[0:TR], by_token(best[0:TR]), ALU.subtract).then_inc(shifted, 1)
            dve.wait_ge(exp_ready, 1)
            ch.link(nc.vector.tensor_reduce(first[0:TR], probs[0:TR], AX.X, ALU.add))
            ch.link(nc.vector.reciprocal(first[0:TR], first[0:TR]))
            ch.link(nc.vector.tensor_tensor(probs[0:TR], probs[0:TR], by_token(first[0:TR]), ALU.mult))
            ch.link(nc.vector.tensor_reduce(best[0:TR], probs[0:TR], AX.X, ALU.max))
            one_hot_first(nc, ch, keep, probs[0:TR], best[0:TR], work[0:TR], first[0:TR], hot[0:TR])
            nc.vector.tensor_copy(mask[0:TR], hot[0:TR]).then_inc(rk.mask_ready, 1)
            ch.link(nc.vector.tensor_tensor(probs[0:TR], hot[0:TR], by_token(best[0:TR]), ALU.mult))
            ch.link(nc.vector.memset(threshold[:], 0.0))
            ch.link(nc.vector.memset(bit[:], 1.0))

            def reach(bound, op, n, steps_):
                steps_.link(nc.vector.tensor_tensor(work[0:TR], probs[0:TR], by_expert(bound), op))
                steps_.link(nc.vector.tensor_reduce(reached[0:TR], work[0:TR].rearrange("p n e -> p e n"), AX.X, ALU.add))
                nc.vector.tensor_copy(reached_b[0:TR], reached[0:TR]).then_inc(reached_ready, 1)
                dve.wait_ge(counted, n + 1)

            with dve.Fori(0, BITS) as j:
                sc = Chain(dve, steps)
                sc.start(j * 6)
                sc.link(nc.vector.tensor_tensor(candidate[0:TR], threshold[0:TR], bit[0:TR].to_broadcast([TR, EXPERTS]),
                                                ALU.add))
                reach(candidate[0:TR], ALU.is_ge, j, sc)
                sc.link(nc.vector.scalar_tensor_tensor(candidate[0:TR], ps_count[0:TR], float(CAPACITY), candidate[0:TR],
                                                       ALU.is_ge, ALU.mult))
                sc.link(nc.vector.tensor_tensor(threshold[0:TR], threshold[0:TR], candidate[0:TR], ALU.max))
                sc.link(nc.vector.tensor_scalar(bit[0:TR], bit[0:TR], 0.5, None, ALU.mult))
            sc = Chain(dve, steps)
            sc.start(BITS * 6)
            reach(threshold[0:TR], ALU.is_gt, BITS, sc)
            ch.link(nc.vector.tensor_copy(above[0:TR], ps_count[0:TR]))
            ch.link(nc.vector.tensor_tensor(logits[0:TR], probs[0:TR], by_expert(threshold[0:TR]), ALU.is_equal))
            nc.vector.tensor_tensor(ties[0:TR], logits[0:TR], hot[0:TR], ALU.mult).then_inc(rk_ties.mask_ready, 1)
            rk_ties.finish(nc, dve, ch, 0)
            ch.link(nc.vector.tensor_tensor(logits[0:TR], rk_ties.rank[0:TR], by_expert(above[0:TR]), ALU.add))
            ch.link(nc.vector.scalar_tensor_tensor(logits[0:TR], logits[0:TR], float(CAPACITY), ties[0:TR],
                                                   ALU.is_lt, ALU.mult))
            ch.link(nc.vector.tensor_tensor(work[0:TR], work[0:TR], logits[0:TR], ALU.add))
            ch.link(nc.vector.tensor_reduce(kept[0:TR], work[0:TR], AX.X, ALU.add))
            ch.link(nc.vector.tensor_tensor(factors[0:TR, 0], best[0:TR], kept[0:TR], ALU.mult))
            nc.vector.tensor_tensor(factors[0:TR, 1], best[0:TR], factors[0:TR, 0], ALU.subtract).then_inc(out_ready, 1)
            rk.finish(nc, dve, ch, 0)
            place_slots(nc, ch, keep, rk, base, keep["tile_expert"], keep["tile_start"][:, 0:TILES1], s)
            ch.link(nc.vector.tensor_tensor(work[0:TR], hot[0:TR], rk.rank[0:TR], ALU.mult))
            ch.link(nc.vector.tensor_reduce(slot_f[0:TR], work[0:TR], AX.X, ALU.add))
            nc.vector.tensor_copy(slots[0:TR], slot_f[0:TR]).then_inc(out_ready, 1)


def output_pass(nc, io):
    with ExitStack() as stack:
        c = Ctx(nc, stack, "out_")
        DEEP = 4
        h4 = c.sb("h4", [128, DEEP, 2, D])
        x5 = c.sb("x5", [128, DEEP, 2, D])
        factors = c.sb("factors", [128, DEEP, 4])
        slots = c.sb("slots", [128, DEEP, 2], I32)
        gathered = c.sb("gathered", [128, DEEP, 2, D])
        part = c.sb("part", [128, DEEP, 2, D])
        out = c.sb("out", [128, DEEP, 2, D])
        slots_in = [c.sem(f"slots_in{u}") for u in range(DEEP)]
        rows_in = [c.sem(f"rows_in{u}") for u in range(DEEP)]
        outputs_in = [c.sem(f"outputs_in{u}") for u in range(DEEP)]
        stored = [c.sem(f"stored{u}") for u in range(DEEP)]
        passed = c.sem("passed")
        part_ready = c.sem("part_ready")
        out_ready = c.sem("out_ready")
        block = stack.enter_context(nc.Block())

        def rows_of(eng, body):
            with eng.Fori(0, B // DEEP) as i:
                for u in range(DEEP):
                    body(Row(i * DEEP + u, u, i))

        @block.sync
        def _(sp):
            def load(r):
                if not r.first:
                    sp.wait_ge(out_ready, r.b - (DEEP - 1))
                    sp.sem_inc(passed, 1)
                sp.dma_start(slots[0:TR, r.u], io["slots"][r.b][:, 0:2]).then_inc(slots_in[r.u], 16)
                sp.dma_start(factors[0:TR, r.u], io["weights"][r.b]).then_inc(rows_in[r.u], 16)
                sp.dma_start(h4[0:TR, r.u], io["h4"][r.b]).then_inc(rows_in[r.u], 16)
                sp.dma_start(x5[0:TR, r.u], io["x5"][r.b]).then_inc(rows_in[r.u], 16)

            def store(r):
                sp.wait_ge(out_ready, r.b + 1)
                sp.sem_inc(passed, 1)
                sp.dma_start(io["out"][r.b].rearrange("(t p) d -> p t d", t=2), out[0:TR, r.u]).then_inc(stored[r.u], 16)

            for u in range(DEEP):
                load(Row(u, u, 0, first=True))
            with sp.Fori(0, B // DEEP - 1) as i:
                for u in range(DEEP):
                    store(Row(i * DEEP + u, u, i))
                    load(Row(i * DEEP + (u + DEEP), u, i + 1))
            for u in range(DEEP):
                store(Row(B - DEEP + u, u, B // DEEP - 1))
            for u in range(DEEP):
                sp.wait_ge(stored[u], 16 + 16 * B // DEEP)

        @block.gpsimd
        def _(pool):
            def fetch(r):
                pool.wait_ge(slots_in[r.u], r.k * 16 + 16)
                pool.sem_inc(passed, 1)
                for t in range(2):
                    nc.gpsimd.indirect_dma_start(gathered[0:TR, r.u, t, :], None, io["slot_out"],
                                                 bass.IndirectOffsetOnAxis(ap=slots[0:TR, r.u, t:t + 1], axis=0))\
                        .then_inc(outputs_in[r.u], 16)

            rows_of(pool, fetch)

        @block.vector
        def _(dve):
            for u in range(DEEP):
                dve.sem_inc(stored[u], 16)

            def combine(r):
                dve.wait_ge(rows_in[r.u], r.k * 48 + 48)
                for t in range(2):
                    last = nc.vector.scalar_tensor_tensor(part[0:TR, r.u, t], x5[0:TR, r.u, t], factors[0:TR, r.u, 2 + t:3 + t],
                                                          h4[0:TR, r.u, t], ALU.mult, ALU.add)
                last.then_inc(part_ready, 1)
                dve.wait_ge(part_ready, r.b + 1)
                dve.sem_inc(passed, 1)
                dve.wait_ge(stored[r.u], r.k * 16 + 16)
                dve.wait_ge(outputs_in[r.u], r.k * 32 + 32)
                for t in range(2):
                    last = nc.vector.scalar_tensor_tensor(out[0:TR, r.u, t], gathered[0:TR, r.u, t], factors[0:TR, r.u, t:t + 1],
                                                          part[0:TR, r.u, t], ALU.mult, ALU.add)
                last.then_inc(out_ready, 1)

            rows_of(dve, combine)


def scratch(nc, name, shape, dt=F32):
    return nc.dram_tensor(name, shape, dt, kind="Internal").ap()


def audio_tower(nc, io):
    for name, shape, dt in (
        ("h1", [B, TR, 2, D], F32), ("xnT", [B, DH, 2, S], F32),
        ("qk", [B, 128, 2 * GROUPS, S], BF16), ("v", [B, TR, 2, D], BF16), ("row_max", [B, TR, 2 * HEADS], F32),
        ("o", [B, TR, 2, D], F32), ("y", [B, TR, 2, D], F32),
        ("hxl", [B, TR, 2, 2, D], F32), ("hx", [B, TR, 2, D], F32), ("zn", [B, TR, 2, D], F32),
        ("logits", [B, TR, 2, EXPERTS], F32),
        ("h4", [B, TR, 2, D], F32), ("x5", [B, TR, 2, D], F32),
        ("slots", [B, TR, 4], I32), ("weights", [B, TR, 4], F32),
        ("slotted", [TILES2 * SLOTS, D], F32), ("slot_out", [TILES2 * SLOTS, D], F32),
    ):
        if name not in io:
            io[name] = scratch(nc, name, shape, dt)
    with ExitStack() as stack:
        c = Ctx(nc, stack, "kept_")
        keep = {
            "ident": c.sb("ident", [128, 128]),
            "identb": c.sb("identb", [128, 128], BF16),
            "padmask": c.sb("padmask", [128, 1]),
            "magic": c.sb("magic", [128, 1]),
            "tri": c.sb("tri", [128, 128], BF16),
            "onesb": c.sb("onesb", [128, 128], BF16),
            "falling": c.sb("falling", [128, EXPERTS]),
            "tile_start": c.sb("tile_start", [1, TILES2]),
            "tile_expert": c.sb("tile_expert", [1, TILES2], I32),
            "par": c.sb("par", [128, 128]),
            "wqkv": c.sb("wqkv", [DH + 1, 2, QKV]),
            "wp": c.sb("wp", [DH, 2, D], BF16),
            "wp_scale": c.sb("wp_scale", [128, D]),
        }
        setup_pass(nc, io, keep)
        token_pass(nc, io, keep)
        quantise_pass(nc, io, keep)
        integer_softmax_pass(nc, io, keep)
        project_out_pass(nc, io, keep)
        softmax_attention_pass(nc, io, keep)
        with ExitStack() as layer:
            weights = ExpertWeights(nc, layer, 0)
            route_two_pass(nc, io, keep, weights)
            experts_pass(nc, io, keep, weights, TILES2, "zn", 2)
        memory_pass(nc, io, keep)
        with ExitStack() as layer:
            weights = ExpertWeights(nc, layer, 1)
            route_one_pass(nc, io, keep, weights)
            experts_pass(nc, io, keep, weights, TILES1, "x5", 1)
        output_pass(nc, io)


def halves(w, bias=None):
    out = np.zeros((DH + 1, 2, w.shape[1]), np.float32)
    out[0:DH, 0], out[0:DH, 1] = w[0:DH], w[DH:D]
    if bias is not None:
        out[DH, 1] = bias
    return out


def padded_heads(w):
    out = np.zeros((*w.shape[:-1], HEADS, HPB), np.float32)
    out[..., 0:HD] = w.reshape(*w.shape[:-1], HEADS, HD)
    return out.reshape(*w.shape[:-1], HEADS * HPB)


def grouped_heads(w, bias):
    out = np.zeros((GROUPS, 4, HPB, w.shape[1]), np.float32)
    out[:, :, 0:HD] = w.reshape(GROUPS, 4, HD, w.shape[1])
    out[0, 0, HD] = bias
    return out.reshape(GROUPS, 128, w.shape[1]).transpose(1, 0, 2)


def by_heads(w):
    return np.concatenate([padded_heads(w[..., 0:D]), padded_heads(w[..., D:2 * D]), w[..., 2 * D:]], axis=-1)


def experts_layout(x, prefix, names, layer):
    w1, b1, w2, b2 = (x[prefix + n] for n in names)
    return {
        f"w1_{layer}": np.stack([halves(w1[e], b1[e]) for e in range(EXPERTS)]),
        f"w2_{layer}": w2.reshape(EXPERTS, HC, 128, D).transpose(0, 2, 1, 3),
        f"b2_{layer}": b2,
    }


def constants():
    t = np.arange(FRAME)
    window = 0.54 - 0.46 * np.cos(2.0 * np.pi * t / (FRAME - 1))
    angle = 2.0 * np.pi * np.outer(t, np.arange(BINS)) / FRAME
    dft = np.concatenate([np.cos(angle), -np.sin(angle)], axis=1) * window[:, None]
    ago = np.arange(S)[None, :] - 1 - np.arange(TR)[:, None]
    decay = np.where(ago >= 0, float(np.float32(DECAY)) ** np.maximum(ago, 0), 0.0)
    decay = np.concatenate([decay, decay[:, 0:TR]], axis=1)
    padmask = np.where(np.arange(128) % HPB < HD, 0.0, BIG)[:, None]
    return {
        "dft": dft.astype(np.float32),
        "ident": np.eye(128, dtype=np.float32),
        "padmask": padmask.astype(np.float32),
        "tri": np.triu(np.ones((128, 128), np.float32), 1),
        "falling": np.tile(np.arange(EXPERTS, 0, -1, dtype=np.float32), (128, 1)),
        "decay": decay.astype(np.float32),
        "spread": (np.arange(128)[:, None] == np.arange(128)[None] // HPB * HPB + HD).astype(np.float32),
        "tile_start": np.arange(TILES2, dtype=np.float32)[None] * SLOTS,
    }


def layouts(x):
    x = {k: np.asarray(v) for k, v in x.items()}
    mel = x["L0_tok_mel_filters"].T
    out = {
        "x": x["x"],
        "mel": np.concatenate([mel, mel], axis=0),
        "dct": x["L0_tok_dct"].T,
        "wtok": np.concatenate([x["L0_tok_w_proj"], x["L0_tok_b_proj"][None]], axis=0),
        "wqkv": halves(by_heads(x["L0_attn_w_qkv"].T), by_heads(x["L0_attn_b_qkv"])),
        "bproj_q": x["L0_attn_b_proj"],
        "wproj_q": halves(x["L0_attn_w_proj"].T)[0:DH],
    }
    gains = np.stack([np.stack([x[f"L0_ffn_ln{n}_{p}"].reshape(2, DH).T for p in "gb"], axis=1) for n in (1, 2)], axis=1)
    out.update({
        "gains": gains,
        "wqkv_f": halves(x["L0_ffn_qkv_w"])[0:DH],
        "wproj_f": grouped_heads(x["L0_ffn_proj_w"], x["L0_ffn_proj_b"]),
        "wgate": halves(x["L0_ffn_gate_w"], x["L0_ffn_gate_b"]),
    })
    out.update(experts_layout(x, "L0_ffn_", "w1 b1 w2 b2".split(), 0))
    out.update(experts_layout(x, "L1_ffn_", "w1 b1 w2 b2".split(), 1))
    out["gb_1"] = np.stack([np.ones((DH, 2)), np.zeros((DH, 2))], axis=1).astype(np.float32)
    out.update({
        "wq_1": halves(x["L1_attn_w_query"].T)[0:DH],
        "wk_1": halves(x["L1_attn_w_key"].T)[0:DH],
        "wv_1": halves(x["L1_attn_w_value"].T)[0:DH],
        "wgate_1": halves(x["L1_attn_w_gate"].T)[0:DH],
        "wout_1": x["L1_attn_w_out"].T.reshape(MEM // 128, 128, D).transpose(1, 0, 2),
        "wswitch": halves(x["L1_ffn_switch_w"], x["L1_ffn_switch_b"]),
    })
    out["gb_0"] = np.ascontiguousarray(gains[:, 1])
    out.update(constants())
    return {k: np.ascontiguousarray(v) for k, v in out.items()}


def kernel(**inputs):
    import concourse.bacc as bacc
    from concourse.bass_utils import run_bass_kernel_spmd

    nc = bacc.Bacc("TRN2", target_bir_lowering=False, num_devices=1)
    arrays = layouts(inputs)
    io = {n: nc.dram_tensor(f"in_{n}", a.shape, mybir.dt.from_np(a.dtype), kind="ExternalInput").ap()
          for n, a in arrays.items()}
    io["out"] = nc.dram_tensor("out", (B, S, D), F32, kind="ExternalOutput").ap()
    audio_tower(nc, io)
    result = run_bass_kernel_spmd(nc, [{f"in_{n}": a for n, a in arrays.items()}], core_ids=[0])
    return result.results[0]["out"]
```
